# Optimizing a Trainium2 kernel written in Bass

```python
import numpy as np
import jax
import jax.numpy as jnp

def _softmax(x, axis=-1):
    return jax.nn.softmax(x, axis=axis)

def _gelu(x):
    return jax.nn.gelu(x, approximate=True)

def _silu(x):
    return jax.nn.silu(x)

def _sigmoid(x):
    return jax.nn.sigmoid(x)

def _layernorm(x, axis=-1, eps=1e-05):
    m = jnp.mean(x, axis=axis, keepdims=True)
    v = jnp.var(x, axis=axis, keepdims=True)
    return (x - m) / jnp.sqrt(v + eps)

def _scatter_add(tgt, idx, src, axis=0):
    return tgt.at[idx].add(src)

def _segment_sum(src, seg, n):
    return jax.ops.segment_sum(src, seg, n)
kernel_name = 'mk_seq_preln_d2_jaxref_r8_a6b657'

def setup_inputs(seed: int=0):
    np.random.seed(seed)
    _w = jnp.asarray

    def _L0_attn_setup():
        import jax, jax.numpy as jnp
        import numpy as np
        B, N, C = (2, 256, 128)
        H = 16
        D = C // H
        key = jax.random.key(seed)
        ks = jax.random.split(key, 5)
        s = 0.02
        return {'x': jax.random.normal(ks[0], (B, N, C), dtype=jnp.float32), 'qkv_w': jax.random.normal(ks[1], (C, 3 * C), dtype=jnp.float32) * s, 'qkv_b': jax.random.normal(ks[2], (3 * C,), dtype=jnp.float32) * s, 'proj_w': jax.random.normal(ks[3], (C, C), dtype=jnp.float32) * s, 'proj_b': jax.random.normal(ks[4], (C,), dtype=jnp.float32) * s}
    _L0_attn_in = _L0_attn_setup()

    def _L0_ffn_setup():
        import jax, jax.numpy as jnp
        import numpy as np
        B, S, H = (8, 512, 128)
        NAV = 128
        E = 8
        F = 2 * H
        key = jax.random.key(seed)
        ks = jax.random.split(key, 12)

        def w(k, shape, fan_in):
            return jax.random.normal(k, shape, dtype=jnp.float32) / np.sqrt(fan_in)
        return {'hidden_states': jax.random.normal(ks[0], (B, S, H), dtype=jnp.float32), 'Wp1': w(ks[1], (H, NAV), H), 'bp1': jnp.zeros((NAV,), jnp.float32), 'Wp2': w(ks[2], (NAV, E), NAV), 'bp2': jnp.zeros((E,), jnp.float32), 'W1': w(ks[3], (E, H, F), H), 'b1': jnp.zeros((E, F), jnp.float32), 'W2': w(ks[4], (E, F, H), F), 'b2': jnp.zeros((E, H), jnp.float32), 'Wo': w(ks[5], (H, H), H), 'bo': jnp.zeros((H,), jnp.float32)}
    _L0_ffn_in = _L0_ffn_setup()

    def _L1_attn_setup():
        import jax, jax.numpy as jnp
        import numpy as np
        from jax import lax
        B, S, H = (8, 512, 128)
        key = jax.random.key(seed)
        ks = jax.random.split(key, 9)
        x = jax.random.normal(ks[0], (B, S, H), dtype=jnp.float32)
        time_decay = jax.random.normal(ks[1], (H,), dtype=jnp.float32) * 0.01
        time_mix_k = jnp.ones((H,), dtype=jnp.float32) * 0.5
        time_mix_v = jnp.ones((H,), dtype=jnp.float32) * 0.5
        time_mix_r = jnp.ones((H,), dtype=jnp.float32) * 0.5
        sc = 1.0 / np.sqrt(H)
        Wk = jax.random.uniform(ks[2], (H, H), jnp.float32, -sc, sc)
        Wv = jax.random.uniform(ks[3], (H, H), jnp.float32, -sc, sc)
        Wr = jax.random.uniform(ks[4], (H, H), jnp.float32, -sc, sc)
        Wo = jax.random.uniform(ks[5], (H, H), jnp.float32, -sc, sc)
        return {'x': x, 'time_decay': time_decay, 'time_mix_k': time_mix_k, 'time_mix_v': time_mix_v, 'time_mix_r': time_mix_r, 'Wk': Wk, 'Wv': Wv, 'Wr': Wr, 'Wo': Wo}
    _L1_attn_in = _L1_attn_setup()

    def _L1_ffn_setup():
        import jax, jax.numpy as jnp
        import numpy as np
        B, S, D, E, H, K = (4, 256, 128, 8, 512, 2)
        EPS = 1e-06

        def _ln(x, scale, bias):
            m = jnp.mean(x, axis=-1, keepdims=True)
            v = jnp.mean(jnp.square(x - m), axis=-1, keepdims=True)
            return (x - m) * jax.lax.rsqrt(v + EPS) * scale + bias
        key = jax.random.key(seed)
        ks = jax.random.split(key, 4)
        s1 = 1.0 / np.sqrt(D)
        s2 = 1.0 / np.sqrt(H)
        return {'x': jax.random.normal(ks[0], (B, S, D), jnp.float32), 'router_ln_scale': jnp.ones((D,), jnp.float32), 'router_ln_bias': jnp.zeros((D,), jnp.float32), 'router_w': jax.random.normal(ks[1], (E, D), jnp.float32) * s1, 'router_b': jnp.zeros((E,), jnp.float32), 'expert_ln_scale': jnp.ones((E, D), jnp.float32), 'expert_ln_bias': jnp.zeros((E, D), jnp.float32), 'w1': jax.random.normal(ks[2], (E, H, D), jnp.float32) * s1, 'b1': jnp.zeros((E, H), jnp.float32), 'w2': jax.random.normal(ks[3], (E, D, H), jnp.float32) * s2, 'b2': jnp.zeros((E, D), jnp.float32)}
    _L1_ffn_in = _L1_ffn_setup()
    _d = {'L0_attn_x': _L0_attn_in['x'], 'L0_attn_qkv_w': _L0_attn_in['qkv_w'], 'L0_attn_qkv_b': _L0_attn_in['qkv_b'], 'L0_attn_proj_w': _L0_attn_in['proj_w'], 'L0_attn_proj_b': _L0_attn_in['proj_b'], 'L0_ffn_Wp1': _L0_ffn_in['Wp1'], 'L0_ffn_bp1': _L0_ffn_in['bp1'], 'L0_ffn_Wp2': _L0_ffn_in['Wp2'], 'L0_ffn_bp2': _L0_ffn_in['bp2'], 'L0_ffn_W1': _L0_ffn_in['W1'], 'L0_ffn_b1': _L0_ffn_in['b1'], 'L0_ffn_W2': _L0_ffn_in['W2'], 'L0_ffn_b2': _L0_ffn_in['b2'], 'L0_ffn_Wo': _L0_ffn_in['Wo'], 'L0_ffn_bo': _L0_ffn_in['bo'], 'L1_attn_time_decay': _L1_attn_in['time_decay'], 'L1_attn_time_mix_k': _L1_attn_in['time_mix_k'], 'L1_attn_time_mix_v': _L1_attn_in['time_mix_v'], 'L1_attn_time_mix_r': _L1_attn_in['time_mix_r'], 'L1_attn_Wk': _L1_attn_in['Wk'], 'L1_attn_Wv': _L1_attn_in['Wv'], 'L1_attn_Wr': _L1_attn_in['Wr'], 'L1_attn_Wo': _L1_attn_in['Wo'], 'L1_ffn_router_ln_scale': _L1_ffn_in['router_ln_scale'], 'L1_ffn_router_ln_bias': _L1_ffn_in['router_ln_bias'], 'L1_ffn_router_w': _L1_ffn_in['router_w'], 'L1_ffn_router_b': _L1_ffn_in['router_b'], 'L1_ffn_expert_ln_scale': _L1_ffn_in['expert_ln_scale'], 'L1_ffn_expert_ln_bias': _L1_ffn_in['expert_ln_bias'], 'L1_ffn_w1': _L1_ffn_in['w1'], 'L1_ffn_b1': _L1_ffn_in['b1'], 'L1_ffn_w2': _L1_ffn_in['w2'], 'L1_ffn_b2': _L1_ffn_in['b2']}
    _x0 = _d['L0_attn_x']
    _d['L0_attn_x'] = jax.random.normal(jax.random.fold_in(jax.random.key(seed), 1), (32, 256, 128), dtype=_x0.dtype)
    del _x0
    return _d

def reference(L0_attn_x, L0_attn_qkv_w, L0_attn_qkv_b, L0_attn_proj_w, L0_attn_proj_b, L0_ffn_Wp1, L0_ffn_bp1, L0_ffn_Wp2, L0_ffn_bp2, L0_ffn_W1, L0_ffn_b1, L0_ffn_W2, L0_ffn_b2, L0_ffn_Wo, L0_ffn_bo, L1_attn_time_decay, L1_attn_time_mix_k, L1_attn_time_mix_v, L1_attn_time_mix_r, L1_attn_Wk, L1_attn_Wv, L1_attn_Wr, L1_attn_Wo, L1_ffn_router_ln_scale, L1_ffn_router_ln_bias, L1_ffn_router_w, L1_ffn_router_b, L1_ffn_expert_ln_scale, L1_ffn_expert_ln_bias, L1_ffn_w1, L1_ffn_b1, L1_ffn_w2, L1_ffn_b2):

    def _L0_attn_ref(x, qkv_w, qkv_b, proj_w, proj_b):
        import jax, jax.numpy as jnp
        import numpy as np
        B, N, C = (2, 256, 128)
        H = 16
        D = C // H
        b, n, c = x.shape
        scale = (c // H) ** (-0.5)
        qkv = x @ qkv_w + qkv_b
        qkv = qkv.reshape(b, n, 3, H, D)
        q, k, v = jnp.moveaxis(qkv, 2, 0)
        attn = jnp.einsum('bnhd,bmhd->bhnm', q, k) * scale
        attn = jax.nn.softmax(attn, axis=-1)
        out = jnp.einsum('bhnm,bmhd->bnhd', attn, v).reshape(b, n, c)
        out = out @ proj_w + proj_b
        return out

    def _L0_ffn_ref(hidden_states, Wp1, bp1, Wp2, bp2, W1, b1, W2, b2, Wo, bo):
        import jax, jax.numpy as jnp
        import numpy as np
        B, S, H = (8, 512, 128)
        NAV = 128
        E = 8
        F = 2 * H
        last = hidden_states[:, -1, :]
        logits = jax.nn.gelu(last @ Wp1 + bp1, approximate=False) @ Wp2 + bp2
        action_probs = jax.nn.softmax(logits, axis=-1)
        sel = jnp.argmax(action_probs, axis=-1)
        w1 = W1[sel]
        w2 = W2[sel]
        h = jax.nn.gelu(jnp.einsum('bsh,bhf->bsf', hidden_states, w1) + b1[sel][:, None, :], approximate=False)
        reasoned = jnp.einsum('bsf,bfh->bsh', h, w2) + b2[sel][:, None, :]
        out = reasoned @ Wo + bo
        return hidden_states + 0.3 * out

    def _L1_attn_ref(x, time_decay, time_mix_k, time_mix_v, time_mix_r, Wk, Wv, Wr, Wo):
        import jax, jax.numpy as jnp
        import numpy as np
        from jax import lax
        B, S, H = (8, 512, 128)
        d = jnp.exp(-jnp.exp(time_decay))
        b, s, h = x.shape

        def step(state, xt):
            new_state = xt + state * d
            return (new_state, state)
        init = jnp.zeros((b, h), dtype=x.dtype)
        _, prev = lax.scan(step, init, jnp.swapaxes(x, 0, 1))
        prev = jnp.swapaxes(prev, 0, 1)
        k_in = x * time_mix_k + prev * (1.0 - time_mix_k)
        v_in = x * time_mix_v + prev * (1.0 - time_mix_v)
        r_in = x * time_mix_r + prev * (1.0 - time_mix_r)
        _k = jnp.einsum('bsh,oh->bso', k_in, Wk)
        v = jnp.einsum('bsh,oh->bso', v_in, Wv)
        r = jax.nn.sigmoid(jnp.einsum('bsh,oh->bso', r_in, Wr))
        out = r * jnp.einsum('bsh,oh->bso', v, Wo)
        return out

    def _L1_ffn_ref(x, router_ln_scale, router_ln_bias, router_w, router_b, expert_ln_scale, expert_ln_bias, w1, b1, w2, b2):
        import jax, jax.numpy as jnp
        import numpy as np
        B, S, D, E, H, K = (4, 256, 128, 8, 512, 2)
        EPS = 1e-06

        def _ln(x, scale, bias):
            m = jnp.mean(x, axis=-1, keepdims=True)
            v = jnp.mean(jnp.square(x - m), axis=-1, keepdims=True)
            return (x - m) * jax.lax.rsqrt(v + EPS) * scale + bias
        orig_shape = x.shape
        xf = x.reshape(-1, D)
        T = xf.shape[0]
        logits = _ln(xf, router_ln_scale, router_ln_bias) @ router_w.T + router_b
        probs = jax.nn.softmax(logits, axis=-1)
        topw, topi = jax.lax.top_k(probs, K)
        topw = topw / jnp.sum(topw, axis=-1, keepdims=True)
        gates = jnp.zeros((T, E), xf.dtype).at[jnp.arange(T)[:, None], topi].set(topw)

        def expert(ls, lb, W1, B1, W2, B2):
            h = jax.nn.gelu(_ln(xf, ls, lb) @ W1.T + B1, approximate=False)
            return h @ W2.T + B2
        ys = jax.vmap(expert)(expert_ln_scale, expert_ln_bias, w1, b1, w2, b2)
        out = jnp.einsum('te,etd->td', gates, ys)
        return out.reshape(orig_shape)
    x = L0_attn_x
    x = x + _L0_attn_ref(_layernorm(x, axis=-1), L0_attn_qkv_w, L0_attn_qkv_b, L0_attn_proj_w, L0_attn_proj_b)
    x = x + _L0_ffn_ref(_layernorm(x, axis=-1), L0_ffn_Wp1, L0_ffn_bp1, L0_ffn_Wp2, L0_ffn_bp2, L0_ffn_W1, L0_ffn_b1, L0_ffn_W2, L0_ffn_b2, L0_ffn_Wo, L0_ffn_bo)
    x = x + _L1_attn_ref(_layernorm(x, axis=-1), L1_attn_time_decay, L1_attn_time_mix_k, L1_attn_time_mix_v, L1_attn_time_mix_r, L1_attn_Wk, L1_attn_Wv, L1_attn_Wr, L1_attn_Wo)
    x = x + _L1_ffn_ref(_layernorm(x, axis=-1), L1_ffn_router_ln_scale, L1_ffn_router_ln_bias, L1_ffn_router_w, L1_ffn_router_b, L1_ffn_expert_ln_scale, L1_ffn_expert_ln_bias, L1_ffn_w1, L1_ffn_b1, L1_ffn_w2, L1_ffn_b2)
    return x

_drawn_inputs = setup_inputs


def setup_inputs(seed=0):
    import zlib

    import numpy as np

    out = dict(_drawn_inputs(seed))
    spreads = {'L0_ffn_bp1': (0.0, 0.1),
     'L0_ffn_bp2': (0.0, 0.1),
     'L0_ffn_b1': (0.0, 0.394),
     'L0_ffn_b2': (0.0, 0.273),
     'L0_ffn_bo': (0.0, 0.1),
     'L1_attn_time_mix_k': (0.5, 0.2),
     'L1_attn_time_mix_v': (0.5, 0.6),
     'L1_attn_time_mix_r': (0.5, 0.6),
     'L1_ffn_router_ln_scale': (1.0, 0.2),
     'L1_ffn_router_ln_bias': (0.0, 0.1),
     'L1_ffn_router_b': (0.0, 0.1),
     'L1_ffn_expert_ln_scale': (1.0, 0.2),
     'L1_ffn_expert_ln_bias': (0.0, 0.322),
     'L1_ffn_b1': (0.0, 0.315),
     'L1_ffn_b2': (0.0, 0.1)}
    factors = {'L0_attn_qkv_w': 5.887,
     'L0_attn_qkv_b': 4.083,
     'L0_attn_proj_w': 3.697,
     'L1_attn_time_decay': 64.0}
    for name, (base, spread) in spreads.items():
        noise = np.random.default_rng([zlib.crc32(name.encode()), seed]).standard_normal(out[name].shape)
        drawn = base * np.exp(spread * noise) if base else spread * noise
        out[name] = jnp.asarray(drawn.astype(out[name].dtype))
    for name, factor in factors.items():
        out[name] = (out[name] * factor).astype(out[name].dtype)
    return out
```

```python
from contextlib import ExitStack

import concourse.bass as bass
from concourse import mybir
from concourse.alu_op_type import AluOpType as ALU

ACT = mybir.ActivationFunctionType
AX = mybir.AxisListType
F32 = mybir.dt.float32
BF16 = mybir.dt.bfloat16
I32 = mybir.dt.int32
U32 = mybir.dt.uint32

P = 128
N_BATCH, SEQ, C = 32, 256, 128
TOKENS = N_BATCH * SEQ
TPG = 4
GT = TPG * P
BPG = GT // SEQ
TPB = SEQ // P
GROUPS = TOKENS // GT
TILES = TOKENS // P

HEADS = 16
HD = C // HEADS
PAIRS = HEADS // 2
HALF = 64
UNITS = BPG * HEADS
MAXU = TPG * PAIRS
LEAD = MAXU - 12
QUAD = 4
QUADS = UNITS // QUAD
FILLS = QUADS // 2
PARTS = 3
RUNS = tuple(PARTS - n for n in range(PARTS))
K_ROWS = HD * sum(RUNS)
C_ROWS = 2
BUFS = 3
VW = P // QUAD
PRB = 8
SCB = 3

LN_EPS = 1e-5
LN2_EPS = 1e-6
NEWTON = 3
RSQRT_SEED = 1597463007.0


class Chip:

    def __init__(self, nc):
        self.nc = nc
        self.phase = ""

    def sb(self, ctx, name, shape, dt):
        return ctx.enter_context(self.nc.sbuf_tensor(self.phase + name, shape, dt))

    def ps(self, ctx, name, shape, dt=F32):
        return ctx.enter_context(self.nc.psum_tensor(self.phase + name, shape, dt))

    def sem(self, ctx, name):
        return ctx.enter_context(self.nc.semaphore(name))

    def dram(self, name, shape, dt):
        return self.nc.dram_tensor(name, shape, dt, kind="Internal").ap()


def rows(v):
    return bass.AP(tensor=v.tensor, offset=v.offset, ap=[[0, P]] + [list(x) for x in v.ap])


def column(v):
    return v.rearrange("(p a) -> p a", a=1)


def wait(eng, sem, count):
    if isinstance(count, int):
        eng.wait_ge(sem, count)
        return
    held = eng.to_reg(count)
    eng.wait_ge(sem, held)
    eng.free_register(held)


def wait_apart(eng, always, sem, count):
    if isinstance(count, int):
        eng.wait_ge(sem, count)
        return
    held = eng.to_reg(count)
    eng.wait_ge(always, 1)
    eng.wait_ge(sem, held)
    eng.free_register(held)


def newton_rsqrt(eng, always, sem, done, y, var, tmp):
    for n in range(NEWTON):
        eng.tensor_tensor(tmp[:, 2 * n], y[:, n], y[:, n], ALU.mult).then_inc(sem, 1)
        done += 1
        wait_apart(eng, always, sem, done)
        eng.tensor_tensor(tmp[:, 2 * n + 1], tmp[:, 2 * n], var, ALU.mult).then_inc(sem, 1)
        done += 1
        wait_apart(eng, always, sem, done)
        eng.tensor_scalar(tmp[:, 2 * n], tmp[:, 2 * n + 1], -0.5, 1.5, ALU.mult, ALU.add).then_inc(sem, 1)
        done += 1
        wait_apart(eng, always, sem, done)
        eng.tensor_tensor(y[:, n + 1], y[:, n], tmp[:, 2 * n], ALU.mult).then_inc(sem, 1)
        done += 1
        wait_apart(eng, always, sem, done)
    return done


NEWTON_OPS = 4 * NEWTON


def attention(nc, chip, X, ident, x_in, qkv_w, qkv_b, proj_w, proj_b):
    qscale = float(HD) ** -0.5
    with ExitStack() as ctx:
        def sb(name, shape, dt=F32):
            return chip.sb(ctx, name, shape, dt)

        Wqkv, Wproj = sb("Wqkv", [P, 3 * C]), sb("Wproj", [P, C])
        Wqk = sb("Wqk", [P, 2, C])
        qb, qbs, kb = sb("qb", [P, 1]), sb("qbs", [P, 1]), sb("kb", [P, 1])
        vb, pb = sb("vb", [P, C]), sb("pb", [P, C])
        QP, KP = sb("QP", [P, BUFS, 2, PAIRS, GT], BF16), sb("KP", [P, BUFS, PAIRS, GT], BF16)
        V = sb("V", [P, BUFS, TPG, HEADS, VW])
        Xs, XN = sb("Xs", [P, TPG, C]), sb("XN", [P, TPG, C])
        stat, mv = sb("stat", [P, TPG, 6]), sb("mv", [P, TPG, 2])
        var = sb("var", [P, TPG])
        ny, ntmp = sb("ny", [P, NEWTON + 1, TPG]), sb("ntmp", [P, 2 * NEWTON, TPG])
        XNT, OT = sb("XNT", [P, GT]), sb("OT", [P, GT])
        qf, kf, qr, kr = (sb(n, [P, GT]) for n in ("qf", "kf", "qr", "kr"))
        QS, KS = (sb(n, [P, PARTS, GT], BF16) for n in ("QS", "KS"))
        MX = sb("MX", [P, BUFS, TPG, HEADS])
        CM = sb("CM", [P, TPG, C_ROWS, HEADS])
        CB = sb("CB", [P, TPG, HEADS], BF16)
        CT = sb("CT", [C_ROWS * HEADS, GT], BF16)
        PR = sb("PR", [P, PRB, GT])
        PVS, REC = sb("PVS", [P, 2, GT]), sb("REC", [P, TPB, 2, QUAD])
        O = sb("O", [P, TPG, HEADS, HD])

        QD, KD = (chip.dram(n, [GROUPS, PARTS, 2, HD, PAIRS, GT], BF16) for n in ("q_parts", "k_parts"))
        CD = chip.dram("shift_rows", [GROUPS, C_ROWS, HEADS, GT], BF16)

        SC = [chip.ps(ctx, f"score{i}", [P, GT]) for i in range(SCB)]
        PM = [chip.ps(ctx, f"smax{i}", [P, GT]) for i in range(2)]
        PV = [chip.ps(ctx, f"pv{i}", [P, GT]) for i in range(2)]
        MB = chip.ps(ctx, "mb", [P, GT])

        def sem(name):
            return chip.sem(ctx, "a_" + name)

        weights_in, ones_set, kones_set, zeros_set, qbs_set, wqk_set = (
            sem(n) for n in ("weights_in", "ones", "kones", "zeros", "qbs", "wqk"))
        x_chunk = [sem(f"x_chunk{i}") for i in range(3)]
        xs_copied, stats, aggr, newton, xn_done, x_biased = (
            sem(n) for n in ("xs", "stats", "aggr", "newton", "xn", "xbias"))
        xnt_full, xnt_out, q_full, q_out, k_full, k_out, v_full, v_out = (
            sem(n) for n in ("xnt_full", "xnt_out", "q_full", "q_out", "k_full", "k_out", "v_full", "v_out"))
        splits, parts_ready, parts_stored, packed = (sem(n) for n in ("splits", "parts", "stored", "packed"))
        max_full, max_out, shift, ct_full, ct_out, ct_stored, shifted = (
            sem(n) for n in ("max_full", "max_out", "shift", "ct_full", "ct_out", "ct_stored", "shifted"))
        score_full, exp_out, pv_full, pv_out, pvt_full, recs, o_out = (
            sem(n) for n in ("score_full", "exp_out", "pv_full", "pv_out", "pvt_full", "recs", "o_out"))
        ot_full, ot_out, proj_full, x_added = (sem(n) for n in ("ot_full", "ot_out", "proj_full", "x_added"))

        N_PACK = 2 * 2 * PARTS
        X_CHUNKS = ((0, 1), (1, 3), (3, GROUPS))

        def tile_cols(t):
            return slice(t * P, (t + 1) * P)

        def run(steps, eng):
            steps(0, 0)
            n = (GROUPS - 3 - 1) // BUFS
            with eng.Fori(0, n) as i:
                for r in range(BUFS):
                    steps(i * BUFS + (1 + r), 1 + r)
            for g in range(1 + n * BUFS, GROUPS):
                steps(g, g)

        def last(r, ahead):
            return r + ahead >= GROUPS

        block = ctx.enter_context(nc.Block())

        @block.sync
        def _(sp):
            for dst, src in ((Wqkv[:, :], qkv_w), (Wproj[:, :], proj_w), (vb[:, :], rows(qkv_b[2 * C:3 * C])),
                             (pb[:, :], rows(proj_b))):
                sp.dma_start(dst, src).then_inc(weights_in, 16)
            for n, dst in enumerate((qb, kb)):
                for half in range(2):
                    src = qkv_b[n * C:(n + 1) * C].rearrange("(j i d a) -> i d j a", i=2, d=HD, a=1)[half]
                    sp.dma_start(dst[half * HALF:(half + 1) * HALF, :], src, allow_slow_non_contiguous=True).then_inc(weights_in, 16)
            xv = x_in.rearrange("b (t p) c -> p (b t) c", p=P)
            for n, (a, b) in enumerate(X_CHUNKS):
                sp.dma_start(X[:, a * TPG:b * TPG, :], xv[:, a * TPG:b * TPG, :]).then_inc(x_chunk[n], 16)

            def store(g):
                sp.wait_ge(parts_ready, (g + 1) * 2)
                for part, d in ((QS, QD), (KS, KD)):
                    sp.dma_start(d[bass.ds(g, 1)].rearrange("g s i d j t -> (i d j) (g s) t"), part[:, :, :])\
                        .then_inc(parts_stored, 16)

            def pack(g, buf):
                sp.wait_ge(parts_stored, (g + 1) * 32)
                for half in range(2):
                    at = HALF * half
                    for n, run_ in enumerate(RUNS):
                        q_parts = QD[bass.ds(g, 1), 0:run_, half].rearrange("g s d j t -> (g s) d (j t)")
                        k_part = KD[bass.ds(g, 1), n, half].rearrange("g d j t -> g d (j t)")\
                            .to_broadcast([run_, HD, PAIRS * GT])
                        sp.dma_start(QP[at:at + HD * run_, buf, half].rearrange("p j t -> p (j t)"), q_parts)\
                            .then_inc(packed, 16)
                        sp.dma_start(KP[at:at + HD * run_, buf].rearrange("p j t -> p (j t)"), k_part)\
                            .then_inc(packed, 16)
                        at += HD * run_

            def shift_out(g):
                sp.wait_ge(ct_out, g + 1)
                sp.dma_start(CD[bass.ds(g, 1)].rearrange("g r h t -> (g r h) t"), CT[:, :]).then_inc(ct_stored, 16)

            def shift_in(g, buf):
                sp.wait_ge(ct_stored, (g + 1) * 16)
                for half in range(2):
                    src = CD[bass.ds(g, 1)].rearrange("g r (j i) t -> i (g r) j t", i=2)[half]
                    at = HALF * half + K_ROWS
                    sp.dma_start(QP[at:at + C_ROWS, buf, half], src).then_inc(shifted, 16)

            sp.wait_ge(kones_set, BUFS)
            sp.wait_ge(zeros_set, BUFS)
            for g in range(2):
                store(g)
                pack(g, g)
                sp.wait_ge(packed, (g + 1) * 16 * N_PACK)
            shift_out(0)
            store(2)
            shift_in(0, 0)

            def step(g, r):
                if not last(r, 2):
                    wait_apart(sp, kones_set, score_full, g * UNITS)
                    pack(g + 2, (r + 2) % BUFS)
                    sp.wait_ge(packed, (g + 3) * (16 * N_PACK))
                if not last(r, 1):
                    shift_out(g + 1)
                    shift_in(g + 1, (r + 1) % BUFS)
                if not last(r, 3):
                    store(g + 3)
                if not last(r, 1):
                    wait_apart(sp, kones_set, shifted, (g + 2) * 32)

            run(step, sp)

        @block.gpsimd
        def _(pool):
            nc.gpsimd.memset(V[:, :, :, :, HD:VW], 1.0).then_inc(ones_set, 1)
            for buf in range(BUFS):
                nc.gpsimd.memset(KP[:, buf], 1.0).then_inc(kones_set, 1)

            def norm(g, chunk=None):
                if chunk is not None:
                    wait_apart(pool, ones_set, x_chunk[chunk], 16)
                wait_apart(pool, ones_set, xnt_full, g)
                nc.gpsimd.tensor_copy(Xs[:, :, :], X[:, bass.ds(g * TPG, TPG), :]).then_inc(xs_copied, 1)
                wait_apart(pool, ones_set, xs_copied, g + 1)
                nc.gpsimd.tensor_tensor(X[:, bass.ds(g * TPG, TPG), :], Xs[:, :, :],
                                        pb[:, :].unsqueeze(1).to_broadcast([P, TPG, C]), ALU.add).then_inc(x_biased, 1)
                wait_apart(pool, ones_set, aggr, (g + 1) * TPG)
                base = g * (NEWTON_OPS + 2)
                nc.gpsimd.tensor_scalar(var[:, :], mv[:, :, 1], LN_EPS, None, ALU.add).then_inc(newton, 1)
                wait_apart(pool, ones_set, newton, base + 1)
                nc.gpsimd.tensor_scalar(ny[:, 0, :].bitcast(I32), var[:, :].bitcast(I32), -0.5, RSQRT_SEED,
                                        ALU.mult, ALU.add).then_inc(newton, 1)
                wait_apart(pool, ones_set, newton, base + 2)
                newton_rsqrt(nc.gpsimd, ones_set, newton, base + 2, ny, var[:, :], ntmp)
                for t in range(TPG):
                    nc.gpsimd.tensor_scalar(XN[:, t, :], Xs[:, t, :], mv[:, t, 0:1], ny[:, NEWTON, t:t + 1],
                                            ALU.subtract, ALU.mult).then_inc(xn_done, 1)

            def split(g):
                for n, (full, f, rem, part) in enumerate(((q_out, qf, qr, QS), (k_out, kf, kr, KS))):
                    base = g * 4 + 2 * n
                    wait_apart(pool, ones_set, full, (g + 1) * 2)
                    nc.gpsimd.tensor_tensor(rem[:, :], f[:, :], part[:, 0, :], ALU.subtract).then_inc(splits, 1)
                    wait_apart(pool, ones_set, splits, base + 1)
                    nc.gpsimd.tensor_copy(part[:, 1, :], rem[:, :]).then_inc(splits, 1)
                    wait_apart(pool, ones_set, splits, base + 2)
                    nc.gpsimd.tensor_tensor(part[:, 2, :], rem[:, :], part[:, 1, :], ALU.subtract)\
                        .then_inc(parts_ready, 1)

            def split_max(g, buf):
                wait_apart(pool, ones_set, max_out, (g + 1) * MAXU)
                wait_apart(pool, ones_set, ct_full, g)
                nc.gpsimd.tensor_scalar(CB[:, :, :], MX[:, buf, :, :], -1.0, None, ALU.mult).then_inc(shift, 1)
                wait_apart(pool, ones_set, shift, g * 4 + 1)
                nc.gpsimd.tensor_scalar(CM[:, :, 0, :], CB[:, :, :], 1.0, None, ALU.mult).then_inc(shift, 1)
                wait_apart(pool, ones_set, shift, g * 4 + 2)
                nc.gpsimd.tensor_tensor(CM[:, :, 1, :], MX[:, buf, :, :], CM[:, :, 0, :], ALU.add).then_inc(shift, 1)
                wait_apart(pool, ones_set, shift, g * 4 + 3)
                nc.gpsimd.tensor_scalar(CM[:, :, 1, :], CM[:, :, 1, :], -1.0, None, ALU.mult).then_inc(shift, 1)

            pool.wait_ge(ones_set, 1)
            pool.wait_ge(weights_in, 128)
            for g in range(3):
                norm(g, 0 if g == 0 else 1)
                split(g)
                if g == 1:
                    split_max(0, 0)

            def step(g, r):
                if not last(r, 3):
                    norm(g + 3, 2 if r == 0 else None)
                if not last(r, 1):
                    split_max(g + 1, (r + 1) % BUFS)
                if not last(r, 3):
                    split(g + 3)

            run(step, pool)

        @block.scalar
        def _(act):
            act.wait_ge(weights_in, 128)
            nc.scalar.mul(qbs[:, :], qb[:, :], qscale).then_inc(qbs_set, 1)
            act.wait_ge(qbs_set, 1)
            for n in range(2):
                nc.scalar.copy(Wqk[:, n, :].rearrange("p (i d j) -> p i d j", i=2, d=HD),
                               Wqkv[:, n * C:(n + 1) * C].rearrange("p (j i d) -> p i d j", i=2, d=HD))\
                    .then_inc(wqk_set, 1)

            def xnt(g):
                act.wait_ge(xnt_full, g + 1)
                act.wait_ge(v_full, g)
                nc.scalar.copy(XNT[:, :], MB[:, :]).then_inc(xnt_out, 1)

            def q_k(g, full, f, part, out, bias, scale):
                act.wait_ge(full, g + 1)
                act.wait_ge(parts_ready, g * 2)
                nc.scalar.activation(f[:, :], MB[:, :], ACT.Identity, bias=bias[:, 0:1], scale=scale).then_inc(out, 1)
                act.wait_ge(parts_stored, g * 32)
                nc.scalar.activation(part[:, 0, :], MB[:, :], ACT.Identity, bias=bias[:, 0:1], scale=scale)\
                    .then_inc(out, 1)

            def q(g):
                q_k(g, q_full, qf, QS, q_out, qbs, qscale)

            def k(g):
                q_k(g, k_full, kf, KS, k_out, kb, 1.0)

            def ct(g):
                act.wait_ge(ct_full, g + 1)
                act.wait_ge(ct_stored, g * 16)
                nc.scalar.copy(CT[:, :], MB[0:C_ROWS * HEADS, :]).then_inc(ct_out, 1)

            def ot(g):
                act.wait_ge(ot_full, g + 1)
                act.wait_ge(proj_full, g)
                nc.scalar.copy(OT[:, :], MB[:, :]).then_inc(ot_out, 1)

            def exps(g, u, r):
                act.wait_ge(score_full, g * UNITS + (u + 1))
                if u % QUAD == 0 and not (isinstance(g, int) and g * UNITS + u < PRB):
                    act.wait_ge(pv_full, g * QUADS + ((u - PRB) // QUAD + 1))
                nc.scalar.activation(PR[:, u % PRB, :], SC[(r * UNITS + u) % SCB][:, :], ACT.Exp).then_inc(exp_out, 1)

            def sums(g, f):
                act.wait_ge(pv_full, g * QUADS + 2 * (f + 1))
                if not (isinstance(g, int) and g * FILLS + f < 2):
                    act.wait_ge(pvt_full, g * FILLS + (f - 1))
                nc.scalar.copy(PVS[:, f % 2, :], PV[f % 2][:, :]).then_inc(pv_out, 1)

            for g in range(3):
                xnt(g)
                q(g)
                k(g)
                if g == 1:
                    ct(0)

            def step(g, r):
                for u in range(UNITS):
                    exps(g, u, r)
                    if u == 3 and r > 0:
                        sums(g - 1, FILLS - 1)
                    if u in (11, 19, 27):
                        sums(g, (u - 11) // 8)
                    if u == 9 and r > 0:
                        ot(g - 1)
                    if not last(r, 3):
                        if u == 16:
                            xnt(g + 3)
                        if u == 18:
                            q(g + 3)
                        if u == 21:
                            k(g + 3)
                    if u == 23 and not last(r, 1):
                        ct(g + 1)

            run(step, act)
            sums(GROUPS - 1, FILLS - 1)
            ot(GROUPS - 1)

        @block.vector
        def _(dve):
            for buf in range(BUFS):
                nc.vector.memset(QP[:, buf].rearrange("p i j t -> p (i j t)").bitcast(F32), 0.0).then_inc(zeros_set, 1)

            def norm_stats(g, t):
                if t == 0:
                    dve.wait_ge(xs_copied, g + 1)
                    dve.wait_ge(xn_done, g * TPG)
                nc.vector.bn_stats(stat[:, t, :], Xs[:, t, :]).then_inc(stats, 1)
                wait_apart(dve, ones_set, stats, g * TPG + (t + 1))
                nc.vector.bn_aggr(mv[:, t, :], stat[:, t, :]).then_inc(aggr, 1)

            def values(g, buf):
                if not (isinstance(g, int) and g < BUFS):
                    dve.wait_ge(pv_full, (g - BUFS + 1) * QUADS)
                dve.wait_ge(v_full, g + 1)
                nc.vector.tensor_tensor(
                    V[:, buf, :, :, 0:HD], MB[:, :].rearrange("p (t h d) -> p t h d", t=TPG, h=HEADS),
                    vb[:, :].rearrange("p (h d) -> p h d", h=HEADS).unsqueeze(1).to_broadcast([P, TPG, HEADS, HD]),
                    ALU.add).then_inc(v_out, 1)

            def row_max(g, w, buf):
                t, j = divmod(w, PAIRS)
                dve.wait_ge(max_full, g * MAXU + (w + 1))
                if w == 0 and not (isinstance(g, int) and g < BUFS):
                    dve.wait_ge(shift, (g - BUFS + 1) * 4)
                nc.vector.tensor_reduce(MX[:, buf, t, 2 * j:2 * j + 2], PM[w % 2][:, :].rearrange("p (h m) -> p h m", h=2),
                                        AX.X, ALU.max).then_inc(max_out, 1)

            def heads(g, f):
                b, half = divmod(f, 2)
                sums = MB[:, :].rearrange("p (n q c w) -> p n q c w", n=TPB, q=2, c=QUAD)
                dve.wait_ge(pvt_full, g * FILLS + (f + 1))
                nc.vector.reciprocal(REC[:, :, :, :], sums[:, :, :, :, HD]).then_inc(recs, 1)
                if f == 0 and not (isinstance(g, int) and g == 0):
                    dve.wait_ge(ot_full, g)
                dve.wait_ge(recs, g * FILLS + (f + 1))
                for n in range(TPB):
                    nc.vector.tensor_tensor(
                        O[:, b * TPB + n, 2 * QUAD * half:2 * QUAD * (half + 1), :].rearrange("p (q c) d -> p q c d", q=2),
                        sums[:, n, :, :, 0:HD], REC[:, n, :, :].unsqueeze(3).to_broadcast([P, 2, QUAD, HD]),
                        ALU.mult).then_inc(o_out, 1)

            def residual(g):
                dve.wait_ge(proj_full, g + 1)
                xg = X[:, bass.ds(g * TPG, TPG), :]
                nc.vector.tensor_tensor(xg, xg, MB[:, :].rearrange("p (t c) -> p t c", t=TPG), ALU.add)\
                    .then_inc(x_added, 1)

            dve.wait_ge(weights_in, 128)
            dve.wait_ge(ones_set, 1)
            for g in range(3):
                for t in range(TPG):
                    norm_stats(g, t)
                if g < 2:
                    values(g, g)
                if g == 1:
                    for w in range(MAXU):
                        row_max(0, w, 0)
            for w in range(LEAD):
                row_max(1, w, 1)

            def step(g, r):
                for u in range(UNITS):
                    if u < MAXU - LEAD:
                        if not last(r, 1):
                            row_max(g + 1, u + LEAD, (r + 1) % BUFS)
                    elif not last(r, 2):
                        row_max(g + 2, u + LEAD - MAXU, (r + 2) % BUFS)
                    if u == 3 and not last(r, 2):
                        values(g + 2, (r + 2) % BUFS)
                    if u in (0, 1, 2, 4) and not last(r, 3):
                        norm_stats(g + 3, (0, 1, 2, 4).index(u))
                    if u == 5 and r > 0:
                        heads(g - 1, FILLS - 1)
                    if u == 11 and r > 0:
                        residual(g - 1)
                    if u in (14, 25, 29):
                        heads(g, (14, 25, 29).index(u))

            run(step, dve)
            heads(GROUPS - 1, FILLS - 1)
            residual(GROUPS - 1)

        @block.tensor
        def _(pe):
            def xnt(g, free, count):
                wait(pe, xn_done, (g + 1) * TPG)
                if free is not None:
                    wait(pe, free, count)
                for t in range(TPG):
                    mm = nc.tensor.transpose(MB[:, tile_cols(t)], XN[:, t, :], ident[:, :])
                mm.then_inc(xnt_full, 1)

            def q(g):
                wait(pe, xnt_out, g + 1)
                nc.tensor.matmul(MB[:, :], Wqk[:, 0, :], XNT[:, :], start=True, stop=True).then_inc(q_full, 1)

            def k(g, free, count):
                wait(pe, free, count)
                nc.tensor.matmul(MB[:, :], Wqk[:, 1, :], XNT[:, :], start=True, stop=True).then_inc(k_full, 1)

            def v(g, free, count):
                wait(pe, free, count)
                for t in range(TPG):
                    mm = nc.tensor.matmul(MB[:, tile_cols(t)], XNT[:, tile_cols(t)], Wqkv[:, 2 * C:3 * C],
                                          start=True, stop=True)
                mm.then_inc(v_full, 1)

            def max_scores(g, w, buf):
                t, j = divmod(w, PAIRS)
                b = t // TPB
                if w == 0:
                    wait(pe, packed, (g + 1) * (16 * N_PACK))
                if not (isinstance(g, int) and g * MAXU + w < 2):
                    wait(pe, max_out, g * MAXU + (w - 1))
                for i in range(2):
                    mm = nc.tensor.matmul(PM[w % 2][:, i * SEQ:(i + 1) * SEQ], QP[:, buf, i, j, tile_cols(t)],
                                          KP[:, buf, j, b * SEQ:(b + 1) * SEQ], start=True, stop=True)
                mm.then_inc(max_full, 1)

            def scores(g, u, r):
                b, h = divmod(u, HEADS)
                buf = r % BUFS
                if u == 0:
                    wait(pe, shifted, (g + 1) * 32)
                if not (isinstance(g, int) and g * UNITS + u < SCB):
                    wait(pe, exp_out, g * UNITS + (u + 1 - SCB))
                for m in range(TPB):
                    mm = nc.tensor.matmul(SC[(r * UNITS + u) % SCB][:, m * SEQ:(m + 1) * SEQ],
                                          KP[:, buf, h // 2, tile_cols(b * TPB + m)],
                                          QP[:, buf, h % 2, h // 2, b * SEQ:(b + 1) * SEQ], start=True, stop=True)
                mm.then_inc(score_full, 1)

            def pv(g, n, buf):
                b, q = divmod(n, QUADS // BPG)
                wait(pe, exp_out, g * UNITS + (n + 1) * QUAD)
                if n == 0:
                    wait(pe, v_out, g + 1)
                if n % 2 == 0 and not (isinstance(g, int) and g * FILLS + n // 2 < 2):
                    wait(pe, pv_out, g * FILLS + (n // 2 - 1))
                for m in range(TPB):
                    for c in range(QUAD):
                        mm = nc.tensor.matmul(
                            PV[n // 2 % 2][c * VW:(c + 1) * VW, n % 2 * SEQ:(n % 2 + 1) * SEQ],
                            V[:, buf, b * TPB + m, q * QUAD + c, :],
                            PR[:, (n * QUAD + c) % PRB, m * SEQ:(m + 1) * SEQ],
                            start=(m == 0), stop=(m == TPB - 1), tile_position=(0, c * VW), skip_group_check=True)
                mm.then_inc(pv_full, 1)

            def pvt(g, f, free, count):
                wait(pe, pv_out, g * FILLS + (f + 1))
                wait(pe, free, count)
                for n in range(TPB):
                    for q in range(2):
                        mm = nc.tensor.transpose(MB[:, tile_cols(2 * n + q)],
                                                 PVS[:, f % 2, q * SEQ + n * P:q * SEQ + (n + 1) * P], ident[:, :])
                mm.then_inc(pvt_full, 1)

            def ct(g, free, count):
                wait(pe, shift, (g + 1) * 4)
                wait(pe, free, count)
                for t in range(TPG):
                    mm = nc.tensor.transpose(MB[0:C_ROWS * HEADS, tile_cols(t)],
                                             CM[:, t, :, :].rearrange("p r h -> p (r h)"), ident[:, :])
                mm.then_inc(ct_full, 1)

            def ot(g, free, count):
                wait(pe, o_out, (g + 1) * TPB * FILLS)
                wait(pe, free, count)
                for t in range(TPG):
                    mm = nc.tensor.transpose(MB[:, tile_cols(t)], O[:, t, :, :].rearrange("p h d -> p (h d)"),
                                             ident[:, :])
                mm.then_inc(ot_full, 1)

            def proj(g):
                wait(pe, ot_out, g + 1)
                for t in range(TPG):
                    mm = nc.tensor.matmul(MB[:, tile_cols(t)], OT[:, tile_cols(t)], Wproj[:, :], start=True, stop=True)
                mm.then_inc(proj_full, 1)

            wait(pe, weights_in, 128)
            wait(pe, wqk_set, 2)
            for g in range(3):
                xnt(g, (None, v_out, ct_out)[g], 1)
                q(g)
                k(g, q_out, 2 * (g + 1))
                if g < 2:
                    v(g, k_out, 2 * (g + 1))
                if g == 1:
                    for w in range(MAXU):
                        max_scores(0, w, 0)
                    ct(0, v_out, 2)
            for w in range(LEAD):
                max_scores(1, w, 1)

            def step(g, r):
                n_o = TPB * FILLS
                for u in range(UNITS):
                    scores(g, u, r)
                    if u == 2 and r > 0:
                        pv(g - 1, QUADS - 1, (r - 1) % BUFS)
                    if u % QUAD == 2 and u > QUAD:
                        pv(g, u // QUAD - 1, r % BUFS)
                    if u < MAXU - LEAD:
                        if not last(r, 1):
                            max_scores(g + 1, u + LEAD, (r + 1) % BUFS)
                    elif not last(r, 2):
                        max_scores(g + 2, u + LEAD - MAXU, (r + 2) % BUFS)
                    if u == 1 and not last(r, 2):
                        if r > 0:
                            v(g + 2, o_out, (g - 1) * n_o + 3 * TPB)
                        else:
                            v(g + 2, k_out, 6)
                    if u == 5 and r > 0:
                        pvt(g - 1, FILLS - 1, *((v_out, g + 3) if not last(r, 2) else (o_out, (g - 1) * n_o + 3 * TPB)))
                    if u == 8 and r > 0:
                        ot(g - 1, o_out, g * n_o)
                    if u == 11 and r > 0:
                        proj(g - 1)
                    if u == 13:
                        pvt(g, 0, *((x_added, g) if r > 0 else (v_out, 3)))
                    if u == 16 and not last(r, 3):
                        xnt(g + 3, o_out, g * n_o + TPB)
                    if u == 18 and not last(r, 3):
                        q(g + 3)
                    if u == 21 and not last(r, 3):
                        k(g + 3, q_out, 2 * (g + 4))
                    if u == 23 and not last(r, 1):
                        ct(g + 1, *((k_out, 2 * (g + 4)) if not last(r, 3) else (o_out, g * n_o + TPB)))
                    if u == 25:
                        pvt(g, 1, *((ct_out, g + 2) if not last(r, 1) else (o_out, g * n_o + TPB)))
                    if u == 29:
                        pvt(g, 2, o_out, g * n_o + 2 * TPB)

            run(step, pe)
            g = GROUPS - 1
            pv(g, QUADS - 1, g % BUFS)
            pvt(g, FILLS - 1, o_out, TPB * (FILLS * g + 3))
            ot(g, o_out, TPB * FILLS * GROUPS)
            proj(g)


def choose_experts(nc, chip, X, ident, chosen, Wp1d, bp1, Wp2d, bp2):
    E = Wp2d.shape[1]
    with ExitStack() as ctx:
        def sb(name, shape, dt=F32):
            return chip.sb(ctx, name, shape, dt)

        Wp1, Wp2, b1c, b2r = sb("Wp1", [C, C]), sb("Wp2", [C, E]), sb("bp1c", [C, 1]), sb("bp2r", [P, E])
        L, LN = sb("L", [N_BATCH, C]), sb("LN", [N_BATCH, C])
        LT, NT = sb("LT", [C, N_BATCH]), sb("NT", [C, N_BATCH])
        stat, mv, var = sb("nstat", [N_BATCH, 6]), sb("nmv", [N_BATCH, 2]), sb("nvar", [N_BATCH, 1])
        ny, ntmp = sb("nny", [N_BATCH, NEWTON + 1, 1]), sb("nntmp", [N_BATCH, 2 * NEWTON, 1])
        logits, best, index = sb("logits", [N_BATCH, E]), sb("best", [N_BATCH, 8]), sb("index", [N_BATCH, 8], U32)
        last_rows = chip.dram("last_rows", [N_BATCH, C], F32)
        PT, PN, PL = (chip.ps(ctx, n, [P, GT]) for n in ("npt", "npn", "npl"))
        (w_in, rows_out, rows_in, chain, newton, t_full, t_out, n_full, n_out, l_full, found, stored) = (
            chip.sem(ctx, "n_" + n) for n in ("w_in rows_out rows_in chain newton t_full t_out n_full n_out l_full "
                                              "found stored").split())
        block = ctx.enter_context(nc.Block())

        @block.sync
        def _(sp):
            for dst, src in ((Wp1[:, :], Wp1d), (Wp2[:, :], Wp2d), (b1c[:, :], column(bp1)), (b2r[:, :], rows(bp2))):
                sp.dma_start(dst, src).then_inc(w_in, 16)
            sp.dma_start(last_rows.rearrange("(a b) c -> a b c", a=1), X[P - 1:P, TPB - 1::TPB, :]).then_inc(rows_out, 16)
            sp.wait_ge(rows_out, 16)
            sp.dma_start(L[:, :], last_rows).then_inc(rows_in, 16)
            sp.wait_ge(found, 1)
            sp.dma_start(chosen, index[:, 0:1]).then_inc(stored, 16)
            sp.wait_ge(stored, 16)

        @block.vector
        def _(dve):
            dve.wait_ge(w_in, 64)
            dve.wait_ge(rows_in, 16)
            nc.vector.bn_stats(stat[:, :], L[:, :]).then_inc(chain, 1)
            dve.wait_ge(chain, 1)
            nc.vector.bn_aggr(mv[:, :], stat[:, :]).then_inc(chain, 1)
            dve.wait_ge(chain, 2)
            nc.vector.tensor_scalar(var[:, :], mv[:, 1:2], LN_EPS, None, ALU.add).then_inc(chain, 1)
            dve.wait_ge(chain, 3)
            nc.vector.tensor_scalar(ny[:, 0, :].bitcast(I32), var[:, :].bitcast(I32), -0.5, RSQRT_SEED,
                                    ALU.mult, ALU.add).then_inc(newton, 1)
            dve.wait_ge(newton, 1)
            newton_rsqrt(nc.vector, w_in, newton, 1, ny, var[:, :], ntmp)
            nc.vector.tensor_scalar(LN[:, :], L[:, :], mv[:, 0:1], ny[:, NEWTON, 0:1], ALU.subtract, ALU.mult)\
                .then_inc(chain, 1)
            dve.wait_ge(t_full, 1)
            nc.vector.tensor_copy(LT[:, :], PT[:, 0:N_BATCH]).then_inc(t_out, 1)
            dve.wait_ge(l_full, 1)
            nc.vector.tensor_tensor(logits[:, :], PL[0:N_BATCH, 0:E], b2r[0:N_BATCH, :], ALU.add).then_inc(chain, 1)
            dve.wait_ge(chain, 5)
            nc.vector.max(best[:, :], logits[:, :]).then_inc(chain, 1)
            dve.wait_ge(chain, 6)
            nc.vector.max_index(index[:, :], best[:, :], logits[:, :]).then_inc(found, 1)

        @block.scalar
        def _(act):
            act.wait_ge(w_in, 64)
            act.wait_ge(n_full, 1)
            nc.scalar.activation(NT[:, :], PN[:, 0:N_BATCH], ACT.Gelu, bias=b1c[:, 0:1]).then_inc(n_out, 1)

        @block.tensor
        def _(pe):
            pe.wait_ge(w_in, 64)
            pe.wait_ge(chain, 4)
            nc.tensor.transpose(PT[:, 0:N_BATCH], LN[:, :], ident[0:N_BATCH, 0:N_BATCH]).then_inc(t_full, 1)
            pe.wait_ge(t_out, 1)
            nc.tensor.matmul(PN[:, 0:N_BATCH], Wp1[:, :], LT[:, :], start=True, stop=True).then_inc(n_full, 1)
            pe.wait_ge(n_out, 1)
            nc.tensor.matmul(PL[0:N_BATCH, 0:E], NT[:, :], Wp2[:, :], start=True, stop=True).then_inc(l_full, 1)


def mixers(nc, chip, X, ident, chosen, zrows, LG, t):
    E, _, F = t["L0_ffn_W1"].shape
    FT = F // P
    NB = FT + 1
    ER = t["L1_ffn_router_w"].shape[0]
    LAST = 5
    with ExitStack() as ctx:
        def sb(name, shape, dt=F32):
            return chip.sb(ctx, name, shape, dt)

        W1e, W2e = sb("W1e", [P, 2, BPG, F]), sb("W2e", [P, 2, BPG, FT, C])
        biases, Be = sb("biases", [P, E, NB]), sb("Be", [P, 2, BPG, NB])
        brow = sb("brow", [E, NB, P])
        sel = sb("sel", [1, N_BATCH], U32)
        Wo, bo3 = sb("Wo", [P, C]), sb("bo3", [P, C])
        Wraw, WT = sb("Wraw", [P, 3, C]), sb("WT", [P, 3, C])
        tmv, tmr, dec, decb = sb("tmv", [P, 1]), sb("tmr", [P, 1]), sb("dec", [P, 1]), sb("decb", [P, SEQ])
        zero = sb("zero", [P, SEQ])
        rw, rwT, rwS = sb("rw", [ER, C]), sb("rwT", [P, ER]), sb("rwS", [P, ER])
        rls, rlb, rbr, rbias = sb("rls", [P, 1]), sb("rlb", [P, 1]), sb("rbr", [P, ER]), sb("rbias", [P, ER])
        rlbb = sb("rlbb", [P, P])
        HN, YN, ZN = (sb(n, [P, TPG, C]) for n in ("HN", "YN", "ZN"))
        HT, RT, YT, VT, ZT = (sb(n, [P, GT]) for n in ("HT", "RT", "YT", "VT", "ZT"))
        G = sb("G", [P, BPG, FT, SEQ])
        ST = sb("ST", [P, BPG, SEQ + 1])
        DL, VI, RI = (sb(n, [P, GT]) for n in ("DL", "VI", "RI"))
        TH, MM = sb("TH", [P, TPG, C]), sb("MM", [P, TPG, C])
        stat = [sb(f"bst{n}", [P, TPG, 6]) for n in range(3)]
        mv = [sb(f"bmv{n}", [P, TPG, 2]) for n in range(3)]
        var = [sb(f"bva{n}", [P, TPG]) for n in range(3)]
        ny = [sb(f"bny{n}", [P, NEWTON + 1, TPG]) for n in range(3)]
        ntmp = [sb(f"bnt{n}", [P, 2 * NEWTON, TPG]) for n in range(3)]

        PT, PR_, PO, PVV, PG, PQ = (chip.ps(ctx, n, [P, GT]) for n in ("bpt", "bpr", "bpo", "bpv", "bpg", "bpq"))
        PH = [chip.ps(ctx, f"bph{n}", [P, GT]) for n in range(BPG)]

        def sem(name):
            return chip.sem(ctx, "b_" + name)

        (w_in, sel_in, zero_set, act_set, dve_set, pe_set, w_exp) = (
            sem(n) for n in ("w_in", "sel_in", "zero_set", "act_set", "dve_set", "pe_set", "w_exp"))
        stats = [sem(f"stats{n}") for n in range(3)]
        aggr = [sem(f"aggr{n}") for n in range(3)]
        newton = [sem(f"newton{n}") for n in range(3)]
        applied = [sem(f"applied{n}") for n in range(3)]
        (hn_added, ht_full, ht_out, h1_full, g_out, r_full, r_out, o_full, x_ffn, yt_full, yt_out, scanned, dl_out,
         mixed, v_full, v_out, gate_full, gate_out, o2_full, gated, x_rwkv, zt_full, zt_out, lg_full, lg_out,
         z_stored) = (sem(n) for n in (
             "hn_added ht_full ht_out h1_full g_out r_full r_out o_full x_ffn yt_full yt_out scanned dl_out mixed "
             "v_full v_out gate_full gate_out o2_full gated x_rwkv zt_full zt_out lg_full lg_out z_stored").split())
        N_IN = 15

        def tile_cols(n):
            return slice(n * P, (n + 1) * P)

        def tiles(m, g):
            return m[:, bass.ds(g * TPG, TPG), :]

        def run(step, eng):
            first, turns = LAST + 2, (GROUPS - 1 - (LAST + 2)) // 2
            for k in range(first):
                step(k, k)
            with eng.Fori(0, turns) as i:
                for r in range(2):
                    step(i * 2 + (first + r), first + r)
            for k in range(first + 2 * turns, GROUPS + LAST):
                step(k, k)

        def at(r, d):
            return 0 <= r - d < GROUPS

        block = ctx.enter_context(nc.Block())

        @block.sync
        def _(sp):
            loads = [
                (brow[:, 0:FT, :], t["L0_ffn_b1"].rearrange("e (n p) -> e n p", n=FT)), (brow[:, FT, :], t["L0_ffn_b2"]),
                (Wo[:, :], t["L0_ffn_Wo"]), (bo3[:, :], rows(t["L0_ffn_bo"])), (Wraw[:, 0, :], t["L1_attn_Wv"]),
                (Wraw[:, 1, :], t["L1_attn_Wr"]), (Wraw[:, 2, :], t["L1_attn_Wo"]),
                (tmv[:, :], column(t["L1_attn_time_mix_v"])), (tmr[:, :], column(t["L1_attn_time_mix_r"])),
                (dec[:, :], column(t["L1_attn_time_decay"])), (rw[:, :], t["L1_ffn_router_w"]),
                (rls[:, :], column(t["L1_ffn_router_ln_scale"])), (rlb[:, :], column(t["L1_ffn_router_ln_bias"])),
                (rbr[:, :], rows(t["L1_ffn_router_b"]))]
            assert len(loads) == N_IN - 1
            for dst, src in loads:
                sp.dma_start(dst, src).then_inc(w_in, 16)
            sp.dma_start(sel[:, :], chosen.rearrange("b a -> a b")).then_inc(sel_in, 16)
            sp.wait_ge(sel_in, 16)
            sp.wait_ge(dve_set, 1)

            def experts(g, r):
                for b in range(BPG):
                    e = sp.value_load(sel[0:1, bass.ds(g * BPG + b, 1)], min_val=0, max_val=E - 1)
                    sp.dma_start(W1e[:, r % 2, b, :], t["L0_ffn_W1"][bass.ds(e, 1)].rearrange("e k f -> k (e f)"))\
                        .then_inc(w_exp, 16)
                    sp.dma_start(W2e[:, r % 2, b, :, :], t["L0_ffn_W2"][bass.ds(e, 1)].rearrange(
                        "e (n p) h -> p (e n) h", n=FT)).then_inc(w_exp, 16)
                    sp.dma_start(Be[:, r % 2, b, :], biases[:, bass.ds(e, 1), :].rearrange("p e n -> p (e n)"))\
                        .then_inc(w_exp, 16)

            def store_z(g):
                wait_apart(sp, sel_in, applied[2], (g + 1) * TPG)
                sp.dma_start(zrows.rearrange("(t p) c -> p t c", p=P)[:, bass.ds(g * TPG, TPG), :], ZN[:, :, :])\
                    .then_inc(z_stored, 16)

            experts(0, 0)

            def step(k, r):
                if at(r, 0) and at(r + 1, 0):
                    wait_apart(sp, sel_in, w_exp, (k + 1) * (3 * 16 * BPG))
                    if r > 0:
                        wait_apart(sp, sel_in, r_out, k * BPG)
                    experts(k + 1, r + 1)
                if at(r, 4):
                    store_z(k - 4)

            run(step, sp)
            sp.wait_ge(z_stored, 16 * GROUPS)

        @block.gpsimd
        def _(pool):
            pool.wait_ge(w_in, 16 * (N_IN - 1))
            nc.gpsimd.memset(zero[:, :], 0.0).then_inc(zero_set, 1)

            def rsqrt(n, g):
                ops = NEWTON_OPS + 2
                base = g * ops
                wait_apart(pool, w_in, aggr[n], (g + 1) * TPG)
                if not (isinstance(g, int) and g == 0):
                    wait_apart(pool, w_in, applied[n], g * TPG)
                if n < 2:
                    nc.gpsimd.tensor_scalar(var[n][:, :], mv[n][:, :, 1], LN_EPS, None, ALU.add).then_inc(newton[n], 1)
                else:
                    nc.gpsimd.tensor_scalar(var[n][:, :], mv[n][:, :, 1], 1.0 + LN2_EPS, LN_EPS * LN2_EPS,
                                            ALU.mult, ALU.add).then_inc(newton[n], 1)
                wait_apart(pool, w_in, newton[n], base + 1)
                nc.gpsimd.tensor_scalar(ny[n][:, 0, :].bitcast(I32), var[n][:, :].bitcast(I32), -0.5, RSQRT_SEED,
                                        ALU.mult, ALU.add).then_inc(newton[n], 1)
                wait_apart(pool, w_in, newton[n], base + 2)
                newton_rsqrt(nc.gpsimd, w_in, newton[n], base + 2, ny[n], var[n][:, :], ntmp[n])

            def differences(g):
                wait_apart(pool, w_in, scanned, (g + 1) * BPG)
                if not (isinstance(g, int) and g == 0):
                    wait_apart(pool, w_in, mixed, g * 2)
                nc.gpsimd.tensor_tensor(DL[:, :].rearrange("p (b s) -> p b s", b=BPG),
                                        YT[:, :].rearrange("p (b s) -> p b s", b=BPG), ST[:, :, 0:SEQ],
                                        ALU.subtract).then_inc(dl_out, 1)

            def add_norm(g):
                wait_apart(pool, w_in, applied[0], (g + 1) * TPG)
                nc.gpsimd.tensor_tensor(tiles(X, g), tiles(X, g), HN[:, :, :], ALU.add).then_inc(hn_added, 1)
                wait_apart(pool, w_in, hn_added, g * 2 + 1)
                nc.gpsimd.tensor_tensor(tiles(X, g), tiles(X, g), bo3[:, :].unsqueeze(1).to_broadcast([P, TPG, C]),
                                        ALU.add).then_inc(hn_added, 1)

            pool.wait_ge(dve_set, 8)
            def step(k, r):
                if at(r, 0):
                    rsqrt(0, k)
                if at(r, 3):
                    differences(k - 3)
                if at(r, 2):
                    rsqrt(1, k - 2)
                if at(r, 0):
                    add_norm(k)
                if at(r, 4):
                    rsqrt(2, k - 4)

            run(step, pool)

        @block.scalar
        def _(act):
            act.wait_ge(w_in, 16 * (N_IN - 1))
            nc.scalar.activation(dec[:, :], dec[:, :], ACT.Exp).then_inc(act_set, 1)
            act.wait_ge(act_set, 1)
            nc.scalar.activation(dec[:, :], dec[:, :], ACT.Exp, scale=-1.0).then_inc(act_set, 1)
            act.wait_ge(act_set, 2)
            act.wait_ge(zero_set, 1)
            nc.scalar.activation(decb[:, :], zero[:, :], ACT.Identity, bias=dec[:, 0:1]).then_inc(act_set, 1)

            def turned(g, full, out, dst, used, per):
                act.wait_ge(full, g + 1)
                if not (isinstance(g, int) and g == 0):
                    act.wait_ge(used, g * per)
                nc.scalar.copy(dst[:, :], PT[:, :]).then_inc(out, 1)

            def gelus(g, b, r):
                act.wait_ge(h1_full, g * BPG + (b + 1))
                act.wait_ge(w_exp, (g + 1) * (3 * 16 * BPG))
                if b == 0 and not (isinstance(g, int) and g == 0):
                    act.wait_ge(r_full, g)
                for n in range(FT):
                    nc.scalar.activation(G[:, b, n, :], PH[b][:, n * SEQ:(n + 1) * SEQ], ACT.Gelu,
                                         bias=Be[:, r % 2, b, n:n + 1]).then_inc(g_out, 1)

            def reasoned(g, r):
                act.wait_ge(r_full, g + 1)
                if not (isinstance(g, int) and g == 0):
                    act.wait_ge(o_full, g)
                for b in range(BPG):
                    nc.scalar.activation(RT[:, b * SEQ:(b + 1) * SEQ], PR_[:, b * SEQ:(b + 1) * SEQ], ACT.Identity,
                                         bias=Be[:, r % 2, b, FT:NB]).then_inc(r_out, 1)

            def values(g):
                act.wait_ge(v_full, g + 1)
                if not (isinstance(g, int) and g == 0):
                    act.wait_ge(o2_full, g)
                nc.scalar.copy(VT[:, :], PVV[:, :]).then_inc(v_out, 1)

            def gate(g):
                act.wait_ge(gate_full, g + 1)
                if not (isinstance(g, int) and g == 0):
                    act.wait_ge(gated, g)
                nc.scalar.activation(TH[:, :, :], PG[:, :].rearrange("p (t c) -> p t c", t=TPG), ACT.Tanh, scale=0.5)\
                    .then_inc(gate_out, 1)

            def step(k, r):
                if at(r, 1):
                    gelus(k - 1, 0, r - 1)
                if at(r, 3):
                    turned(k - 3, yt_full, yt_out, YT, mixed, 2)
                if at(r, 4):
                    values(k - 4)
                    gate(k - 4)
                if at(r, 1):
                    gelus(k - 1, 1, r - 1)
                if at(r, 5):
                    turned(k - 5, zt_full, zt_out, ZT, lg_full, 1)
                if at(r, 1):
                    reasoned(k - 1, r - 1)
                if at(r, 0):
                    turned(k, ht_full, ht_out, HT, h1_full, BPG)

            run(step, act)

        @block.vector
        def _(dve):
            dve.wait_ge(w_in, 16 * (N_IN - 1))
            dve.wait_ge(pe_set, 1)
            nc.vector.tensor_copy(biases[:, :, :].rearrange("p e n -> p n e"),
                                  PT[:, 0:NB * E].rearrange("p (n e) -> p n e", n=NB)).then_inc(dve_set, 1)
            dve.wait_ge(pe_set, 2)
            nc.vector.tensor_copy(WT[:, :, :], PO[:, 0:3 * C].rearrange("p (n c) -> p n c", n=3)).then_inc(dve_set, 1)
            nc.vector.tensor_scalar(bo3[:, :], bo3[:, :], 0.3, None, ALU.mult).then_inc(dve_set, 1)
            nc.vector.memset(ST[:, :, 0:1], 0.0).then_inc(dve_set, 1)
            dve.wait_ge(pe_set, 3)
            nc.vector.tensor_copy(rwT[:, :], PG[:, 0:ER]).then_inc(dve_set, 1)
            nc.vector.tensor_scalar(rwS[:, :], PG[:, 0:ER], rls[:, 0:1], None, ALU.mult).then_inc(dve_set, 1)
            nc.vector.tensor_scalar(rlbb[:, :], ident[:, :], 0.0, rlb[:, 0:1], ALU.mult, ALU.add).then_inc(dve_set, 1)
            dve.wait_ge(pe_set, 4)
            nc.vector.tensor_tensor(rbias[:, :], PQ[:, 0:ER], rbr[:, :], ALU.add).then_inc(dve_set, 1)
            dve.wait_ge(dve_set, 8)
            dve.wait_ge(act_set, 3)

            def norm_stats(n, g):
                if not (isinstance(g, int) and g == 0):
                    wait_apart(dve, w_in, applied[n], g * TPG)
                for i in range(TPG):
                    nc.vector.bn_stats(stat[n][:, i, :], X[:, bass.ds(g * TPG + i, 1), :].rearrange("p a c -> p (a c)"))\
                        .then_inc(stats[n], 1)
                for i in range(TPG):
                    wait_apart(dve, w_in, stats[n], g * TPG + (i + 1))
                    nc.vector.bn_aggr(mv[n][:, i, :], stat[n][:, i, :]).then_inc(aggr[n], 1)

            def apply(n, g, dst, used, per):
                dve.wait_ge(newton[n], (g + 1) * (NEWTON_OPS + 2))
                if not (isinstance(g, int) and g == 0):
                    dve.wait_ge(used, g * per)
                    if n == 2:
                        dve.wait_ge(z_stored, g * 16)
                    if n == 0:
                        dve.wait_ge(hn_added, g * 2)
                for i in range(TPG):
                    nc.vector.tensor_scalar(dst[:, i, :], X[:, bass.ds(g * TPG + i, 1), :].rearrange("p a c -> p (a c)"),
                                            mv[n][:, i, 0:1], ny[n][:, NEWTON, i:i + 1], ALU.subtract, ALU.mult)\
                        .then_inc(applied[n], 1)

            def scan(g):
                dve.wait_ge(yt_out, g + 1)
                if not (isinstance(g, int) and g == 0):
                    dve.wait_ge(mixed, g * 2)
                for b in range(BPG):
                    nc.vector.tensor_tensor_scan(ST[:, b, 1:SEQ + 1], decb[:, :], YT[:, b * SEQ:(b + 1) * SEQ], 0.0,
                                                 ALU.mult, ALU.add).then_inc(scanned, 1)

            def mixes(g):
                dve.wait_ge(dl_out, g + 1)
                if not (isinstance(g, int) and g == 0):
                    dve.wait_ge(gate_full, g)
                for dst, m in ((VI, tmv), (RI, tmr)):
                    nc.vector.scalar_tensor_tensor(
                        out=dst[:, :].rearrange("p (b s) -> p b s", b=BPG), in0=DL[:, :].rearrange("p (b s) -> p b s", b=BPG),
                        scalar=m[:, 0:1], in1=ST[:, :, 0:SEQ], op0=ALU.mult, op1=ALU.add).then_inc(mixed, 1)

            def ffn_residual(g):
                dve.wait_ge(o_full, g + 1)
                dve.wait_ge(hn_added, (g + 1) * 2)
                nc.vector.scalar_tensor_tensor(out=tiles(X, g), in0=PO[:, :].rearrange("p (t c) -> p t c", t=TPG), scalar=0.3,
                                               in1=tiles(X, g), op0=ALU.mult, op1=ALU.add).then_inc(x_ffn, 1)
                dve.wait_ge(x_ffn, g + 1)

            def rwkv_residual(g):
                dve.wait_ge(gate_out, g + 1)
                dve.wait_ge(o2_full, g + 1)
                nc.vector.scalar_tensor_tensor(out=MM[:, :, :], in0=TH[:, :, :], scalar=1.0,
                                               in1=PQ[:, :].rearrange("p (t c) -> p t c", t=TPG), op0=ALU.add,
                                               op1=ALU.mult).then_inc(gated, 1)
                dve.wait_ge(gated, g + 1)
                nc.vector.scalar_tensor_tensor(out=tiles(X, g), in0=MM[:, :, :], scalar=0.5, in1=tiles(X, g),
                                               op0=ALU.mult, op1=ALU.add).then_inc(x_rwkv, 1)
                dve.wait_ge(x_rwkv, g + 1)

            def logits(g):
                dve.wait_ge(lg_full, g + 1)
                nc.vector.tensor_tensor(LG[:, bass.ds(g * TPG, TPG), :], PT[:, 0:TPG * ER].rearrange("p (t e) -> p t e", t=TPG),
                                        rbias[:, :].unsqueeze(1).to_broadcast([P, TPG, ER]), ALU.add).then_inc(lg_out, 1)

            def step(k, r):
                if at(r, 0):
                    norm_stats(0, k)
                if at(r, 3):
                    scan(k - 3)
                if at(r, 2):
                    ffn_residual(k - 2)
                    norm_stats(1, k - 2)
                if at(r, 0):
                    apply(0, k, HN, ht_full, 1)
                if at(r, 3):
                    mixes(k - 3)
                if at(r, 4):
                    rwkv_residual(k - 4)
                    norm_stats(2, k - 4)
                if at(r, 5):
                    logits(k - 5)
                if at(r, 2):
                    apply(1, k - 2, YN, yt_full, 1)
                if at(r, 4):
                    apply(2, k - 4, ZN, zt_full, 1)

            run(step, dve)

        @block.tensor
        def _(pe):
            wait(pe, w_in, 16 * (N_IN - 1))
            for n in range(NB):
                mm = nc.tensor.transpose(PT[:, n * E:(n + 1) * E], brow[:, n, :], ident[0:E, 0:E])
            mm.then_inc(pe_set, 1)
            for n in range(3):
                mm = nc.tensor.transpose(PO[:, tile_cols(n)], Wraw[:, n, :], ident[:, :])
            mm.then_inc(pe_set, 1)
            nc.tensor.transpose(PG[:, 0:ER], rw[:, :], ident[0:ER, 0:ER]).then_inc(pe_set, 1)
            wait(pe, dve_set, 7)
            nc.tensor.matmul(PQ[:, 0:ER], rlbb[:, :], rwT[:, :], start=True, stop=True).then_inc(pe_set, 1)
            wait(pe, dve_set, 8)

            def turn(src, ready, full, g, free, count):
                wait(pe, ready, (g + 1) * TPG)
                wait(pe, free, count)
                for n in range(TPG):
                    mm = nc.tensor.transpose(PT[:, tile_cols(n)], src[:, n, :], ident[:, :])
                mm.then_inc(full, 1)

            def first_product(g, r):
                wait(pe, ht_out, g + 1)
                wait(pe, w_exp, (g + 1) * (3 * 16 * BPG))
                if not (isinstance(g, int) and g == 0):
                    wait(pe, g_out, g * BPG * FT)
                for b in range(BPG):
                    for n in range(FT):
                        mm = nc.tensor.matmul(PH[b][:, n * SEQ:(n + 1) * SEQ], W1e[:, r % 2, b, n * P:(n + 1) * P],
                                              HT[:, b * SEQ:(b + 1) * SEQ], start=True, stop=True)
                    mm.then_inc(h1_full, 1)

            def second_product(g, r):
                wait(pe, g_out, (g + 1) * BPG * FT)
                if not (isinstance(g, int) and g == 0):
                    wait(pe, r_out, g * BPG)
                for b in range(BPG):
                    for n in range(FT):
                        mm = nc.tensor.matmul(PR_[:, b * SEQ:(b + 1) * SEQ], W2e[:, r % 2, b, n, :], G[:, b, n, :],
                                              start=(n == 0), stop=(n == FT - 1))
                mm.then_inc(r_full, 1)

            def by_rows(bank, src, w, full):
                for n in range(TPG):
                    mm = nc.tensor.matmul(bank[:, tile_cols(n)], src[:, tile_cols(n)], w, start=True, stop=True)
                mm.then_inc(full, 1)

            def ffn_out(g):
                wait(pe, r_out, (g + 1) * BPG)
                if not (isinstance(g, int) and g == 0):
                    wait(pe, x_ffn, g)
                by_rows(PO, RT, Wo[:, :], o_full)

            def values_gates(g):
                wait(pe, mixed, (g + 1) * 2)
                if not (isinstance(g, int) and g == 0):
                    wait(pe, v_out, g)
                nc.tensor.matmul(PVV[:, :], WT[:, 0, :], VI[:, :], start=True, stop=True).then_inc(v_full, 1)
                if not (isinstance(g, int) and g == 0):
                    wait(pe, gate_out, g)
                by_rows(PG, RI, WT[:, 1, :], gate_full)

            def rwkv_out(g):
                wait(pe, v_out, g + 1)
                if not (isinstance(g, int) and g == 0):
                    wait(pe, gated, g)
                by_rows(PQ, VT, WT[:, 2, :], o2_full)

            def router(g):
                wait(pe, zt_out, g + 1)
                for n in range(TPG):
                    mm = nc.tensor.matmul(PT[:, n * ER:(n + 1) * ER], ZT[:, tile_cols(n)], rwS[:, :], start=True, stop=True)
                mm.then_inc(lg_full, 1)

            def step(k, r):
                before = [(dve_set, 8)]
                if at(r - 1, 0):
                    before = [(ht_out, k)]
                elif at(r - 1, 5):
                    before = [(lg_out, k - 5)]
                elif at(r - 1, 3):
                    before = [(yt_out, k - 3)]
                if at(r, 1):
                    first_product(k - 1, r - 1)
                if at(r, 3):
                    turn(YN, applied[1], yt_full, k - 3, *before[0])
                    before = [(yt_out, k - 2)]
                if at(r, 4):
                    values_gates(k - 4)
                if at(r, 2):
                    ffn_out(k - 2)
                if at(r, 5):
                    turn(ZN, applied[2], zt_full, k - 5, *before[0])
                if at(r, 1):
                    second_product(k - 1, r - 1)
                if at(r, 4):
                    rwkv_out(k - 4)
                if at(r, 5):
                    router(k - 5)
                    before = [(lg_out, k - 4)]
                if at(r, 0):
                    turn(HN, applied[0], ht_full, k, *before[0])

            run(step, pe)


E_SLOTS = 512
SUB = E_SLOTS // P
BIG = 3.0e38


def fold_weights(nc, chip, ident, W1T, W2T, B1, t):
    E, H, D = t["L1_ffn_w1"].shape
    HT = H // P
    with ExitStack() as ctx:
        def sb(name, shape, dt=F32):
            return chip.sb(ctx, name, shape, dt)

        R1, R2 = sb("R1", [P, E, HT, D]), sb("R2", [P, E, H])
        lrow, brow = sb("lrow", [E, 2, D]), sb("b1row", [E, H])
        lcol = sb("lcol", [P, 2, E])
        PA, PB = ([chip.ps(ctx, f"f{n}{i}", [P, H]) for i in range(2)] for n in "ab")
        PC, PD = chip.ps(ctx, "fc", [P, GT]), chip.ps(ctx, "fd", [P, GT])
        (w_in, c_full, c_out, a_full, a_out, a_scaled, b_full, b_out, bias_full, bias_out) = (
            chip.sem(ctx, "f_" + n) for n in "w_in c_full c_out a_full a_out a_scaled b_full b_out bias_full bias_out".split())
        block = ctx.enter_context(nc.Block())

        @block.sync
        def _(sp):
            for dst, src in ((lrow[:, 0, :], t["L1_ffn_expert_ln_scale"]), (lrow[:, 1, :], t["L1_ffn_expert_ln_bias"]),
                             (brow[:, :], t["L1_ffn_b1"]), (R1[:, :, :, :], t["L1_ffn_w1"].rearrange(
                                 "e (n p) d -> p e n d", p=P)), (R2[:, :, :], t["L1_ffn_w2"].rearrange("e d h -> d e h"))):
                sp.dma_start(dst, src).then_inc(w_in, 16)

        @block.tensor
        def _(pe):
            pe.wait_ge(w_in, 80)
            for n in range(2):
                nc.tensor.transpose(PC[:, n * E:(n + 1) * E], lrow[:, n, :], ident[0:E, 0:E])
            for n in range(HT):
                mm = nc.tensor.transpose(PC[:, (2 + n) * E:(3 + n) * E], brow[:, n * P:(n + 1) * P], ident[0:E, 0:E])
            mm.then_inc(c_full, 1)
            for e in range(E):
                if e >= 2:
                    pe.wait_ge(a_out, e - 1)
                    pe.wait_ge(b_out, e - 1)
                for n in range(HT):
                    mm = nc.tensor.transpose(PA[e % 2][:, n * P:(n + 1) * P], R1[:, e, n, :], ident[:, :])
                mm.then_inc(a_full, 1)
                for n in range(HT):
                    mm = nc.tensor.transpose(PB[e % 2][:, n * P:(n + 1) * P], R2[:, e, n * P:(n + 1) * P], ident[:, :])
                mm.then_inc(b_full, 1)
            pe.wait_ge(c_out, 1)
            pe.wait_ge(a_out, E)
            for e in range(E):
                for n in range(HT):
                    mm = nc.tensor.matmul(PD[:, e * HT + n:e * HT + n + 1], W1T[:, e, n * P:(n + 1) * P],
                                          lcol[:, 1, e:e + 1], start=True, stop=True)
            mm.then_inc(bias_full, 1)

        @block.vector
        def _(dve):
            dve.wait_ge(c_full, 1)
            nc.vector.tensor_copy(lcol[:, :, :], PC[:, 0:2 * E].rearrange("p (n e) -> p n e", n=2)).then_inc(c_out, 1)
            nc.vector.tensor_copy(B1[:, :, :].rearrange("p e n -> p n e"),
                                  PC[:, 2 * E:(2 + HT) * E].rearrange("p (n e) -> p n e", n=HT)).then_inc(c_out, 1)
            for e in range(E):
                dve.wait_ge(a_full, e + 1)
                nc.vector.tensor_copy(W1T[:, e, :], PA[e % 2][:, :]).then_inc(a_out, 1)
            dve.wait_ge(bias_full, 1)
            dve.wait_ge(c_out, 2)
            nc.vector.tensor_tensor(B1[:, :, :], B1[:, :, :], PD[:, 0:E * HT].rearrange("p (e n) -> p e n", e=E), ALU.add)\
                .then_inc(bias_out, 1)
            dve.wait_ge(a_out, E)
            for e in range(E):
                nc.vector.tensor_scalar(W1T[:, e, :], W1T[:, e, :], lcol[:, 0, e:e + 1], None, ALU.mult)\
                    .then_inc(a_scaled, 1)

        @block.scalar
        def _(act):
            for e in range(E):
                act.wait_ge(b_full, e + 1)
                nc.scalar.copy(W2T[:, e, :], PB[e % 2][:, :]).then_inc(b_out, 1)


def route(nc, chip, LG, gates, source, target, owner, NT):
    E = LG.shape[2]
    NB = NT * SUB
    with ExitStack() as ctx:
        def sb(name, shape, dt=F32):
            return chip.sb(ctx, name, shape, dt)

        EQ, L2, SL = (sb(n, [P, TILES, E]) for n in ("EQ", "L2", "SL"))
        M = [sb(f"M{n}", [P, TILES, E]) for n in range(2)]
        m = [sb(f"m{n}", [P, TILES]) for n in range(2)]
        r = [sb(f"r{n}", [P, TILES]) for n in range(2)]
        revi, rev = sb("revi", [P, E], I32), sb("rev", [P, E])
        diff, ed, den = (sb(n, [P, TILES]) for n in ("diff", "ed", "den"))
        tri, ones = sb("tri", [P, P]), sb("ones", [P, P])
        M12, CT, one_t = sb("M12", [P, TILES, E]), sb("CT", [P, E, TILES]), sb("one_t", [P, TILES * E])
        SX = sb("SX", [P, TILES * E + 1])
        ni, nf, EB, OFF = sb("ni", [P, E], I32), sb("nf", [P, E]), sb("EB", [P, E + 1]), sb("OFF", [P, E])
        slot, sloti = sb("slot", [P, 2, TILES]), sb("sloti", [P, 2, TILES], I32)
        blk_i, row_i = sb("blk_i", [P, 2, TILES], I32), sb("row_i", [P, 2, TILES], I32)
        blk, row = sb("blk", [P, 2, TILES]), sb("row", [P, 2, TILES])
        ids_i, ids = sb("ids_i", [P, 2 * TILES], I32), sb("ids", [P, 2 * TILES])
        ior_i, ior = sb("ior_i", [P, P], I32), sb("ior", [P, P])
        iob_i, iob = sb("iob_i", [P, NB], I32), sb("iob", [P, NB])
        iot_i, iot = sb("iot_i", [1, NT], I32), sb("iot", [1, NT])
        RH, BH = sb("RH", [P, 4, P]), sb("BH", [P, 4, NB])
        val, em, tg, si = sb("val", [P, NB]), sb("em", [P, NB]), sb("tg", [P, NB]), sb("si", [P, NB], I32)
        cmp_, cnt = sb("cmp", [1, NT, E - 1]), sb("cnt", [1, NT])
        PP, PT, PI = (chip.ps(ctx, n, [P, 512]) for n in ("rpp", "rpt", "rpi"))
        iotas, consts, chain, exped, masked, counted, ready, rows_up, blocks_up, inverse, matched = (
            chip.sem(ctx, "r_" + n) for n in
            "iotas consts chain exped masked counted ready rows_up blocks_up inverse matched".split())
        N = 2 * TILES
        block = ctx.enter_context(nc.Block())

        @block.gpsimd
        def _(pool):
            nc.gpsimd.iota(revi[:, :], pattern=[[-1, E]], base=E, channel_multiplier=0).then_inc(iotas, 1)
            nc.gpsimd.iota(ids_i[:, :], pattern=[[P, N]], base=1, channel_multiplier=1).then_inc(iotas, 1)
            nc.gpsimd.iota(ior_i[:, :], pattern=[[1, P]], base=0, channel_multiplier=0).then_inc(iotas, 1)
            nc.gpsimd.iota(iob_i[:, :], pattern=[[1, NB]], base=0, channel_multiplier=0).then_inc(iotas, 1)
            nc.gpsimd.iota(iot_i[:, :], pattern=[[E_SLOTS, NT]], base=0, channel_multiplier=0).then_inc(iotas, 1)
            nc.gpsimd.memset(tri[:, :], 1.0).then_inc(consts, 1)
            nc.gpsimd.memset(ones[:, :], 1.0).then_inc(consts, 1)
            nc.gpsimd.memset(one_t[:, :], 1.0).then_inc(consts, 1)
            pool.wait_ge(consts, 3)
            nc.gpsimd.affine_select(out=tri[:, :], in_=tri[:, :], compare_op=ALU.is_gt, fill=0.0, base=0,
                                    pattern=[[1, P]], channel_multiplier=-1).then_inc(consts, 1)
            pool.wait_ge(ready, 1)
            for n in range(N):
                k, tile = divmod(n, TILES)
                if n >= 4:
                    pool.wait_ge(matched, n - 3)
                nc.gpsimd.tensor_scalar(BH[:, n % 4, :], iob[:, :], blk[:, k, tile:tile + 1], ids[:, n:n + 1],
                                        ALU.is_equal, ALU.mult).then_inc(blocks_up, 1)

        @block.scalar
        def _(act):
            act.wait_ge(exped, 1)
            nc.scalar.activation(ed[:, :], diff[:, :], ACT.Exp).then_inc(exped, 1)

        @block.tensor
        def _(pe):
            pe.wait_ge(consts, 4)
            pe.wait_ge(masked, 1)
            m12 = M12[:, :, :].rearrange("p t e -> p (t e)")
            nc.tensor.matmul(PP[:, :], tri[:, :], m12, start=True, stop=True)
            nc.tensor.matmul(PT[:, :], ones[:, :], m12, start=True, stop=True).then_inc(counted, 1)
            for n in range(N):
                pe.wait_ge(rows_up, n + 1)
                pe.wait_ge(blocks_up, n + 1)
                nc.tensor.matmul(PI[:, 0:NB], RH[:, n % 4, :], BH[:, n % 4, :], start=(n == 0), stop=(n == N - 1))\
                    .then_inc(matched, 1)

        @block.vector
        def _(dve):
            done = [0]

            def link(ins):
                done[0] += 1
                ins.then_inc(chain, 1)
                dve.wait_ge(chain, done[0])

            def over_e(x):
                return x.unsqueeze(2).to_broadcast([P, TILES, E])

            def over_t(x):
                return x.unsqueeze(1).to_broadcast([P, TILES, E])

            dve.wait_ge(iotas, 5)
            for dst, src in ((rev, revi), (ids, ids_i), (ior, ior_i), (iob, iob_i), (iot, iot_i)):
                link(nc.vector.tensor_copy(dst[:, :], src[:, :]))
            for n, l in enumerate((LG, L2)):
                link(nc.vector.tensor_reduce(m[n][:, :], l[:, :, :], AX.X, ALU.max))
                link(nc.vector.tensor_tensor(EQ[:, :, :], l[:, :, :], over_e(m[n][:, :]), ALU.is_equal))
                link(nc.vector.tensor_tensor(EQ[:, :, :], EQ[:, :, :], over_t(rev[:, :]), ALU.mult))
                link(nc.vector.tensor_reduce(r[n][:, :], EQ[:, :, :], AX.X, ALU.max))
                link(nc.vector.tensor_tensor(M[n][:, :, :], over_t(rev[:, :]), over_e(r[n][:, :]), ALU.is_equal))
                if n == 0:
                    link(nc.vector.scalar_tensor_tensor(out=L2[:, :, :], in0=M[0][:, :, :], scalar=-BIG,
                                                        in1=LG[:, :, :], op0=ALU.mult, op1=ALU.add))
            nc.vector.tensor_tensor(M12[:, :, :], M[0][:, :, :], M[1][:, :, :], ALU.add).then_inc(masked, 1)
            nc.vector.tensor_tensor(diff[:, :], m[1][:, :], m[0][:, :], ALU.subtract).then_inc(exped, 1)
            dve.wait_ge(exped, 2)
            link(nc.vector.tensor_scalar(den[:, :], ed[:, :], 1.0, None, ALU.add))
            link(nc.vector.reciprocal(gates[:, 0, :], den[:, :]))
            link(nc.vector.tensor_tensor(gates[:, 1, :], ed[:, :], gates[:, 0, :], ALU.mult))
            dve.wait_ge(counted, 1)
            link(nc.vector.tensor_copy(CT[:, :, :], PT[:, :].rearrange("p (t e) -> p e t", e=E)))
            link(nc.vector.memset(SX[:, 0:1], 0.0))
            link(nc.vector.tensor_tensor_scan(SX[:, 1:], one_t[:, :], CT[:, :, :].rearrange("p e t -> p (e t)"), 0.0,
                                              ALU.mult, ALU.add))
            link(nc.vector.tensor_tensor(nf[:, :], SX[:, TILES::TILES], SX[:, 0:TILES * E:TILES], ALU.subtract))
            link(nc.vector.tensor_scalar(ni[:, :], nf[:, :], float(E_SLOTS - 1), None, ALU.add))
            shift = E_SLOTS.bit_length() - 1
            link(nc.vector.tensor_scalar(ni[:, :], ni[:, :], shift, shift, ALU.logical_shift_right,
                                         ALU.logical_shift_left))
            link(nc.vector.tensor_copy(nf[:, :], ni[:, :]))
            link(nc.vector.memset(EB[:, 0:1], 0.0))
            link(nc.vector.tensor_tensor_scan(EB[:, 1:], one_t[:, 0:E], nf[:, :], 0.0, ALU.mult, ALU.add))
            link(nc.vector.tensor_tensor(OFF[:, :], EB[:, 0:E], SX[:, 0:TILES * E:TILES], ALU.subtract))
            link(nc.vector.tensor_tensor(SL[:, :, :], PP[:, :].rearrange("p (t e) -> p t e", e=E),
                                         SX[:, 0:TILES * E].rearrange("p (e t) -> p t e", e=E), ALU.add))
            link(nc.vector.tensor_tensor(SL[:, :, :], SL[:, :, :], over_t(OFF[:, :]), ALU.add))
            for n in range(2):
                link(nc.vector.tensor_tensor(EQ[:, :, :], SL[:, :, :], M[n][:, :, :], ALU.mult))
                link(nc.vector.tensor_reduce(slot[:, n, :], EQ[:, :, :], AX.X, ALU.add))
            link(nc.vector.tensor_copy(sloti[:, :, :], slot[:, :, :]))
            link(nc.vector.tensor_scalar(blk_i[:, :, :], sloti[:, :, :], 7, None, ALU.logical_shift_right))
            link(nc.vector.tensor_scalar(row_i[:, :, :], sloti[:, :, :], P - 1, None, ALU.bitwise_and))
            link(nc.vector.tensor_copy(row[:, :, :], row_i[:, :, :]))
            nc.vector.tensor_copy(blk[:, :, :], blk_i[:, :, :]).then_inc(ready, 1)
            for n in range(N):
                k, tile = divmod(n, TILES)
                if n >= 4:
                    dve.wait_ge(matched, n - 3)
                nc.vector.tensor_scalar(RH[:, n % 4, :], ior[:, :], row[:, k, tile:tile + 1], None, ALU.is_equal)\
                    .then_inc(rows_up, 1)
                if n == 4:
                    link(nc.vector.tensor_tensor(cmp_[:, :, :], iot[:, :].unsqueeze(2).to_broadcast([1, NT, E - 1]),
                                                 EB[0:1, 1:E].unsqueeze(1).to_broadcast([1, NT, E - 1]), ALU.is_ge))
                    link(nc.vector.tensor_reduce(cnt[:, :], cmp_[:, :, :], AX.X, ALU.add))
                    link(nc.vector.tensor_copy(owner[:, :], cnt[:, :]))
            dve.wait_ge(matched, N)
            link(nc.vector.tensor_copy(val[:, :], PI[:, 0:NB]))
            link(nc.vector.tensor_scalar(em[:, :], val[:, :], 0.0, float(4 * TOKENS), ALU.is_equal, ALU.mult))
            link(nc.vector.scalar_tensor_tensor(out=tg[:, :], in0=val[:, :], scalar=-1.0, in1=em[:, :], op0=ALU.add,
                                                op1=ALU.add))
            link(nc.vector.tensor_copy(target[:, :], tg[:, :]))
            link(nc.vector.tensor_copy(si[:, :], tg[:, :]))
            link(nc.vector.tensor_scalar(source[:, :].bitcast(I32), si[:, :], TOKENS - 1, None, ALU.bitwise_and))


def routed_experts(nc, chip, X, ident, zrows, gates, source, target, owner, W1T, W2T, B1, b2, out, NT):
    E, H = W1T.shape[1], W1T.shape[2]
    HT = H // P
    LAST = 4
    LOAD = 8
    with ExitStack() as ctx:
        def sb(name, shape, dt=F32):
            return chip.sb(ctx, name, shape, dt)

        W1e, W2e, b1e, b2e = (sb("W1x", [P, 2, H]), sb("W2x", [P, 3, H]), sb("b1x", [P, 2, HT]), sb("b2x", [P, 4, C]))
        IS, IT = sb("IS", [P, 2, SUB], U32), sb("IT", [P, 2, SUB], U32)
        GX, GT_ = sb("GX", [P, 2, SUB, C]), sb("GXT", [P, 2, E_SLOTS])
        HG = sb("HG", [P, 2, HT, E_SLOTS])
        YS = sb("YS", [P, 2, SUB, C])
        Y = sb("Y", [P, 2, 2, LOAD, C])
        results = chip.dram("results", [2 * TOKENS, C], F32)
        PT = chip.ps(ctx, "xpt", [P, E_SLOTS])
        PH = [chip.ps(ctx, f"xph{n}", [P, E_SLOTS]) for n in range(HT)]
        PY = [chip.ps(ctx, f"xpy{n}", [P, E_SLOTS]) for n in range(2)]
        idx_ok = chip.sem(ctx, "x_start")
        (w1_in, w2_in, idx, gathered, t_full, t_out, h_full, h_out, y_full, y_out, scattered, tgt, y_in, mixed, added,
         x_out) = (chip.sem(ctx, "x_" + n) for n in (
             "w1_in w2_in idx gathered t_full t_out h_full h_out y_full y_out scattered tgt y_in mixed added x_out").split())

        def run(step, eng):
            first = LAST + 2
            turns = (NT - 1 - first) // 2
            for k in range(first):
                step(k, k)
            with eng.Fori(0, turns) as i:
                for r in range(2):
                    step(i * 2 + (first + r), first + r)
            for k in range(first + 2 * turns, NT + LAST):
                step(k, k)

        def at(r, d):
            return 0 <= r - d < NT

        def early(g, n):
            return isinstance(g, int) and g < n

        def store(sp, n):
            sp.wait_ge(added, (n + 1) * LOAD)
            sp.dma_start(out.rearrange("b (t p) c -> p (b t) c", p=P)[:, n * LOAD:(n + 1) * LOAD, :],
                         X[:, n * LOAD:(n + 1) * LOAD, :]).then_inc(x_out, 16)

        block = ctx.enter_context(nc.Block())

        @block.sync
        def _(sp):
            sp.dma_start(b2e[:, 2, :], rows(b2[0, :])).then_inc(idx_ok, 16)
            sp.wait_ge(idx_ok, 16)

            def load(j, r):
                e = sp.value_load(owner[0:1, bass.ds(j, 1)], min_val=0, max_val=E - 1)
                if not early(j, 1):
                    wait_apart(sp, idx_ok, w1_in, j * 32)
                if not early(j, 2):
                    wait_apart(sp, idx_ok, h_full, (j - 1) * HT)
                    wait_apart(sp, idx_ok, h_out, (j - 1) * HT)
                sp.dma_start(W1e[:, r % 2, :], W1T[:, bass.ds(e, 1), :].rearrange("p e h -> p (e h)")).then_inc(w1_in, 16)
                sp.dma_start(b1e[:, r % 2, :], B1[:, bass.ds(e, 1), :].rearrange("p e h -> p (e h)")).then_inc(w1_in, 16)

            def load2(j, r):
                e = sp.value_load(owner[0:1, bass.ds(j, 1)], min_val=0, max_val=E - 1)
                if not early(j, 1):
                    wait_apart(sp, idx_ok, w2_in, j * 32)
                if not early(j, 2):
                    wait_apart(sp, idx_ok, y_full, j - 1)
                    wait_apart(sp, idx_ok, y_out, j - 1)
                sp.dma_start(W2e[:, r % 2, :], W2T[:, bass.ds(e, 1), :].rearrange("p e h -> p (e h)")).then_inc(w2_in, 16)
                sp.dma_start(b2e[:, r % 2, :], bass.AP(tensor=b2.tensor, offset=b2.offset, ap=[[0, P]] + [list(x) for x in b2.ap])[
                    :, bass.ds(e, 1), :].rearrange("p e h -> p (e h)")).then_inc(w2_in, 16)

            def step(k, r):
                if at(r, 1):
                    load(k - 1, r - 1)
                if at(r, 2):
                    load2(k - 2, r - 2)

            run(step, sp)
            sp.wait_ge(scattered, NT * SUB * 16)
            for n in range(TILES // LOAD):
                if n >= 2:
                    sp.wait_ge(added, (n - 1) * LOAD)
                sp.wait_ge(y_in, 32 * n)
                for k in range(2):
                    sp.dma_start(Y[:, n % 2, k, :, :], results.rearrange("(k t p) c -> p k t c", k=2, p=P)[
                        :, k, n * LOAD:(n + 1) * LOAD, :]).then_inc(y_in, 16)
                if n > 0:
                    store(sp, n - 1)
            store(sp, TILES // LOAD - 1)
            sp.wait_ge(x_out, 16 * (TILES // LOAD))

        @block.gpsimd
        def _(pool):
            def gather(j, r):
                wait_apart(pool, idx_ok, idx, j + 1)
                if not early(j, 1):
                    wait_apart(pool, idx_ok, gathered, j * SUB * 16)
                if not early(j, 2):
                    wait_apart(pool, idx_ok, t_full, j - 1)
                for n in range(SUB):
                    nc.gpsimd.indirect_dma_start(out=GX[:, r % 2, n, :], out_offset=None, in_=zrows,
                                                 in_offset=bass.IndirectOffsetOnAxis(ap=IS[:, r % 2, n:n + 1], axis=0))\
                        .then_inc(gathered, 16)

            def scatter(j, r):
                wait_apart(pool, idx_ok, tgt, j + 1)
                wait_apart(pool, idx_ok, y_out, j + 1)
                if not early(j, 1):
                    wait_apart(pool, idx_ok, scattered, j * SUB * 16)
                for n in range(SUB):
                    nc.gpsimd.indirect_dma_start(out=results, out_offset=bass.IndirectOffsetOnAxis(
                        ap=IT[:, r % 2, n:n + 1], axis=0), in_=YS[:, r % 2, n, :], in_offset=None,
                        bounds_check=2 * TOKENS - 1, oob_is_err=False).then_inc(scattered, 16)

            def step(k, r):
                if at(r, 0):
                    gather(k, r)
                if at(r, 4):
                    scatter(k - 4, r - 4)

            run(step, pool)

        @block.vector
        def _(dve):
            def indices(j, r):
                if not early(j, 2):
                    dve.wait_ge(gathered, (j - 1) * SUB * 16)
                nc.vector.tensor_copy(IS[:, r % 2, :], source[:, bass.ds(j * SUB, SUB)]).then_inc(idx, 1)

            def targets(j, r):
                if not early(j, 2):
                    dve.wait_ge(scattered, (j - 1) * SUB * 16)
                nc.vector.tensor_copy(IT[:, r % 2, :], target[:, bass.ds(j * SUB, SUB)]).then_inc(tgt, 1)

            def results_out(j, r):
                dve.wait_ge(y_full, j + 1)
                dve.wait_ge(w2_in, (j + 1) * 32)
                nc.vector.tensor_tensor(YS[:, r % 2, :, :], PY[r % 2][:, :].rearrange("p (n c) -> p n c", n=SUB),
                                        b2e[:, r % 2, :].unsqueeze(1).to_broadcast([P, SUB, C]), ALU.add).then_inc(y_out, 1)

            def step(k, r):
                if at(r, 0):
                    indices(k, r)
                if at(r, 3):
                    targets(k - 3, r - 3)
                    results_out(k - 3, r - 3)

            run(step, dve)
            for n in range(TILES // LOAD):
                dve.wait_ge(y_in, 32 * (n + 1))
                for i in range(LOAD):
                    tile = n * LOAD + i
                    for k in range(2):
                        if k:
                            dve.wait_ge(mixed, tile + 1)
                        nc.vector.scalar_tensor_tensor(out=X[:, tile, :], in0=Y[:, n % 2, k, i, :],
                                                       scalar=gates[:, k, tile:tile + 1], in1=X[:, tile, :],
                                                       op0=ALU.mult, op1=ALU.add).then_inc((mixed, added)[k], 1)

        @block.scalar
        def _(act):
            def turned(j, r):
                act.wait_ge(t_full, j + 1)
                if not early(j, 2):
                    act.wait_ge(h_full, (j - 1) * HT)
                nc.scalar.copy(GT_[:, r % 2, :], PT[:, :]).then_inc(t_out, 1)

            def gelus(j, r):
                act.wait_ge(w1_in, (j + 1) * 32)
                if not early(j, 2):
                    act.wait_ge(y_full, j - 1)
                for n in range(HT):
                    act.wait_ge(h_full, j * HT + (n + 1))
                    nc.scalar.activation(HG[:, r % 2, n, :], PH[n][:, :], ACT.Gelu, bias=b1e[:, r % 2, n:n + 1])\
                        .then_inc(h_out, 1)

            def step(k, r):
                if at(r, 1):
                    turned(k - 1, r - 1)
                if at(r, 2):
                    gelus(k - 2, r - 2)

            run(step, act)

        @block.tensor
        def _(pe):
            def turn(j, r):
                wait(pe, gathered, (j + 1) * SUB * 16)
                if not early(j, 1):
                    wait(pe, t_out, j)
                for n in range(SUB):
                    mm = nc.tensor.transpose(PT[:, n * P:(n + 1) * P], GX[:, r % 2, n, :], ident[:, :])
                mm.then_inc(t_full, 1)

            def first_product(j, r):
                wait(pe, t_out, j + 1)
                wait(pe, w1_in, (j + 1) * 32)
                for n in range(HT):
                    if not early(j, 1):
                        wait(pe, h_out, (j - 1) * HT + (n + 1))
                    nc.tensor.matmul(PH[n][:, :], W1e[:, r % 2, n * P:(n + 1) * P], GT_[:, r % 2, :], start=True, stop=True)\
                        .then_inc(h_full, 1)

            def second_product(j, r):
                wait(pe, h_out, (j + 1) * HT)
                wait(pe, w2_in, (j + 1) * 32)
                if not early(j, 2):
                    wait(pe, y_out, j - 1)
                for i in range(SUB):
                    for n in range(HT):
                        mm = nc.tensor.matmul(PY[r % 2][:, i * P:(i + 1) * P], HG[:, r % 2, n, i * P:(i + 1) * P],
                                              W2e[:, r % 2, n * P:(n + 1) * P], start=(n == 0), stop=(n == HT - 1))
                mm.then_inc(y_full, 1)

            def step(k, r):
                if at(r, 1):
                    turn(k - 1, r - 1)
                if at(r, 2):
                    first_product(k - 2, r - 2)
                if at(r, 3):
                    second_product(k - 3, r - 3)

            run(step, pe)


def network(nc, t, out):
    chip = Chip(nc)
    nc.disable_value_cache = True
    chosen = chip.dram("chosen", [N_BATCH, 1], U32)
    zrows = chip.dram("zrows", [TOKENS, C], F32)
    with ExitStack() as ctx:
        X = chip.sb(ctx, "X", [P, TILES, C], F32)
        ident = chip.sb(ctx, "ident", [P, P], F32)
        LG = chip.sb(ctx, "LG", [P, TILES, t["L1_ffn_router_w"].shape[0]], F32)
        id_zero, id_set = (chip.sem(ctx, n) for n in ("id_zero", "id_set"))
        with nc.Block() as block:
            @block.gpsimd
            def _(pool):
                nc.gpsimd.memset(ident[:, :], 0.0).then_inc(id_zero, 1)
                pool.wait_ge(id_zero, 1)
                nc.gpsimd.affine_select(out=ident[:, :], in_=ident[:, :], compare_op=ALU.not_equal, fill=1.0,
                                        base=0, pattern=[[-1, P]], channel_multiplier=1).then_inc(id_set, 1)
                pool.wait_ge(id_set, 1)
        chip.phase = "attn_"
        attention(nc, chip, X, ident, t["L0_attn_x"], t["L0_attn_qkv_w"], t["L0_attn_qkv_b"],
                  t["L0_attn_proj_w"], t["L0_attn_proj_b"])
        chip.phase = "choose_"
        choose_experts(nc, chip, X, ident, chosen, t["L0_ffn_Wp1"], t["L0_ffn_bp1"], t["L0_ffn_Wp2"], t["L0_ffn_bp2"])
        chip.phase = "mix_"
        mixers(nc, chip, X, ident, chosen, zrows, LG, t)
        E, H, _ = t["L1_ffn_w1"].shape
        NT = 2 * TOKENS // E_SLOTS + E - 1
        W1T, W2T = (chip.sb(ctx, n, [P, E, H], F32) for n in ("W1T", "W2T"))
        B1 = chip.sb(ctx, "B1", [P, E, H // P], F32)
        gates = chip.sb(ctx, "gates", [P, 2, TILES], F32)
        source, target = (chip.sb(ctx, n, [P, NT * SUB], U32) for n in ("source", "target"))
        owner = chip.sb(ctx, "owner", [1, NT], U32)
        chip.phase = "fold_"
        fold_weights(nc, chip, ident, W1T, W2T, B1, t)
        chip.phase = "route_"
        route(nc, chip, LG, gates, source, target, owner, NT)
        chip.phase = "moe_"
        routed_experts(nc, chip, X, ident, zrows, gates, source, target, owner, W1T, W2T, B1, t["L1_ffn_b2"], out, NT)


_OUT = ((32, 256, 128), "float32")


def kernel(**inputs):
    import numpy as _np
    import concourse.bacc as _bacc
    from concourse import mybir as _mybir
    from concourse.bass_utils import run_bass_kernel_spmd as _run

    nc = _bacc.Bacc("TRN2", target_bir_lowering=False, num_devices=1)
    arrays, args = {}, {}
    for name in sorted(inputs):
        a = _np.ascontiguousarray(inputs[name])
        arrays[f"in_{name}"] = a
        args[name] = nc.dram_tensor(f"in_{name}", a.shape, _mybir.dt.from_np(a.dtype), kind="ExternalInput").ap()
    out = nc.dram_tensor("out_0", _OUT[0], _mybir.dt.from_np(_np.dtype(_OUT[1])), kind="ExternalOutput").ap()
    network(nc, args, out)
    r = _run(nc, [arrays], core_ids=[0])
    return r.results[0]["out_0"]
```

```python
from contextlib import ExitStack

import concourse.bass as bass
from concourse import mybir
from concourse.alu_op_type import AluOpType as ALU

ACT = mybir.ActivationFunctionType
AX = mybir.AxisListType
F32 = mybir.dt.float32
BF16 = mybir.dt.bfloat16
I32 = mybir.dt.int32
U32 = mybir.dt.uint32

P = 128
N_BATCH, SEQ, C = 32, 256, 128
TOKENS = N_BATCH * SEQ
TPG = 4
GT = TPG * P
BPG = GT // SEQ
TPB = SEQ // P
GROUPS = TOKENS // GT
TILES = TOKENS // P

HEADS = 16
HD = C // HEADS
PAIRS = HEADS // 2
HALF = 64
UNITS = BPG * HEADS
MAXU = TPG * PAIRS
LEAD = MAXU - 12
QUAD = 4
QUADS = UNITS // QUAD
FILLS = QUADS // 2
PARTS = 3
RUNS = tuple(PARTS - n for n in range(PARTS))
K_ROWS = HD * sum(RUNS)
C_ROWS = 2
BUFS = 3
VW = P // QUAD
PRB = 8
SCB = 3

E_SLOTS = 256
SUB = E_SLOTS // P
CAP = TOKENS + E_SLOTS
ROW = C + 1
TOP = 2
SHARE = TPG * TOP
BIG = 3.0e38

LN_EPS = 1e-5
LN2_EPS = 1e-6
NEWTON = 3
ONE_PAIR = 1.0 + 0x3F80 / 2.0 ** 23
RSQRT_SEED = 1597463007.0


class Chip:

    def __init__(self, nc):
        self.nc = nc
        self.phase = ""

    def sb(self, ctx, name, shape, dt):
        return ctx.enter_context(self.nc.sbuf_tensor(self.phase + name, shape, dt))

    def ps(self, ctx, name, shape, dt=F32):
        return ctx.enter_context(self.nc.psum_tensor(self.phase + name, shape, dt))

    def sem(self, ctx, name):
        return ctx.enter_context(self.nc.semaphore(name))

    def dram(self, name, shape, dt):
        return self.nc.dram_tensor(name, shape, dt, kind="Internal").ap()


def rows(v):
    return bass.AP(tensor=v.tensor, offset=v.offset, ap=[[0, P]] + [list(x) for x in v.ap])


def column(v):
    return v.rearrange("(p a) -> p a", a=1)


def wait(eng, sem, count):
    if isinstance(count, int):
        eng.wait_ge(sem, count)
        return
    held = eng.to_reg(count)
    eng.wait_ge(sem, held)
    eng.free_register(held)


def wait_apart(eng, always, sem, count):
    if isinstance(count, int):
        eng.wait_ge(sem, count)
        return
    held = eng.to_reg(count)
    eng.wait_ge(always, 1)
    eng.wait_ge(sem, held)
    eng.free_register(held)


def newton_rsqrt(eng, always, sem, done, y, var, tmp):
    for n in range(NEWTON):
        eng.tensor_tensor(tmp[:, 2 * n], y[:, n], y[:, n], ALU.mult).then_inc(sem, 1)
        done += 1
        wait_apart(eng, always, sem, done)
        eng.tensor_tensor(tmp[:, 2 * n + 1], tmp[:, 2 * n], var, ALU.mult).then_inc(sem, 1)
        done += 1
        wait_apart(eng, always, sem, done)
        eng.tensor_scalar(tmp[:, 2 * n], tmp[:, 2 * n + 1], -0.5, 1.5, ALU.mult, ALU.add).then_inc(sem, 1)
        done += 1
        wait_apart(eng, always, sem, done)
        eng.tensor_tensor(y[:, n + 1], y[:, n], tmp[:, 2 * n], ALU.mult).then_inc(sem, 1)
        done += 1
        wait_apart(eng, always, sem, done)
    return done


NEWTON_OPS = 4 * NEWTON


def attention(nc, chip, X, ident, x_in, qkv_w, qkv_b, proj_w, proj_b):
    qscale = float(HD) ** -0.5
    with ExitStack() as ctx:
        def sb(name, shape, dt=F32):
            return chip.sb(ctx, name, shape, dt)

        Wqkv, Wproj = sb("Wqkv", [P, 3 * C]), sb("Wproj", [P, C])
        Wqk = sb("Wqk", [P, 2, C])
        qb, qbs, kb = sb("qb", [P, 1]), sb("qbs", [P, 1]), sb("kb", [P, 1])
        vb, pb = sb("vb", [P, C]), sb("pb", [P, C])
        QP, KP = sb("QP", [P, BUFS, 2, PAIRS, GT], BF16), sb("KP", [P, BUFS, PAIRS, GT], BF16)
        V = sb("V", [P, BUFS, TPG, HEADS, VW])
        Xs, XN = sb("Xs", [P, TPG, C]), sb("XN", [P, TPG, C])
        stat, mv = sb("stat", [P, TPG, 6]), sb("mv", [P, TPG, 2])
        var = sb("var", [P, TPG])
        ny, ntmp = sb("ny", [P, NEWTON + 1, TPG]), sb("ntmp", [P, 2 * NEWTON, TPG])
        XNT, OT = sb("XNT", [P, GT]), sb("OT", [P, GT])
        qf, kf, qr, kr = (sb(n, [P, GT]) for n in ("qf", "kf", "qr", "kr"))
        QS, KS = (sb(n, [P, PARTS, GT], BF16) for n in ("QS", "KS"))
        MX = sb("MX", [P, BUFS, TPG, HEADS])
        CM = sb("CM", [P, TPG, C_ROWS, HEADS])
        CB = sb("CB", [P, TPG, HEADS], BF16)
        CT = sb("CT", [C_ROWS * HEADS, GT], BF16)
        PR = sb("PR", [P, PRB, GT])
        PVS, REC = sb("PVS", [P, 2, GT]), sb("REC", [P, TPB, 2, QUAD])
        O = sb("O", [P, TPG, HEADS, HD])

        QD, KD = (chip.dram(n, [GROUPS, PARTS, 2, HD, PAIRS, GT], BF16) for n in ("q_parts", "k_parts"))
        CD = chip.dram("shift_rows", [GROUPS, C_ROWS, HEADS, GT], BF16)

        SC = [chip.ps(ctx, f"score{i}", [P, GT]) for i in range(SCB)]
        PM = [chip.ps(ctx, f"smax{i}", [P, GT]) for i in range(2)]
        PV = [chip.ps(ctx, f"pv{i}", [P, GT]) for i in range(2)]
        MB = chip.ps(ctx, "mb", [P, GT])

        def sem(name):
            return chip.sem(ctx, "a_" + name)

        weights_in, ones_set, kones_set, zeros_set, qbs_set, wqk_set = (
            sem(n) for n in ("weights_in", "ones", "kones", "zeros", "qbs", "wqk"))
        x_chunk = [sem(f"x_chunk{i}") for i in range(3)]
        xs_copied, stats, aggr, newton, xn_done, x_biased = (
            sem(n) for n in ("xs", "stats", "aggr", "newton", "xn", "xbias"))
        xnt_full, xnt_out, q_full, q_out, k_full, k_out, v_full, v_out = (
            sem(n) for n in ("xnt_full", "xnt_out", "q_full", "q_out", "k_full", "k_out", "v_full", "v_out"))
        splits, parts_ready, parts_stored, packed = (sem(n) for n in ("splits", "parts", "stored", "packed"))
        max_full, max_out, shift, ct_full, ct_out, ct_stored, shifted = (
            sem(n) for n in ("max_full", "max_out", "shift", "ct_full", "ct_out", "ct_stored", "shifted"))
        score_full, exp_out, pv_full, pv_out, pvt_full, recs, o_out = (
            sem(n) for n in ("score_full", "exp_out", "pv_full", "pv_out", "pvt_full", "recs", "o_out"))
        ot_full, ot_out, proj_full, x_added = (sem(n) for n in ("ot_full", "ot_out", "proj_full", "x_added"))

        N_PACK = 2 * 2 * PARTS
        X_CHUNKS = ((0, 1), (1, 3), (3, GROUPS))

        def tile_cols(t):
            return slice(t * P, (t + 1) * P)

        def run(steps, eng):
            steps(0, 0)
            n = (GROUPS - 3 - 1) // BUFS
            with eng.Fori(0, n) as i:
                for r in range(BUFS):
                    steps(i * BUFS + (1 + r), 1 + r)
            for g in range(1 + n * BUFS, GROUPS):
                steps(g, g)

        def last(r, ahead):
            return r + ahead >= GROUPS

        block = ctx.enter_context(nc.Block())

        @block.sync
        def _(sp):
            xv = x_in.rearrange("b (t p) c -> p (b t) c", p=P)

            def load_x(n):
                a, b = X_CHUNKS[n]
                sp.dma_start(X[:, a * TPG:b * TPG, :], xv[:, a * TPG:b * TPG, :]).then_inc(x_chunk[n], 16)

            load_x(0)
            for dst, src in ((Wqkv[:, :], qkv_w), (Wproj[:, :], proj_w), (vb[:, :], rows(qkv_b[2 * C:3 * C])),
                             (pb[:, :], rows(proj_b))):
                sp.dma_start(dst, src).then_inc(weights_in, 16)
            for n, dst in enumerate((qb, kb)):
                for half in range(2):
                    src = qkv_b[n * C:(n + 1) * C].rearrange("(j i d a) -> i d j a", i=2, d=HD, a=1)[half]
                    sp.dma_start(dst[half * HALF:(half + 1) * HALF, :], src, allow_slow_non_contiguous=True).then_inc(weights_in, 16)
            load_x(1)
            load_x(2)

            def store(g):
                sp.wait_ge(parts_ready, (g + 1) * 2)
                for part, d in ((QS, QD), (KS, KD)):
                    sp.dma_start(d[bass.ds(g, 1)].rearrange("g s i d j t -> (i d j) (g s) t"), part[:, :, :])\
                        .then_inc(parts_stored, 16)

            def pack(g, buf):
                sp.wait_ge(parts_stored, (g + 1) * 32)
                for half in range(2):
                    at = HALF * half
                    for n, run_ in enumerate(RUNS):
                        q_parts = QD[bass.ds(g, 1), 0:run_, half].rearrange("g s d j t -> (g s) d (j t)")
                        k_part = KD[bass.ds(g, 1), n, half].rearrange("g d j t -> g d (j t)")\
                            .to_broadcast([run_, HD, PAIRS * GT])
                        sp.dma_start(QP[at:at + HD * run_, buf, half].rearrange("p j t -> p (j t)"), q_parts)\
                            .then_inc(packed, 16)
                        sp.dma_start(KP[at:at + HD * run_, buf].rearrange("p j t -> p (j t)"), k_part)\
                            .then_inc(packed, 16)
                        at += HD * run_

            def shift_out(g):
                sp.wait_ge(ct_out, g + 1)
                sp.dma_start(CD[bass.ds(g, 1)].rearrange("g r h t -> (g r h) t"), CT[:, :]).then_inc(ct_stored, 16)

            def shift_in(g, buf):
                sp.wait_ge(ct_stored, (g + 1) * 16)
                for half in range(2):
                    src = CD[bass.ds(g, 1)].rearrange("g r (j i) t -> i (g r) j t", i=2)[half]
                    at = HALF * half + K_ROWS
                    sp.dma_start(QP[at:at + C_ROWS, buf, half], src).then_inc(shifted, 16)

            for g in range(2):
                store(g)
                sp.wait_ge(kones_set, g + 1)
                sp.wait_ge(zeros_set, g + 1)
                pack(g, g)
                if g == 1:
                    shift_out(0)
                sp.wait_ge(packed, (g + 1) * 16 * N_PACK)
            shift_in(0, 0)
            store(2)
            sp.wait_ge(kones_set, BUFS)
            sp.wait_ge(zeros_set, BUFS)

            def step(g, r):
                if not last(r, 2):
                    wait_apart(sp, kones_set, score_full, g * UNITS)
                    pack(g + 2, (r + 2) % BUFS)
                    sp.wait_ge(packed, (g + 3) * (16 * N_PACK))
                if not last(r, 1):
                    shift_out(g + 1)
                    shift_in(g + 1, (r + 1) % BUFS)
                if not last(r, 3):
                    store(g + 3)
                if not last(r, 1):
                    wait_apart(sp, kones_set, shifted, (g + 2) * 32)

            run(step, sp)

        @block.gpsimd
        def _(pool):
            nc.gpsimd.memset(V[:, :, :, :, HD:VW], 1.0).then_inc(ones_set, 1)

            def norm(g, chunk=None):
                if chunk is not None:
                    wait_apart(pool, ones_set, x_chunk[chunk], 16)
                if not (isinstance(g, int) and g == 0):
                    wait_apart(pool, ones_set, xn_done, g * TPG)
                nc.gpsimd.tensor_copy(Xs[:, :, :], X[:, bass.ds(g * TPG, TPG), :]).then_inc(xs_copied, 1)
                wait_apart(pool, ones_set, xs_copied, g + 1)
                nc.gpsimd.tensor_tensor(X[:, bass.ds(g * TPG, TPG), :], Xs[:, :, :],
                                        pb[:, :].unsqueeze(1).to_broadcast([P, TPG, C]), ALU.add).then_inc(x_biased, 1)
                wait_apart(pool, ones_set, aggr, (g + 1) * TPG)
                base = g * (NEWTON_OPS + 2)
                nc.gpsimd.tensor_scalar(var[:, :], mv[:, :, 1], LN_EPS, None, ALU.add).then_inc(newton, 1)
                wait_apart(pool, ones_set, newton, base + 1)
                nc.gpsimd.tensor_scalar(ny[:, 0, :].bitcast(I32), var[:, :].bitcast(I32), -0.5, RSQRT_SEED,
                                        ALU.mult, ALU.add).then_inc(newton, 1)
                wait_apart(pool, ones_set, newton, base + 2)
                newton_rsqrt(nc.gpsimd, ones_set, newton, base + 2, ny, var[:, :], ntmp)

            def split(g):
                for n, (full, f, rem, part) in enumerate(((q_out, qf, qr, QS), (k_out, kf, kr, KS))):
                    base = g * 4 + 2 * n
                    wait_apart(pool, ones_set, full, (g + 1) * 2)
                    nc.gpsimd.tensor_tensor(rem[:, :], f[:, :], part[:, 0, :], ALU.subtract).then_inc(splits, 1)
                    wait_apart(pool, ones_set, splits, base + 1)
                    nc.gpsimd.tensor_copy(part[:, 1, :], rem[:, :]).then_inc(splits, 1)
                    wait_apart(pool, ones_set, splits, base + 2)
                    nc.gpsimd.tensor_tensor(part[:, 2, :], rem[:, :], part[:, 1, :], ALU.subtract)\
                        .then_inc(parts_ready, 1)

            def split_max(g, buf):
                wait_apart(pool, ones_set, max_out, (g + 1) * MAXU)
                wait_apart(pool, ones_set, ct_full, g)
                nc.gpsimd.tensor_scalar(CB[:, :, :], MX[:, buf, :, :], -1.0, None, ALU.mult).then_inc(shift, 1)
                wait_apart(pool, ones_set, shift, g * 4 + 1)
                nc.gpsimd.tensor_scalar(CM[:, :, 0, :], CB[:, :, :], 1.0, None, ALU.mult).then_inc(shift, 1)
                wait_apart(pool, ones_set, shift, g * 4 + 2)
                nc.gpsimd.tensor_tensor(CM[:, :, 1, :], MX[:, buf, :, :], CM[:, :, 0, :], ALU.add).then_inc(shift, 1)
                wait_apart(pool, ones_set, shift, g * 4 + 3)
                nc.gpsimd.tensor_scalar(CM[:, :, 1, :], CM[:, :, 1, :], -1.0, None, ALU.mult).then_inc(shift, 1)

            pool.wait_ge(ones_set, 1)
            pool.wait_ge(weights_in, 128)
            norm(0, 0)
            for buf in range(BUFS):
                nc.gpsimd.memset(KP[:, buf].rearrange("p j t -> p (j t)").bitcast(F32), ONE_PAIR).then_inc(kones_set, 1)
            split(0)
            norm(1, 1)
            split(1)
            norm(2, 1)
            split_max(0, 0)
            split(2)

            def step(g, r):
                if not last(r, 3):
                    norm(g + 3, 2 if r == 0 else None)
                if not last(r, 1):
                    split_max(g + 1, (r + 1) % BUFS)
                if not last(r, 3):
                    split(g + 3)

            run(step, pool)

        @block.scalar
        def _(act):
            act.wait_ge(weights_in, 128)
            nc.scalar.mul(qbs[:, :], qb[:, :], qscale).then_inc(qbs_set, 1)
            act.wait_ge(qbs_set, 1)
            for n in range(2):
                nc.scalar.copy(Wqk[:, n, :].rearrange("p (i d j) -> p i d j", i=2, d=HD),
                               Wqkv[:, n * C:(n + 1) * C].rearrange("p (j i d) -> p i d j", i=2, d=HD))\
                    .then_inc(wqk_set, 1)

            def xnt(g):
                act.wait_ge(xnt_full, g + 1)
                act.wait_ge(v_full, g)
                nc.scalar.copy(XNT[:, :], MB[:, :]).then_inc(xnt_out, 1)

            def q_k(g, full, f, part, out, bias, scale):
                act.wait_ge(full, g + 1)
                act.wait_ge(parts_ready, g * 2)
                nc.scalar.activation(f[:, :], MB[:, :], ACT.Identity, bias=bias[:, 0:1], scale=scale).then_inc(out, 1)
                act.wait_ge(parts_stored, g * 32)
                nc.scalar.activation(part[:, 0, :], MB[:, :], ACT.Identity, bias=bias[:, 0:1], scale=scale)\
                    .then_inc(out, 1)

            def q(g):
                q_k(g, q_full, qf, QS, q_out, qbs, qscale)

            def k(g):
                q_k(g, k_full, kf, KS, k_out, kb, 1.0)

            def ct(g):
                act.wait_ge(ct_full, g + 1)
                act.wait_ge(ct_stored, g * 16)
                nc.scalar.copy(CT[:, :], MB[0:C_ROWS * HEADS, :]).then_inc(ct_out, 1)

            def ot(g):
                act.wait_ge(ot_full, g + 1)
                act.wait_ge(proj_full, g)
                nc.scalar.copy(OT[:, :], MB[:, :]).then_inc(ot_out, 1)

            def exps(g, u, r):
                act.wait_ge(score_full, g * UNITS + (u + 1))
                if u % QUAD == 0 and not (isinstance(g, int) and g * UNITS + u < PRB):
                    act.wait_ge(pv_full, g * QUADS + ((u - PRB) // QUAD + 1))
                nc.scalar.activation(PR[:, u % PRB, :], SC[(r * UNITS + u) % SCB][:, :], ACT.Exp).then_inc(exp_out, 1)

            def sums(g, f):
                act.wait_ge(pv_full, g * QUADS + 2 * (f + 1))
                if not (isinstance(g, int) and g * FILLS + f < 2):
                    act.wait_ge(pvt_full, g * FILLS + (f - 1))
                nc.scalar.copy(PVS[:, f % 2, :], PV[f % 2][:, :]).then_inc(pv_out, 1)

            for g in range(3):
                xnt(g)
                q(g)
                k(g)
                if g == 1:
                    ct(0)

            def step(g, r):
                for u in range(UNITS):
                    exps(g, u, r)
                    if u == 3 and r > 0:
                        sums(g - 1, FILLS - 1)
                    if u in (11, 19, 27):
                        sums(g, (u - 11) // 8)
                    if u == 9 and r > 0:
                        ot(g - 1)
                    if not last(r, 3):
                        if u == 16:
                            xnt(g + 3)
                        if u == 18:
                            q(g + 3)
                        if u == 21:
                            k(g + 3)
                    if u == 23 and not last(r, 1):
                        ct(g + 1)

            run(step, act)
            sums(GROUPS - 1, FILLS - 1)
            ot(GROUPS - 1)

        @block.vector
        def _(dve):
            nc.vector.memset(QP[:, 0].rearrange("p i j t -> p (i j t)").bitcast(F32), 0.0).then_inc(zeros_set, 1)

            def norm_stats(g, t):
                if t == 0:
                    dve.wait_ge(xs_copied, g + 1)
                    dve.wait_ge(xn_done, g * TPG)
                nc.vector.bn_stats(stat[:, t, :], Xs[:, t, :]).then_inc(stats, 1)
                wait_apart(dve, ones_set, stats, g * TPG + (t + 1))
                nc.vector.bn_aggr(mv[:, t, :], stat[:, t, :]).then_inc(aggr, 1)

            def normed(g):
                dve.wait_ge(newton, (g + 1) * (NEWTON_OPS + 2))
                if not (isinstance(g, int) and g == 0):
                    dve.wait_ge(xnt_full, g)
                for t in range(TPG):
                    nc.vector.tensor_scalar(XN[:, t, :], Xs[:, t, :], mv[:, t, 0:1], ny[:, NEWTON, t:t + 1],
                                            ALU.subtract, ALU.mult).then_inc(xn_done, 1)

            def values(g, buf):
                if not (isinstance(g, int) and g < BUFS):
                    dve.wait_ge(pv_full, (g - BUFS + 1) * QUADS)
                dve.wait_ge(v_full, g + 1)
                nc.vector.tensor_tensor(
                    V[:, buf, :, :, 0:HD], MB[:, :].rearrange("p (t h d) -> p t h d", t=TPG, h=HEADS),
                    vb[:, :].rearrange("p (h d) -> p h d", h=HEADS).unsqueeze(1).to_broadcast([P, TPG, HEADS, HD]),
                    ALU.add).then_inc(v_out, 1)

            def row_max(g, w, buf):
                t, j = divmod(w, PAIRS)
                dve.wait_ge(max_full, g * MAXU + (w + 1))
                if w == 0 and not (isinstance(g, int) and g < BUFS):
                    dve.wait_ge(shift, (g - BUFS + 1) * 4)
                nc.vector.tensor_reduce(MX[:, buf, t, 2 * j:2 * j + 2], PM[w % 2][:, :].rearrange("p (h m) -> p h m", h=2),
                                        AX.X, ALU.max).then_inc(max_out, 1)

            def heads(g, f):
                b, half = divmod(f, 2)
                sums = MB[:, :].rearrange("p (n q c w) -> p n q c w", n=TPB, q=2, c=QUAD)
                dve.wait_ge(pvt_full, g * FILLS + (f + 1))
                nc.vector.reciprocal(REC[:, :, :, :], sums[:, :, :, :, HD]).then_inc(recs, 1)
                if f == 0 and not (isinstance(g, int) and g == 0):
                    dve.wait_ge(ot_full, g)
                dve.wait_ge(recs, g * FILLS + (f + 1))
                for n in range(TPB):
                    nc.vector.tensor_tensor(
                        O[:, b * TPB + n, 2 * QUAD * half:2 * QUAD * (half + 1), :].rearrange("p (q c) d -> p q c d", q=2),
                        sums[:, n, :, :, 0:HD], REC[:, n, :, :].unsqueeze(3).to_broadcast([P, 2, QUAD, HD]),
                        ALU.mult).then_inc(o_out, 1)

            def residual(g):
                dve.wait_ge(proj_full, g + 1)
                xg = X[:, bass.ds(g * TPG, TPG), :]
                nc.vector.tensor_tensor(xg, xg, MB[:, :].rearrange("p (t c) -> p t c", t=TPG), ALU.add)\
                    .then_inc(x_added, 1)

            dve.wait_ge(weights_in, 128)
            dve.wait_ge(ones_set, 1)
            for t in range(TPG):
                norm_stats(0, t)
            normed(0)
            for buf in range(1, BUFS):
                nc.vector.memset(QP[:, buf].rearrange("p i j t -> p (i j t)").bitcast(F32), 0.0).then_inc(zeros_set, 1)
            values(0, 0)
            for t in range(TPG):
                norm_stats(1, t)
            normed(1)
            for w in range(MAXU):
                row_max(0, w, 0)
                if w == 14:
                    values(1, 1)
                if w == 24:
                    for t in range(TPG):
                        norm_stats(2, t)
            normed(2)
            for w in range(LEAD):
                row_max(1, w, 1)

            def step(g, r):
                for u in range(UNITS):
                    if u < MAXU - LEAD:
                        if not last(r, 1):
                            row_max(g + 1, u + LEAD, (r + 1) % BUFS)
                    elif not last(r, 2):
                        row_max(g + 2, u + LEAD - MAXU, (r + 2) % BUFS)
                    if u == 3 and not last(r, 2):
                        values(g + 2, (r + 2) % BUFS)
                    if u in (0, 1, 2, 4) and not last(r, 3):
                        norm_stats(g + 3, (0, 1, 2, 4).index(u))
                    if u == 10 and not last(r, 3):
                        normed(g + 3)
                    if u == 5 and r > 0:
                        heads(g - 1, FILLS - 1)
                    if u == 11 and r > 0:
                        residual(g - 1)
                    if u in (14, 25, 29):
                        heads(g, (14, 25, 29).index(u))

            run(step, dve)
            heads(GROUPS - 1, FILLS - 1)
            residual(GROUPS - 1)

        @block.tensor
        def _(pe):
            def xnt(g, free, count):
                wait(pe, xn_done, (g + 1) * TPG)
                if free is not None:
                    wait(pe, free, count)
                for t in range(TPG):
                    mm = nc.tensor.transpose(MB[:, tile_cols(t)], XN[:, t, :], ident[:, :])
                mm.then_inc(xnt_full, 1)

            def q(g):
                wait(pe, xnt_out, g + 1)
                nc.tensor.matmul(MB[:, :], Wqk[:, 0, :], XNT[:, :], start=True, stop=True).then_inc(q_full, 1)

            def k(g, free, count):
                wait(pe, free, count)
                nc.tensor.matmul(MB[:, :], Wqk[:, 1, :], XNT[:, :], start=True, stop=True).then_inc(k_full, 1)

            def v(g, free, count):
                wait(pe, free, count)
                for t in range(TPG):
                    mm = nc.tensor.matmul(MB[:, tile_cols(t)], XNT[:, tile_cols(t)], Wqkv[:, 2 * C:3 * C],
                                          start=True, stop=True)
                mm.then_inc(v_full, 1)

            def max_scores(g, w, buf):
                t, j = divmod(w, PAIRS)
                b = t // TPB
                if w == 0:
                    wait(pe, packed, (g + 1) * (16 * N_PACK))
                if not (isinstance(g, int) and g * MAXU + w < 2):
                    wait(pe, max_out, g * MAXU + (w - 1))
                for i in range(2):
                    mm = nc.tensor.matmul(PM[w % 2][:, i * SEQ:(i + 1) * SEQ], QP[:, buf, i, j, tile_cols(t)],
                                          KP[:, buf, j, b * SEQ:(b + 1) * SEQ], start=True, stop=True)
                mm.then_inc(max_full, 1)

            def scores(g, u, r):
                b, h = divmod(u, HEADS)
                buf = r % BUFS
                if u == 0:
                    wait(pe, shifted, (g + 1) * 32)
                if not (isinstance(g, int) and g * UNITS + u < SCB):
                    wait(pe, exp_out, g * UNITS + (u + 1 - SCB))
                for m in range(TPB):
                    mm = nc.tensor.matmul(SC[(r * UNITS + u) % SCB][:, m * SEQ:(m + 1) * SEQ],
                                          KP[:, buf, h // 2, tile_cols(b * TPB + m)],
                                          QP[:, buf, h % 2, h // 2, b * SEQ:(b + 1) * SEQ], start=True, stop=True)
                mm.then_inc(score_full, 1)

            def pv(g, n, buf):
                b, q = divmod(n, QUADS // BPG)
                wait(pe, exp_out, g * UNITS + (n + 1) * QUAD)
                if n == 0:
                    wait(pe, v_out, g + 1)
                if n % 2 == 0 and not (isinstance(g, int) and g * FILLS + n // 2 < 2):
                    wait(pe, pv_out, g * FILLS + (n // 2 - 1))
                for m in range(TPB):
                    for c in range(QUAD):
                        mm = nc.tensor.matmul(
                            PV[n // 2 % 2][c * VW:(c + 1) * VW, n % 2 * SEQ:(n % 2 + 1) * SEQ],
                            V[:, buf, b * TPB + m, q * QUAD + c, :],
                            PR[:, (n * QUAD + c) % PRB, m * SEQ:(m + 1) * SEQ],
                            start=(m == 0), stop=(m == TPB - 1), tile_position=(0, c * VW), skip_group_check=True)
                mm.then_inc(pv_full, 1)

            def pvt(g, f, free, count):
                wait(pe, pv_out, g * FILLS + (f + 1))
                wait(pe, free, count)
                for n in range(TPB):
                    for q in range(2):
                        mm = nc.tensor.transpose(MB[:, tile_cols(2 * n + q)],
                                                 PVS[:, f % 2, q * SEQ + n * P:q * SEQ + (n + 1) * P], ident[:, :])
                mm.then_inc(pvt_full, 1)

            def ct(g, free, count):
                wait(pe, shift, (g + 1) * 4)
                wait(pe, free, count)
                for t in range(TPG):
                    mm = nc.tensor.transpose(MB[0:C_ROWS * HEADS, tile_cols(t)],
                                             CM[:, t, :, :].rearrange("p r h -> p (r h)"), ident[:, :])
                mm.then_inc(ct_full, 1)

            def ot(g, free, count):
                wait(pe, o_out, (g + 1) * TPB * FILLS)
                wait(pe, free, count)
                for t in range(TPG):
                    mm = nc.tensor.transpose(MB[:, tile_cols(t)], O[:, t, :, :].rearrange("p h d -> p (h d)"),
                                             ident[:, :])
                mm.then_inc(ot_full, 1)

            def proj(g):
                wait(pe, ot_out, g + 1)
                for t in range(TPG):
                    mm = nc.tensor.matmul(MB[:, tile_cols(t)], OT[:, tile_cols(t)], Wproj[:, :], start=True, stop=True)
                mm.then_inc(proj_full, 1)

            wait(pe, weights_in, 128)
            wait(pe, wqk_set, 2)
            xnt(0, None, 0)
            q(0)
            k(0, q_out, 2)
            v(0, k_out, 2)
            xnt(1, v_out, 1)
            for w in range(MAXU):
                max_scores(0, w, 0)
                if w == 3:
                    q(1)
                if w == 7:
                    k(1, q_out, 4)
                if w == 11:
                    v(1, k_out, 4)
            ct(0, v_out, 2)
            for w in range(LEAD):
                max_scores(1, w, 1)
                if w == 0:
                    xnt(2, ct_out, 1)
                if w == 3:
                    q(2)
                if w == 7:
                    k(2, q_out, 6)

            def step(g, r):
                n_o = TPB * FILLS
                for u in range(UNITS):
                    scores(g, u, r)
                    if u == 2 and r > 0:
                        pv(g - 1, QUADS - 1, (r - 1) % BUFS)
                    if u % QUAD == 2 and u > QUAD:
                        pv(g, u // QUAD - 1, r % BUFS)
                    if u < MAXU - LEAD:
                        if not last(r, 1):
                            max_scores(g + 1, u + LEAD, (r + 1) % BUFS)
                    elif not last(r, 2):
                        max_scores(g + 2, u + LEAD - MAXU, (r + 2) % BUFS)
                    if u == 1 and not last(r, 2):
                        if r > 0:
                            v(g + 2, o_out, (g - 1) * n_o + 3 * TPB)
                        else:
                            v(g + 2, k_out, 6)
                    if u == 5 and r > 0:
                        pvt(g - 1, FILLS - 1, *((v_out, g + 3) if not last(r, 2) else (o_out, (g - 1) * n_o + 3 * TPB)))
                    if u == 8 and r > 0:
                        ot(g - 1, o_out, g * n_o)
                    if u == 11 and r > 0:
                        proj(g - 1)
                    if u == 13:
                        pvt(g, 0, *((x_added, g) if r > 0 else (v_out, 3)))
                    if u == 16 and not last(r, 3):
                        xnt(g + 3, o_out, g * n_o + TPB)
                    if u == 18 and not last(r, 3):
                        q(g + 3)
                    if u == 21 and not last(r, 3):
                        k(g + 3, q_out, 2 * (g + 4))
                    if u == 23 and not last(r, 1):
                        ct(g + 1, *((k_out, 2 * (g + 4)) if not last(r, 3) else (o_out, g * n_o + TPB)))
                    if u == 25:
                        pvt(g, 1, *((ct_out, g + 2) if not last(r, 1) else (o_out, g * n_o + TPB)))
                    if u == 29:
                        pvt(g, 2, o_out, g * n_o + 2 * TPB)

            run(step, pe)
            g = GROUPS - 1
            pv(g, QUADS - 1, g % BUFS)
            pvt(g, FILLS - 1, o_out, TPB * (FILLS * g + 3))
            ot(g, o_out, TPB * FILLS * GROUPS)
            proj(g)


def prepare(nc, chip, X, ident, chosen, W1T, W2T, B1, t):
    Wp1d, bp1, Wp2d, bp2 = t["L0_ffn_Wp1"], t["L0_ffn_bp1"], t["L0_ffn_Wp2"], t["L0_ffn_bp2"]
    EB = Wp2d.shape[1]
    E, H, D = t["L1_ffn_w1"].shape
    HT = H // P
    with ExitStack() as ctx:
        def sb(name, shape, dt=F32):
            return chip.sb(ctx, name, shape, dt)

        Wp1, Wp2, b1c, b2r = sb("Wp1", [C, C]), sb("Wp2", [C, EB]), sb("bp1c", [C, 1]), sb("bp2r", [P, EB])
        L, LN = sb("L", [N_BATCH, C]), sb("LN", [N_BATCH, C])
        LT, NT = sb("LT", [C, N_BATCH]), sb("NT", [C, N_BATCH])
        stat, mv, var = sb("nstat", [N_BATCH, 6]), sb("nmv", [N_BATCH, 2]), sb("nvar", [N_BATCH, 1])
        ny, ntmp = sb("nny", [N_BATCH, NEWTON + 1, 1]), sb("nntmp", [N_BATCH, 2 * NEWTON, 1])
        logits, best, index = sb("logits", [N_BATCH, EB]), sb("best", [N_BATCH, 8]), sb("index", [N_BATCH, 8], U32)
        last_rows = chip.dram("last_rows", [N_BATCH, C], F32)
        PT, PN = (chip.ps(ctx, n, [P, GT]) for n in ("npt", "npn"))
        (w_in, rows_out, rows_in, chain, newton, t_full, t_out, n_full, n_out, l_full, found, stored) = (
            chip.sem(ctx, "n_" + n) for n in ("w_in rows_out rows_in chain newton t_full t_out n_full n_out l_full "
                                              "found stored").split())
        R1, R2 = sb("R1", [P, E, HT, D]), sb("R2", [P, E, H])
        lrow, brow = sb("lrow", [E, 2, D]), sb("b1row", [E, H])
        lcol = sb("lcol", [P, 2, E])
        PA, PB = ([chip.ps(ctx, f"f{n}{i}", [P, H]) for i in range(2)] for n in "ab")
        PC, PD = chip.ps(ctx, "fc", [P, GT]), chip.ps(ctx, "fd", [P, GT])
        (e_in, c_full, c_out, a_full, a_out, a_scaled, b_full, b_out, bias_full, bias_out) = (
            chip.sem(ctx, "f_" + n) for n in "e_in c_full c_out a_full a_out a_scaled b_full b_out bias_full bias_out".split())
        expert_in = [chip.sem(ctx, f"f_expert_in{e}") for e in range(E)]
        block = ctx.enter_context(nc.Block())

        @block.sync
        def _(sp):
            for dst, src in ((Wp1[:, :], Wp1d), (Wp2[:, :], Wp2d), (b1c[:, :], column(bp1)), (b2r[:, :], rows(bp2))):
                sp.dma_start(dst, src).then_inc(w_in, 16)
            sp.dma_start(last_rows.rearrange("(a b) c -> a b c", a=1), X[P - 1:P, TPB - 1::TPB, :]).then_inc(rows_out, 16)
            sp.wait_ge(rows_out, 16)
            sp.dma_start(L[:, :], last_rows).then_inc(rows_in, 16)
            for dst, src in ((lrow[:, 0, :], t["L1_ffn_expert_ln_scale"]), (lrow[:, 1, :], t["L1_ffn_expert_ln_bias"]),
                             (brow[:, :], t["L1_ffn_b1"])):
                sp.dma_start(dst, src).then_inc(e_in, 16)
            for e in range(E):
                sp.dma_start(R1[:, e, :, :], t["L1_ffn_w1"][e].rearrange("(n p) d -> p n d", p=P)).then_inc(expert_in[e], 16)
                sp.dma_start(R2[:, e, :], t["L1_ffn_w2"][e]).then_inc(expert_in[e], 16)
            sp.wait_ge(found, 1)
            sp.dma_start(chosen, index[:, 0:1]).then_inc(stored, 16)
            sp.wait_ge(stored, 16)

        @block.vector
        def _(dve):
            dve.wait_ge(w_in, 64)
            dve.wait_ge(rows_in, 16)
            nc.vector.bn_stats(stat[:, :], L[:, :]).then_inc(chain, 1)
            dve.wait_ge(chain, 1)
            nc.vector.bn_aggr(mv[:, :], stat[:, :]).then_inc(chain, 1)
            dve.wait_ge(chain, 2)
            nc.vector.tensor_scalar(var[:, :], mv[:, 1:2], LN_EPS, None, ALU.add).then_inc(chain, 1)
            dve.wait_ge(chain, 3)
            nc.vector.tensor_scalar(ny[:, 0, :].bitcast(I32), var[:, :].bitcast(I32), -0.5, RSQRT_SEED,
                                    ALU.mult, ALU.add).then_inc(newton, 1)
            dve.wait_ge(newton, 1)
            newton_rsqrt(nc.vector, w_in, newton, 1, ny, var[:, :], ntmp)
            nc.vector.tensor_scalar(LN[:, :], L[:, :], mv[:, 0:1], ny[:, NEWTON, 0:1], ALU.subtract, ALU.mult)\
                .then_inc(chain, 1)
            dve.wait_ge(t_full, 1)
            nc.vector.tensor_copy(LT[:, :], PT[:, 0:N_BATCH]).then_inc(t_out, 1)
            dve.wait_ge(l_full, 1)
            nc.vector.tensor_tensor(logits[:, :], PT[0:N_BATCH, 0:EB], b2r[0:N_BATCH, :], ALU.add).then_inc(chain, 1)
            dve.wait_ge(chain, 5)
            nc.vector.max(best[:, :], logits[:, :]).then_inc(chain, 1)
            dve.wait_ge(chain, 6)
            nc.vector.max_index(index[:, :], best[:, :], logits[:, :]).then_inc(found, 1)

            dve.wait_ge(c_full, 1)
            nc.vector.tensor_copy(lcol[:, :, :], PC[:, 0:2 * E].rearrange("p (n e) -> p n e", n=2)).then_inc(c_out, 1)
            nc.vector.tensor_copy(B1[:, :, :].rearrange("p e n -> p n e"),
                                  PC[:, 2 * E:(2 + HT) * E].rearrange("p (n e) -> p n e", n=HT)).then_inc(c_out, 1)
            for e in range(E):
                dve.wait_ge(a_full, e + 1)
                nc.vector.tensor_copy(W1T[:, e, :], PA[e % 2][:, :]).then_inc(a_out, 1)
            dve.wait_ge(bias_full, E)
            dve.wait_ge(c_out, 2)
            nc.vector.tensor_tensor(B1[:, :, :], B1[:, :, :], PD[:, 0:E * HT].rearrange("p (e n) -> p e n", e=E), ALU.add)\
                .then_inc(bias_out, 1)
            dve.wait_ge(a_out, E)
            for e in range(E):
                nc.vector.tensor_scalar(W1T[:, e, :], W1T[:, e, :], lcol[:, 0, e:e + 1], None, ALU.mult)\
                    .then_inc(a_scaled, 1)

        @block.scalar
        def _(act):
            act.wait_ge(w_in, 64)
            act.wait_ge(n_full, 1)
            nc.scalar.activation(NT[:, :], PN[:, 0:N_BATCH], ACT.Gelu, bias=b1c[:, 0:1]).then_inc(n_out, 1)
            for e in range(E):
                act.wait_ge(b_full, e + 1)
                nc.scalar.copy(W2T[:, e, :], PB[e % 2][:, :]).then_inc(b_out, 1)

        @block.tensor
        def _(pe):
            pe.wait_ge(w_in, 64)
            pe.wait_ge(chain, 4)
            nc.tensor.transpose(PT[:, 0:N_BATCH], LN[:, :], ident[0:N_BATCH, 0:N_BATCH]).then_inc(t_full, 1)
            pe.wait_ge(t_out, 1)
            nc.tensor.matmul(PN[:, 0:N_BATCH], Wp1[:, :], LT[:, :], start=True, stop=True).then_inc(n_full, 1)
            pe.wait_ge(n_out, 1)
            nc.tensor.matmul(PT[0:N_BATCH, 0:EB], NT[:, :], Wp2[:, :], start=True, stop=True).then_inc(l_full, 1)

            pe.wait_ge(e_in, 48)
            for n in range(2):
                nc.tensor.transpose(PC[:, n * E:(n + 1) * E], lrow[:, n, :], ident[0:E, 0:E])
            for n in range(HT):
                mm = nc.tensor.transpose(PC[:, (2 + n) * E:(3 + n) * E], brow[:, n * P:(n + 1) * P], ident[0:E, 0:E])
            mm.then_inc(c_full, 1)
            def bias(e):
                pe.wait_ge(a_out, e + 1)
                for n in range(HT):
                    mm = nc.tensor.matmul(PD[:, e * HT + n:e * HT + n + 1], W1T[:, e, n * P:(n + 1) * P],
                                          lcol[:, 1, e:e + 1], start=True, stop=True)
                mm.then_inc(bias_full, 1)

            for e in range(E):
                pe.wait_ge(expert_in[e], 32)
                if e >= 2:
                    pe.wait_ge(b_out, e - 1)
                for n in range(HT):
                    mm = nc.tensor.transpose(PA[e % 2][:, n * P:(n + 1) * P], R1[:, e, n, :], ident[:, :])
                mm.then_inc(a_full, 1)
                for n in range(HT):
                    mm = nc.tensor.transpose(PB[e % 2][:, n * P:(n + 1) * P], R2[:, e, n * P:(n + 1) * P], ident[:, :])
                mm.then_inc(b_full, 1)
                if e == 0:
                    pe.wait_ge(c_out, 1)
                else:
                    bias(e - 1)
            bias(E - 1)


def mixers(nc, chip, X, ident, chosen, sorted_rows, next_rows, second_less_first, t):
    E, _, F = t["L0_ffn_W1"].shape
    FT = F // P
    NB = FT + 1
    ER = t["L1_ffn_router_w"].shape[0]
    LAST = 6
    with ExitStack() as ctx:
        def sb(name, shape, dt=F32):
            return chip.sb(ctx, name, shape, dt)

        W1e, W2e = sb("W1e", [P, 2, BPG, F]), sb("W2e", [P, 2, BPG, FT, C])
        biases, Be = sb("biases", [P, E, NB]), sb("Be", [P, 2, BPG, NB])
        brow = sb("brow", [E, NB, P])
        sel = sb("sel", [1, N_BATCH], U32)
        Wo, bo, one_row = sb("Wo", [P, C]), sb("bo", [1, C]), sb("one_row", [1, P])
        Wraw, WT = sb("Wraw", [P, 3, C]), sb("WT", [P, 3, C])
        tmv, tmr, dec, decb = sb("tmv", [P, 1]), sb("tmr", [P, 1]), sb("dec", [P, 1]), sb("decb", [P, SEQ])
        zero = sb("zero", [P, SEQ])
        rw, rwT, rwS = sb("rw", [ER, C]), sb("rwT", [P, ER]), sb("rwS", [P, ER])
        rls, rlb, rbr, rbias = sb("rls", [P, 1]), sb("rlb", [P, 1]), sb("rbr", [P, ER]), sb("rbias", [P, ER])
        rlbb = sb("rlbb", [P, P])
        HN, YN, ZN = (sb(n, [P, TPG, C]) for n in ("HN", "YN", "ZN"))
        ZX = sb("ZX", [P, 2, TOP, TPG, ROW])
        goal = sb("goal", [P, TOP, TILES], I32)
        L1, L2 = sb("L1", [P, TPG, ER]), sb("L2", [P, TPG, ER])
        EQ, EQ2, M = sb("EQ", [P, TPG, ER]), sb("EQ2", [P, TOP, TPG, ER]), sb("M", [P, TOP, TPG, ER])
        M12 = sb("M12", [P, TPG, ER], BF16)
        top, which = sb("top", [P, TOP, TPG]), sb("which", [P, TOP, TPG])
        revi, rev = sb("revi", [P, ER], I32), sb("rev", [P, ER])
        starti = sb("starti", [P, ER], I32)
        tri, ones = sb("tri", [P, P]), sb("ones", [P, P])
        trib, onesb = sb("trib", [P, P], BF16), sb("onesb", [P, P], BF16)
        keep = sb("keep", [P, ER, TPG + 1])
        D1, SX = sb("D1", [P, ER, TPG + 1]), sb("SX", [P, ER, TPG + 1])
        SL, slot = sb("SL", [P, TPG, ER]), sb("slot", [P, TOP, TPG])
        SI = sb("SI", [P, 2, TOP, TPG], U32)
        HT, RT, YT, VT, ZT = (sb(n, [P, GT]) for n in ("HT", "RT", "YT", "VT", "ZT"))
        G = sb("G", [P, BPG, FT, SEQ])
        ST = sb("ST", [P, BPG, SEQ + 1])
        WM = sb("WM", [P, 2, 2, C])
        rest = sb("rest", [P, 2])
        TH, MM = sb("TH", [P, TPG, C]), sb("MM", [P, TPG, C])
        stat = [sb(f"bst{n}", [P, TPG, 6]) for n in range(3)]
        mv = [sb(f"bmv{n}", [P, TPG, 2]) for n in range(3)]
        var, ny, ntmp = sb("bva", [P, 3 * TPG]), sb("bny", [P, NEWTON + 1, 3 * TPG]), sb("bnt", [P, 2 * NEWTON, 3 * TPG])

        PT, PR_, PO, PVV, PG, PQ = (chip.ps(ctx, n, [P, GT]) for n in ("bpt", "bpr", "bpo", "bpv", "bpg", "bpq"))
        PH = [chip.ps(ctx, f"bph{n}", [P, GT]) for n in range(BPG)]

        def sem(name):
            return chip.sem(ctx, "b_" + name)

        (w_in, sel_in, zero_set, act_set, dve_set, pe_set, w_exp) = (
            sem(n) for n in ("w_in", "sel_in", "zero_set", "act_set", "dve_set", "pe_set", "w_exp"))
        stats = [sem(f"stats{n}") for n in range(3)]
        aggr = [sem(f"aggr{n}") for n in range(3)]
        var_set = [sem(f"var{n}") for n in range(3)]
        newton, tables, consts, mix_set = (sem(n) for n in ("newton", "tables", "consts", "mix_set"))
        applied = [sem(f"applied{n}") for n in range(3)]
        (hn_added, ht_full, ht_out, h1_full, g_out, r_full, r_out, o_full, x_ffn, yt_full, yt_out, scanned,
         v_full, v_out, gate_full, gate_out, o2_full, gated, x_rwkv, zt_full, zt_out, lg_full, lg_out,
         z_copied, goals_in, chain, masked, ranks_full, placed, run_in, scattered) = (sem(n) for n in (
             "hn_added ht_full ht_out h1_full g_out r_full r_out o_full x_ffn yt_full yt_out scanned "
             "v_full v_out gate_full gate_out o2_full gated x_rwkv zt_full zt_out lg_full lg_out z_copied goals_in "
             "chain masked ranks_full placed run_in scattered").split())
        N_IN = 15

        def tile_cols(n):
            return slice(n * P, (n + 1) * P)

        def tiles(m, g):
            return m[:, bass.ds(g * TPG, TPG), :]

        def tiles1(m, g):
            return m[:, bass.ds(g * TPG, TPG)]

        def run(step, eng):
            first, turns = LAST + 2, (GROUPS - 1 - (LAST + 2)) // 2
            for k in range(first):
                step(k, k)
            with eng.Fori(0, turns) as i:
                for r in range(2):
                    step(i * 2 + (first + r), first + r)
            for k in range(first + 2 * turns, GROUPS + LAST):
                step(k, k)

        def at(r, d):
            return 0 <= r - d < GROUPS

        block = ctx.enter_context(nc.Block())

        @block.sync
        def _(sp):
            loads = [
                (brow[:, 0:FT, :], t["L0_ffn_b1"].rearrange("e (n p) -> e n p", n=FT)), (brow[:, FT, :], t["L0_ffn_b2"]),
                (Wo[:, :], t["L0_ffn_Wo"]), (bo[:, :], t["L0_ffn_bo"].rearrange("(a c) -> a c", a=1)), (Wraw[:, 0, :], t["L1_attn_Wv"]),
                (Wraw[:, 1, :], t["L1_attn_Wr"]), (Wraw[:, 2, :], t["L1_attn_Wo"]),
                (tmv[:, :], column(t["L1_attn_time_mix_v"])), (tmr[:, :], column(t["L1_attn_time_mix_r"])),
                (dec[:, :], column(t["L1_attn_time_decay"])), (rw[:, :], t["L1_ffn_router_w"]),
                (rls[:, :], column(t["L1_ffn_router_ln_scale"])), (rlb[:, :], column(t["L1_ffn_router_ln_bias"])),
                (rbr[:, :], rows(t["L1_ffn_router_b"]))]
            assert len(loads) == N_IN - 1
            for dst, src in loads:
                sp.dma_start(dst, src).then_inc(w_in, 16)
            sp.dma_start(sel[:, :], chosen.rearrange("b a -> a b")).then_inc(sel_in, 16)
            sp.wait_ge(sel_in, 16)
            sp.wait_ge(dve_set, 1)

            def experts(g, r):
                for b in range(BPG):
                    e = sp.value_load(sel[0:1, bass.ds(g * BPG + b, 1)], min_val=0, max_val=E - 1)
                    sp.dma_start(W1e[:, r % 2, b, :], t["L0_ffn_W1"][bass.ds(e, 1)].rearrange("e k f -> k (e f)"))\
                        .then_inc(w_exp, 16)
                    sp.dma_start(W2e[:, r % 2, b, :, :], t["L0_ffn_W2"][bass.ds(e, 1)].rearrange(
                        "e (n p) h -> p (e n) h", n=FT)).then_inc(w_exp, 16)
                    sp.dma_start(Be[:, r % 2, b, :], biases[:, bass.ds(e, 1), :].rearrange("p e n -> p (e n)"))\
                        .then_inc(w_exp, 16)

            experts(0, 0)

            def step(k, r):
                if at(r, 0) and at(r + 1, 0):
                    wait_apart(sp, sel_in, w_exp, (k + 1) * (3 * 16 * BPG))
                    if r > 0:
                        wait_apart(sp, sel_in, r_out, k * BPG)
                    experts(k + 1, r + 1)

            run(step, sp)
            sp.wait_ge(scattered, 16 * SHARE * GROUPS)

        @block.gpsimd
        def _(pool):
            pool.wait_ge(w_in, 16 * (N_IN - 1))
            nc.gpsimd.memset(zero[:, :], 0.0).then_inc(zero_set, 1)

            nc.gpsimd.iota(revi[:, :], pattern=[[-1, ER]], base=ER, channel_multiplier=0).then_inc(consts, 1)
            nc.gpsimd.iota(starti[:, :], pattern=[[CAP, ER]], base=0, channel_multiplier=0).then_inc(consts, 1)
            nc.gpsimd.iota(goal[:, :, :].rearrange("p k t -> p (k t)"), pattern=[[P, TOP * TILES]], base=0,
                           channel_multiplier=1).then_inc(consts, 1)
            nc.gpsimd.memset(tri[:, :], 1.0).then_inc(consts, 1)
            nc.gpsimd.memset(ones[:, :], 1.0).then_inc(consts, 1)
            nc.gpsimd.memset(keep[:, :, :], 1.0).then_inc(consts, 1)
            pool.wait_ge(consts, 6)
            nc.gpsimd.affine_select(out=tri[:, :], in_=tri[:, :], compare_op=ALU.is_gt, fill=0.0, base=0,
                                    pattern=[[1, P]], channel_multiplier=-1).then_inc(consts, 1)

            def rsqrts(k, r):
                norms = [n for n in range(3) if at(r, 2 * n)]
                for n in norms:
                    g = k - 2 * n
                    wait_apart(pool, w_in, aggr[n], (g + 1) * TPG)
                    if not (isinstance(g, int) and g == 0):
                        wait_apart(pool, w_in, applied[n], g * TPG)
                    slope, least = (1.0, LN_EPS) if n < 2 else (1.0 + LN2_EPS, LN_EPS * LN2_EPS)
                    nc.gpsimd.tensor_scalar(var[:, n * TPG:(n + 1) * TPG], mv[n][:, :, 1], slope, least,
                                            ALU.mult, ALU.add).then_inc(var_set[n], 1)
                for n in norms:
                    wait_apart(pool, w_in, var_set[n], k - 2 * n + 1)
                part = slice(norms[0] * TPG, (norms[-1] + 1) * TPG)
                nc.gpsimd.tensor_scalar(ny[:, 0, part].bitcast(I32), var[:, part].bitcast(I32), -0.5, RSQRT_SEED,
                                        ALU.mult, ALU.add).then_inc(newton, 1)
                wait_apart(pool, w_in, newton, k * (NEWTON_OPS + 1) + 1)
                newton_rsqrt(nc.gpsimd, w_in, newton, k * (NEWTON_OPS + 1) + 1, ny[:, :, part], var[:, part],
                             ntmp[:, :, part])

            def add_norm(g):
                wait_apart(pool, w_in, applied[0], (g + 1) * TPG)
                nc.gpsimd.tensor_tensor(tiles(X, g), tiles(X, g), HN[:, :, :], ALU.add).then_inc(hn_added, 1)

            def scatter(g, r, tiles_):
                if tiles_[0] == 0:
                    wait_apart(pool, w_in, placed, (g + 1) * 6)
                    wait_apart(pool, w_in, goals_in, g + 1)
                    wait_apart(pool, w_in, z_copied, (g + 1) * TOP)
                    if not (isinstance(g, int) and g == 0):
                        wait_apart(pool, w_in, scattered, g * (16 * SHARE))
                for i in tiles_:
                    for n in range(TOP):
                        nc.gpsimd.indirect_dma_start(out=sorted_rows, out_offset=bass.IndirectOffsetOnAxis(
                            ap=SI[:, r % 2, n, i:i + 1], axis=0), in_=ZX[:, r % 2, n, i, :], in_offset=None)\
                            .then_inc(scattered, 16)

            pool.wait_ge(dve_set, 14)

            def step(k, r):
                if at(r, 6):
                    scatter(k - 6, r - 6, range(TPG // 2))
                if at(r, 0) or at(r, 2) or at(r, 4):
                    rsqrts(k, r)
                if at(r, 6):
                    scatter(k - 6, r - 6, range(TPG // 2, TPG))
                if at(r, 0):
                    add_norm(k)

            run(step, pool)

        @block.scalar
        def _(act):
            act.wait_ge(w_in, 16 * (N_IN - 1))
            nc.scalar.activation(dec[:, :], dec[:, :], ACT.Exp).then_inc(act_set, 1)
            act.wait_ge(act_set, 1)
            nc.scalar.activation(dec[:, :], dec[:, :], ACT.Exp, scale=-1.0).then_inc(act_set, 1)
            act.wait_ge(act_set, 2)
            act.wait_ge(zero_set, 1)
            nc.scalar.activation(decb[:, :], zero[:, :], ACT.Identity, bias=dec[:, 0:1]).then_inc(act_set, 1)

            def turned(g, full, out, dst, used, per):
                act.wait_ge(full, g + 1)
                if not (isinstance(g, int) and g == 0):
                    act.wait_ge(used, g * per)
                nc.scalar.copy(dst[:, :], PT[:, :]).then_inc(out, 1)

            def gelus(g, b, r):
                act.wait_ge(h1_full, g * BPG + (b + 1))
                act.wait_ge(w_exp, (g + 1) * (3 * 16 * BPG))
                if b == 0 and not (isinstance(g, int) and g == 0):
                    act.wait_ge(r_full, g)
                for n in range(FT):
                    nc.scalar.activation(G[:, b, n, :], PH[b][:, n * SEQ:(n + 1) * SEQ], ACT.Gelu,
                                         bias=Be[:, r % 2, b, n:n + 1]).then_inc(g_out, 1)

            def reasoned(g, r):
                act.wait_ge(r_full, g + 1)
                if not (isinstance(g, int) and g == 0):
                    act.wait_ge(o_full, g)
                for b in range(BPG):
                    nc.scalar.activation(RT[:, b * SEQ:(b + 1) * SEQ], PR_[:, b * SEQ:(b + 1) * SEQ], ACT.Identity,
                                         bias=Be[:, r % 2, b, FT:NB]).then_inc(r_out, 1)

            def values(g):
                act.wait_ge(v_full, g + 1)
                if not (isinstance(g, int) and g == 0):
                    act.wait_ge(o2_full, g)
                nc.scalar.copy(VT[:, :], PVV[:, :]).then_inc(v_out, 1)

            def gate(g):
                act.wait_ge(gate_full, g + 1)
                if not (isinstance(g, int) and g == 0):
                    act.wait_ge(gated, g)
                nc.scalar.activation(TH[:, :, :], PG[:, :].rearrange("p (t c) -> p t c", t=TPG), ACT.Tanh, scale=0.5)\
                    .then_inc(gate_out, 1)

            def copies(g, r):
                act.wait_ge(applied[2], (g + 1) * TPG)
                if not (isinstance(g, int) and g < 2):
                    act.wait_ge(scattered, (g - 1) * (16 * SHARE))
                for n in range(TOP):
                    nc.scalar.copy(ZX[:, r % 2, n, :, 0:C], ZN[:, :, :]).then_inc(z_copied, 1)

            def step(k, r):
                if at(r, 4):
                    values(k - 4)
                    gate(k - 4)
                if at(r, 1):
                    turned(k - 1, ht_full, ht_out, HT, h1_full, BPG)
                if at(r, 3):
                    turned(k - 3, yt_full, yt_out, YT, gate_full, 1)
                if at(r, 1):
                    gelus(k - 1, 0, r - 1)
                    gelus(k - 1, 1, r - 1)
                if at(r, 5):
                    turned(k - 5, zt_full, zt_out, ZT, lg_full, 1)
                    copies(k - 5, r - 5)
                if at(r, 1):
                    reasoned(k - 1, r - 1)

            run(step, act)

        @block.vector
        def _(dve):
            dve.wait_ge(w_in, 16 * (N_IN - 1))
            dve.wait_ge(pe_set, 1)
            nc.vector.tensor_copy(biases[:, :, :].rearrange("p e n -> p n e"),
                                  PT[:, 0:NB * E].rearrange("p (n e) -> p n e", n=NB)).then_inc(dve_set, 1)
            dve.wait_ge(pe_set, 2)
            nc.vector.tensor_copy(WT[:, :, :], PO[:, 0:3 * C].rearrange("p (n c) -> p n c", n=3)).then_inc(dve_set, 1)
            for n, m in enumerate((tmv, tmr)):
                nc.vector.tensor_scalar(rest[:, n:n + 1], m[:, :], -1.0, 1.0, ALU.mult, ALU.add).then_inc(mix_set, 1)
            dve.wait_ge(mix_set, 2)
            dve.wait_ge(dve_set, 2)
            for n, m in enumerate((tmv, tmr)):
                nc.vector.tensor_scalar(WM[:, n, 0, :], WT[:, n, :], m[:, 0:1], None, ALU.mult).then_inc(mix_set, 1)
                nc.vector.tensor_scalar(WM[:, n, 1, :], WT[:, n, :], rest[:, n:n + 1], None, ALU.mult).then_inc(mix_set, 1)
            nc.vector.memset(one_row[:, :], 1.0).then_inc(dve_set, 1)
            nc.vector.memset(ST[:, :, 0:1], 0.0).then_inc(dve_set, 1)
            dve.wait_ge(pe_set, 3)
            nc.vector.tensor_copy(rwT[:, :], PG[:, 0:ER]).then_inc(dve_set, 1)
            nc.vector.tensor_scalar(rwS[:, :], PG[:, 0:ER], rls[:, 0:1], None, ALU.mult).then_inc(dve_set, 1)
            nc.vector.tensor_scalar(rlbb[:, :], ident[:, :], 0.0, rlb[:, 0:1], ALU.mult, ALU.add).then_inc(dve_set, 1)
            dve.wait_ge(pe_set, 4)
            nc.vector.tensor_tensor(rbias[:, :], PQ[:, 0:ER], rbr[:, :], ALU.add).then_inc(dve_set, 1)
            dve.wait_ge(consts, 7)
            nc.vector.tensor_copy(rev[:, :], revi[:, :]).then_inc(dve_set, 1)
            nc.vector.tensor_copy(SX[:, :, TPG], starti[:, :]).then_inc(dve_set, 1)
            nc.vector.tensor_copy(trib[:, :], tri[:, :]).then_inc(dve_set, 1)
            nc.vector.tensor_copy(onesb[:, :], ones[:, :]).then_inc(dve_set, 1)
            nc.vector.memset(keep[:, :, 0:1], 0.0).then_inc(dve_set, 1)
            nc.vector.memset(ZX[:, :, :, :, :].rearrange("p b k t c -> p (b k t c)"), 0.0).then_inc(dve_set, 1)
            dve.wait_ge(dve_set, 14)
            dve.wait_ge(act_set, 3)

            def norm_stats(n, g):
                if not (isinstance(g, int) and g == 0):
                    wait_apart(dve, w_in, applied[n], g * TPG)
                for i in range(TPG):
                    nc.vector.bn_stats(stat[n][:, i, :], X[:, bass.ds(g * TPG + i, 1), :].rearrange("p a c -> p (a c)"))\
                        .then_inc(stats[n], 1)
                wait_apart(dve, w_in, stats[n], (g + 1) * TPG)
                for i in range(TPG):
                    nc.vector.bn_aggr(mv[n][:, i, :], stat[n][:, i, :]).then_inc(aggr[n], 1)

            def apply(n, g, dst, used, per):
                dve.wait_ge(newton, (g + (2 * n + 1)) * (NEWTON_OPS + 1))
                if not (isinstance(g, int) and g == 0):
                    dve.wait_ge(used, g * per)
                    if n == 2:
                        dve.wait_ge(z_copied, g * TOP)
                    if n == 0:
                        dve.wait_ge(hn_added, g)
                for i in range(TPG):
                    nc.vector.tensor_scalar(dst[:, i, :], X[:, bass.ds(g * TPG + i, 1), :].rearrange("p a c -> p (a c)"),
                                            mv[n][:, i, 0:1], ny[:, NEWTON, n * TPG + i:n * TPG + i + 1], ALU.subtract, ALU.mult)\
                        .then_inc(applied[n], 1)

            def scan(g):
                dve.wait_ge(yt_out, g + 1)
                if not (isinstance(g, int) and g == 0):
                    dve.wait_ge(gate_full, g)
                for b in range(BPG):
                    nc.vector.tensor_tensor_scan(ST[:, b, 1:SEQ + 1], decb[:, :], YT[:, b * SEQ:(b + 1) * SEQ], 0.0,
                                                 ALU.mult, ALU.add).then_inc(scanned, 1)

            def ffn_residual(g):
                dve.wait_ge(o_full, g + 1)
                dve.wait_ge(hn_added, g + 1)
                nc.vector.scalar_tensor_tensor(out=tiles(X, g), in0=PO[:, :].rearrange("p (t c) -> p t c", t=TPG), scalar=0.3,
                                               in1=tiles(X, g), op0=ALU.mult, op1=ALU.add).then_inc(x_ffn, 1)
                dve.wait_ge(x_ffn, g + 1)

            def rwkv_residual(g):
                dve.wait_ge(gate_out, g + 1)
                dve.wait_ge(o2_full, g + 1)
                nc.vector.scalar_tensor_tensor(out=MM[:, :, :], in0=TH[:, :, :], scalar=1.0,
                                               in1=PQ[:, :].rearrange("p (t c) -> p t c", t=TPG), op0=ALU.add,
                                               op1=ALU.mult).then_inc(gated, 1)
                dve.wait_ge(gated, g + 1)
                nc.vector.scalar_tensor_tensor(out=tiles(X, g), in0=MM[:, :, :], scalar=0.5, in1=tiles(X, g),
                                               op0=ALU.mult, op1=ALU.add).then_inc(x_rwkv, 1)
                dve.wait_ge(x_rwkv, g + 1)

            def over_e(x):
                return x.unsqueeze(2).to_broadcast([P, TPG, ER])

            def over_t(x):
                return x.unsqueeze(1).to_broadcast([P, TPG, ER])

            def best_two(g, r):
                done = [0]

                def link(ins):
                    done[0] += 1
                    ins.then_inc(chain, 1)
                    dve.wait_ge(chain, g * 12 + done[0])

                dve.wait_ge(lg_full, g + 1)
                nc.vector.tensor_tensor(L1[:, :, :], PT[:, 0:TPG * ER].rearrange("p (t e) -> p t e", t=TPG),
                                        over_t(rbias[:, :]), ALU.add).then_inc(lg_out, 1)
                dve.wait_ge(lg_out, g + 1)
                for n, l in enumerate((L1, L2)):
                    link(nc.vector.tensor_reduce(top[:, n, :], l[:, :, :], AX.X, ALU.max))
                    link(nc.vector.tensor_tensor(EQ[:, :, :], l[:, :, :], over_e(top[:, n, :]), ALU.is_equal))
                    link(nc.vector.tensor_tensor(EQ[:, :, :], EQ[:, :, :], over_t(rev[:, :]), ALU.mult))
                    link(nc.vector.tensor_reduce(which[:, n, :], EQ[:, :, :], AX.X, ALU.max))
                    link(nc.vector.tensor_tensor(M[:, n, :, :], over_t(rev[:, :]), over_e(which[:, n, :]), ALU.is_equal))
                    if n == 0:
                        link(nc.vector.scalar_tensor_tensor(out=L2[:, :, :], in0=M[:, 0, :, :], scalar=-BIG,
                                                            in1=L1[:, :, :], op0=ALU.mult, op1=ALU.add))
                if not (isinstance(g, int) and g == 0):
                    dve.wait_ge(ranks_full, g)
                nc.vector.tensor_tensor(M12[:, :, :], M[:, 0, :, :], M[:, 1, :, :], ALU.add).then_inc(masked, 1)
                link(nc.vector.tensor_tensor(tiles1(second_less_first, g), top[:, 1, :], top[:, 0, :], ALU.subtract))
                if not (isinstance(g, int) and g < 2):
                    dve.wait_ge(scattered, (g - 1) * (16 * SHARE))
                nc.vector.tensor_copy(ZX[:, r % 2, :, :, C].bitcast(I32), goal[:, :, bass.ds(g * TPG, TPG)])\
                    .then_inc(goals_in, 1)

            def places(g, r):
                done = [0]

                def link(ins):
                    done[0] += 1
                    ins.then_inc(placed, 1)
                    dve.wait_ge(placed, g * 6 + done[0])

                nc.vector.tensor_copy(D1[:, :, 0], SX[:, :, TPG]).then_inc(run_in, 1)
                dve.wait_ge(ranks_full, g + 1)
                link(nc.vector.tensor_copy(D1[:, :, 1:], PVV[:, TPG * ER:2 * TPG * ER].rearrange(
                    "p (t e) -> p e t", t=TPG)))
                dve.wait_ge(run_in, g + 1)
                link(nc.vector.tensor_tensor_scan(SX[:, :, :].rearrange("p e t -> p (e t)"),
                                                  keep[:, :, :].rearrange("p e t -> p (e t)"),
                                                  D1[:, :, :].rearrange("p e t -> p (e t)"), 0.0, ALU.mult, ALU.add))
                link(nc.vector.tensor_tensor(SL[:, :, :], PVV[:, 0:TPG * ER].rearrange("p (t e) -> p t e", t=TPG),
                                             SX[:, :, 0:TPG].rearrange("p e t -> p t e"), ALU.add))
                link(nc.vector.tensor_tensor(EQ2[:, :, :, :], M[:, :, :, :],
                                             SL[:, :, :].unsqueeze(1).to_broadcast([P, TOP, TPG, ER]), ALU.mult))
                link(nc.vector.tensor_reduce(slot[:, :, :], EQ2[:, :, :, :], AX.X, ALU.add))
                if not (isinstance(g, int) and g < 2):
                    dve.wait_ge(scattered, (g - 1) * (16 * SHARE))
                link(nc.vector.tensor_copy(SI[:, r % 2, :, :], slot[:, :, :]))

            def step(k, r):
                if at(r, 0):
                    norm_stats(0, k)
                if at(r, 2):
                    ffn_residual(k - 2)
                    norm_stats(1, k - 2)
                if at(r, 4):
                    rwkv_residual(k - 4)
                    norm_stats(2, k - 4)
                if at(r, 3):
                    scan(k - 3)
                if at(r, 5):
                    best_two(k - 5, r - 5)
                if at(r, 5):
                    places(k - 5, r - 5)
                if at(r, 0):
                    apply(0, k, HN, ht_full, 1)
                if at(r, 2):
                    apply(1, k - 2, YN, yt_full, 1)
                if at(r, 4):
                    apply(2, k - 4, ZN, zt_full, 1)

            run(step, dve)
            nc.vector.tensor_copy(next_rows[:, :], SX[:, :, TPG]).then_inc(tables, 1)

        @block.tensor
        def _(pe):
            wait(pe, w_in, 16 * (N_IN - 1))
            for n in range(NB):
                mm = nc.tensor.transpose(PT[:, n * E:(n + 1) * E], brow[:, n, :], ident[0:E, 0:E])
            mm.then_inc(pe_set, 1)
            for n in range(3):
                mm = nc.tensor.transpose(PO[:, tile_cols(n)], Wraw[:, n, :], ident[:, :])
            mm.then_inc(pe_set, 1)
            nc.tensor.transpose(PG[:, 0:ER], rw[:, :], ident[0:ER, 0:ER]).then_inc(pe_set, 1)
            wait(pe, dve_set, 7)
            nc.tensor.matmul(PQ[:, 0:ER], rlbb[:, :], rwT[:, :], start=True, stop=True).then_inc(pe_set, 1)
            wait(pe, dve_set, 14)
            wait(pe, mix_set, 6)

            def turn(src, ready, full, g, free, count):
                wait(pe, ready, (g + 1) * TPG)
                wait(pe, free, count)
                for n in range(TPG):
                    mm = nc.tensor.transpose(PT[:, tile_cols(n)], src[:, n, :], ident[:, :])
                mm.then_inc(full, 1)

            def first_product(g, r):
                wait(pe, ht_out, g + 1)
                wait(pe, w_exp, (g + 1) * (3 * 16 * BPG))
                if not (isinstance(g, int) and g == 0):
                    wait(pe, g_out, g * BPG * FT)
                for b in range(BPG):
                    for n in range(FT):
                        mm = nc.tensor.matmul(PH[b][:, n * SEQ:(n + 1) * SEQ], W1e[:, r % 2, b, n * P:(n + 1) * P],
                                              HT[:, b * SEQ:(b + 1) * SEQ], start=True, stop=True)
                    mm.then_inc(h1_full, 1)

            def second_product(g, r):
                wait(pe, g_out, (g + 1) * BPG * FT)
                if not (isinstance(g, int) and g == 0):
                    wait(pe, r_out, g * BPG)
                for b in range(BPG):
                    for n in range(FT):
                        mm = nc.tensor.matmul(PR_[:, b * SEQ:(b + 1) * SEQ], W2e[:, r % 2, b, n, :], G[:, b, n, :],
                                              start=(n == 0), stop=(n == FT - 1))
                mm.then_inc(r_full, 1)

            def by_rows(bank, src, w, full):
                for n in range(TPG):
                    mm = nc.tensor.matmul(bank[:, tile_cols(n)], src[:, tile_cols(n)], w, start=True, stop=True)
                mm.then_inc(full, 1)

            def ffn_out(g):
                wait(pe, r_out, (g + 1) * BPG)
                if not (isinstance(g, int) and g == 0):
                    wait(pe, x_ffn, g)
                for n in range(TPG):
                    nc.tensor.matmul(PO[:, tile_cols(n)], RT[:, tile_cols(n)], Wo[:, :], start=True, stop=False)
                    mm = nc.tensor.matmul(PO[:, tile_cols(n)], one_row[:, :], bo[:, :], start=False, stop=True)
                mm.then_inc(o_full, 1)

            def ranks(g, free):
                wait(pe, masked, g + 1)
                wait(pe, v_out, free)
                m12 = M12[:, :, :].rearrange("p t e -> p (t e)")
                nc.tensor.matmul(PVV[:, 0:TPG * ER], trib[:, :], m12, start=True, stop=True)
                nc.tensor.matmul(PVV[:, TPG * ER:2 * TPG * ER], onesb[:, :], m12, start=True, stop=True)\
                    .then_inc(ranks_full, 1)

            def values_gates(g, r):
                wait(pe, scanned, (g + 1) * BPG)
                wait(pe, yt_out, g + 1)
                if not (isinstance(g, int) and g == 0):
                    wait(pe, v_out, g)
                if at(r, 2):
                    wait(pe, placed, (g - 1) * 6)
                nc.tensor.matmul(PVV[:, :], WM[:, 0, 0, :], YT[:, :], start=True, stop=False)
                nc.tensor.matmul(PVV[:, :].rearrange("p (b s) -> p b s", b=BPG), WM[:, 0, 1, :], ST[:, :, 0:SEQ],
                                 start=False, stop=True).then_inc(v_full, 1)
                if not (isinstance(g, int) and g == 0):
                    wait(pe, gate_out, g)
                for n in range(TPG):
                    b, i = divmod(n, TPB)
                    nc.tensor.matmul(PG[:, tile_cols(n)], YT[:, tile_cols(n)], WM[:, 1, 0, :], start=True, stop=False)
                    mm = nc.tensor.matmul(PG[:, tile_cols(n)], ST[:, b, i * P:(i + 1) * P], WM[:, 1, 1, :],
                                          start=False, stop=True)
                mm.then_inc(gate_full, 1)

            def rwkv_out(g):
                wait(pe, v_out, g + 1)
                if not (isinstance(g, int) and g == 0):
                    wait(pe, gated, g)
                by_rows(PQ, VT, WT[:, 2, :], o2_full)

            def router(g):
                wait(pe, zt_out, g + 1)
                for n in range(TPG):
                    mm = nc.tensor.matmul(PT[:, n * ER:(n + 1) * ER], ZT[:, tile_cols(n)], rwS[:, :], start=True, stop=True)
                mm.then_inc(lg_full, 1)

            def step(k, r):
                before = (dve_set, 14)
                if at(r - 1, 5):
                    before = (lg_out, k - 5)
                elif at(r - 1, 3):
                    before = (yt_out, k - 3)
                elif at(r - 1, 1):
                    before = (ht_out, k - 1)
                if at(r, 2):
                    ffn_out(k - 2)
                if at(r, 4):
                    values_gates(k - 4, r - 4)
                    rwkv_out(k - 4)
                if at(r, 1):
                    turn(HN, applied[0], ht_full, k - 1, *before)
                    before = (ht_out, k)
                if at(r, 3):
                    turn(YN, applied[1], yt_full, k - 3, *before)
                    before = (yt_out, k - 2)
                if at(r, 1):
                    first_product(k - 1, r - 1)
                if at(r, 5):
                    turn(ZN, applied[2], zt_full, k - 5, *before)
                    router(k - 5)
                if at(r, 1):
                    second_product(k - 1, r - 1)
                if at(r, 5):
                    ranks(k - 5, k - 3 if at(r, 4) else GROUPS)

            run(step, pe)


def plan(nc, chip, next_rows, second_less_first, gates, tile_expert, tile_row, sorted_rows, NT):
    E = next_rows.shape[1]
    with ExitStack() as ctx:
        def sb(name, shape, dt=F32):
            return chip.sb(ctx, name, shape, dt)

        ed, den = sb("ed", [P, TILES]), sb("den", [P, TILES])
        starti, start = sb("starti", [1, E], I32), sb("start", [1, E])
        count, padi, pad, ends, gain = sb("count", [1, E]), sb("padi", [1, E], I32), sb("pad", [1, E]), sb("ends", [1, E]), sb("gain", [1, E])
        one = sb("one", [1, E])
        ioti, iot = sb("ioti", [1, NT], I32), sb("iot", [1, NT])
        after, moved = sb("after", [1, NT, E - 1]), sb("moved", [1, NT, E - 1])
        cnt, shift, at = sb("cnt", [1, NT]), sb("shift", [1, NT]), sb("at", [1, NT])
        headi = sb("headi", [1, E], U32)
        empty = sb("empty", [P, SUB, ROW])
        consts, chain, exped, pads_in, pad_set = (chip.sem(ctx, "p_" + n) for n in "consts chain exped pads_in pad_set".split())
        block = ctx.enter_context(nc.Block())

        @block.gpsimd
        def _(pool):
            nc.gpsimd.iota(starti[:, :], pattern=[[CAP, E]], base=0, channel_multiplier=0).then_inc(consts, 1)
            nc.gpsimd.iota(ioti[:, :], pattern=[[E_SLOTS, NT]], base=0, channel_multiplier=0).then_inc(consts, 1)
            nc.gpsimd.memset(one[:, :], 1.0).then_inc(consts, 1)
            nc.gpsimd.memset(empty[:, :, :], 0.0).then_inc(pad_set, 1)
            pool.wait_ge(pad_set, 1)
            nc.gpsimd.memset(empty[:, :, C:ROW].bitcast(I32), 4 * TOKENS).then_inc(pad_set, 1)

        @block.scalar
        def _(act):
            nc.scalar.activation(ed[:, :], second_less_first[:, :], ACT.Exp).then_inc(exped, 1)

        @block.sync
        def _(sp):
            sp.wait_ge(pad_set, 2)
            sp.wait_ge(chain, 1)
            for e in range(E):
                row = sp.value_load(headi[0:1, e:e + 1], min_val=0, max_val=E * CAP - E_SLOTS)
                sp.dma_start(sorted_rows[bass.ds(row, E_SLOTS), :].rearrange("(n p) c -> p n c", p=P), empty[:, :, :])\
                    .then_inc(pads_in, 16)
            sp.wait_ge(pads_in, 16 * E)

        @block.vector
        def _(dve):
            done = [0]

            def link(ins):
                done[0] += 1
                ins.then_inc(chain, 1)
                dve.wait_ge(chain, done[0])

            head = next_rows[0:1, :]
            link(nc.vector.tensor_copy(headi[:, :], head))
            dve.wait_ge(consts, 3)
            link(nc.vector.tensor_copy(start[:, :], starti[:, :]))
            link(nc.vector.tensor_copy(iot[:, :], ioti[:, :]))
            link(nc.vector.tensor_tensor(count[:, :], head, start[:, :], ALU.subtract))
            link(nc.vector.tensor_scalar(padi[:, :], count[:, :], float(E_SLOTS - 1), None, ALU.add))
            bits = E_SLOTS.bit_length() - 1
            link(nc.vector.tensor_scalar(padi[:, :], padi[:, :], bits, bits, ALU.logical_shift_right,
                                         ALU.logical_shift_left))
            link(nc.vector.tensor_copy(pad[:, :], padi[:, :]))
            link(nc.vector.tensor_tensor_scan(ends[:, :], one[:, :], pad[:, :], 0.0, ALU.mult, ALU.add))
            link(nc.vector.tensor_tensor(after[:, :, :], iot[:, :].unsqueeze(2).to_broadcast([1, NT, E - 1]),
                                         ends[:, 0:E - 1].unsqueeze(1).to_broadcast([1, NT, E - 1]), ALU.is_ge))
            link(nc.vector.tensor_reduce(cnt[:, :], after[:, :, :], AX.X, ALU.add))
            link(nc.vector.tensor_copy(tile_expert[:, :], cnt[:, :]))
            link(nc.vector.tensor_scalar(gain[:, :], pad[:, :], -1.0, float(CAP), ALU.mult, ALU.add))
            link(nc.vector.tensor_tensor(moved[:, :, :], after[:, :, :],
                                         gain[:, 0:E - 1].unsqueeze(1).to_broadcast([1, NT, E - 1]), ALU.mult))
            link(nc.vector.tensor_reduce(shift[:, :], moved[:, :, :], AX.X, ALU.add))
            link(nc.vector.tensor_tensor(at[:, :], iot[:, :], shift[:, :], ALU.add))
            link(nc.vector.tensor_tensor(at[:, :], at[:, :], head[:, E - 1:E].to_broadcast([1, NT]), ALU.min))
            link(nc.vector.tensor_copy(tile_row[:, :], at[:, :]))
            dve.wait_ge(exped, 1)
            link(nc.vector.tensor_scalar(den[:, :], ed[:, :], 1.0, None, ALU.add))
            link(nc.vector.reciprocal(gates[:, 0, :], den[:, :]))
            link(nc.vector.tensor_tensor(gates[:, 1, :], ed[:, :], gates[:, 0, :], ALU.mult))


def routed_experts(nc, chip, X, ident, sorted_rows, gates, tile_expert, tile_row, W1T, W2T, B1, b2, out, NT):
    E, H = W1T.shape[1], W1T.shape[2]
    HT = H // P
    LAST = 4
    TURN = 4
    LOAD = 8
    with ExitStack() as ctx:
        def sb(name, shape, dt=F32):
            return chip.sb(ctx, name, shape, dt)

        W1e, b1e, b2e = sb("W1x", [P, TURN, H]), sb("b1x", [P, TURN, HT]), sb("b2x", [P, E, C])
        IT = sb("IT", [P, TURN, SUB], U32)
        GX, GT_ = sb("GX", [P, TURN, SUB, ROW]), sb("GXT", [P, 2, E_SLOTS])
        HG = sb("HG", [P, 2, HT, E_SLOTS])
        YS = sb("YS", [P, 2, SUB, C])
        Y = sb("Y", [P, 2, 2, LOAD, C])
        results = chip.dram("results", [2 * TOKENS, C], F32)
        PT = chip.ps(ctx, "xpt", [P, E_SLOTS])
        PH = [chip.ps(ctx, f"xph{n}", [P, E_SLOTS]) for n in range(HT)]
        PY = [chip.ps(ctx, f"xpy{n}", [P, E_SLOTS]) for n in range(2)]
        idx_ok = chip.sem(ctx, "x_start")
        (w1_in, gathered, t_full, t_out, h_full, h_out, y_full, y_out, scattered, tgt, y_in, mixed, added,
         x_out) = (chip.sem(ctx, "x_" + n) for n in (
             "w1_in gathered t_full t_out h_full h_out y_full y_out scattered tgt y_in mixed added x_out").split())

        def run(step, eng):
            first = LAST + 2
            turns = (NT - 1 - first) // TURN
            for k in range(first):
                step(k, k)
            with eng.Fori(0, turns) as i:
                for r in range(TURN):
                    step(i * TURN + (first + r), first + r)
            for k in range(first + TURN * turns, NT + LAST):
                step(k, k)

        def at(r, d):
            return 0 <= r - d < NT

        def early(g, n):
            return isinstance(g, int) and g < n

        def store(sp, n):
            sp.wait_ge(added, (n + 1) * LOAD)
            sp.dma_start(out.rearrange("b (t p) c -> p (b t) c", p=P)[:, n * LOAD:(n + 1) * LOAD, :],
                         X[:, n * LOAD:(n + 1) * LOAD, :]).then_inc(x_out, 16)

        block = ctx.enter_context(nc.Block())

        @block.sync
        def _(sp):
            sp.dma_start(b2e[:, :, :], rows(b2)).then_inc(idx_ok, 16)
            sp.wait_ge(idx_ok, 16)

            def load_rows(j, r):
                row = sp.value_load(tile_row[0:1, bass.ds(j, 1)], min_val=0, max_val=E * CAP - E_SLOTS)
                if not early(j, 1):
                    wait_apart(sp, idx_ok, gathered, j * 16)
                if not early(j, TURN):
                    wait_apart(sp, idx_ok, t_full, j - (TURN - 1))
                    wait_apart(sp, idx_ok, tgt, j - (TURN - 1))
                sp.dma_start(GX[:, r % TURN, :, :], sorted_rows[bass.ds(row, E_SLOTS), :].rearrange("(n p) c -> p n c", p=P))\
                    .then_inc(gathered, 16)

            def load(j, r):
                e = sp.value_load(tile_expert[0:1, bass.ds(j, 1)], min_val=0, max_val=E - 1)
                if not early(j, 1):
                    wait_apart(sp, idx_ok, w1_in, j * 32)
                if not early(j, TURN):
                    wait_apart(sp, idx_ok, h_full, (j - (TURN - 1)) * HT)
                    wait_apart(sp, idx_ok, h_out, (j - (TURN - 1)) * HT)
                sp.dma_start(W1e[:, r % TURN, :], W1T[:, bass.ds(e, 1), :].rearrange("p e h -> p (e h)")).then_inc(w1_in, 16)
                sp.dma_start(b1e[:, r % TURN, :], B1[:, bass.ds(e, 1), :].rearrange("p e h -> p (e h)")).then_inc(w1_in, 16)

            def step(k, r):
                if at(r, 0):
                    load_rows(k, r)
                    load(k, r)

            run(step, sp)
            sp.wait_ge(scattered, NT * SUB * 16)
            for n in range(TILES // LOAD):
                if n >= 2:
                    sp.wait_ge(added, (n - 1) * LOAD)
                sp.wait_ge(y_in, 32 * n)
                for k in range(2):
                    sp.dma_start(Y[:, n % 2, k, :, :], results.rearrange("(k t p) c -> p k t c", k=2, p=P)[
                        :, k, n * LOAD:(n + 1) * LOAD, :]).then_inc(y_in, 16)
                if n > 0:
                    store(sp, n - 1)
            store(sp, TILES // LOAD - 1)
            sp.wait_ge(x_out, 16 * (TILES // LOAD))

        @block.gpsimd
        def _(pool):
            def scatter(j, r):
                wait_apart(pool, idx_ok, tgt, j + 1)
                wait_apart(pool, idx_ok, y_out, j + 1)
                if not early(j, 1):
                    wait_apart(pool, idx_ok, scattered, j * SUB * 16)
                for n in range(SUB):
                    nc.gpsimd.indirect_dma_start(out=results, out_offset=bass.IndirectOffsetOnAxis(
                        ap=IT[:, r % TURN, n:n + 1], axis=0), in_=YS[:, r % 2, n, :], in_offset=None,
                        bounds_check=2 * TOKENS - 1, oob_is_err=False).then_inc(scattered, 16)

            def step(k, r):
                if at(r, 4):
                    scatter(k - 4, r - 4)

            run(step, pool)

        @block.vector
        def _(dve):
            def targets(j, r):
                dve.wait_ge(gathered, (j + 1) * 16)
                if not early(j, TURN):
                    dve.wait_ge(scattered, (j - (TURN - 1)) * SUB * 16)
                nc.vector.tensor_copy(IT[:, r % TURN, :], GX[:, r % TURN, :, C].bitcast(U32)).then_inc(tgt, 1)

            def results_out(j, r):
                dve.wait_ge(y_full, j + 1)
                if not early(j, 2):
                    dve.wait_ge(scattered, (j - 1) * SUB * 16)
                e = dve.value_load(tile_expert[0:1, bass.ds(j, 1)], min_val=0, max_val=E - 1)
                bias = b2e[:, bass.ds(e, 1), :].to_broadcast([P, SUB, C])
                nc.vector.tensor_tensor(YS[:, r % 2, :, :], PY[r % 2][:, :].rearrange("p (n c) -> p n c", n=SUB),
                                        bias, ALU.add).then_inc(y_out, 1)

            def step(k, r):
                if at(r, 1):
                    targets(k - 1, r - 1)
                if at(r, 3):
                    results_out(k - 3, r - 3)

            run(step, dve)
            for n in range(TILES // LOAD):
                dve.wait_ge(y_in, 32 * (n + 1))
                for i in range(LOAD):
                    tile = n * LOAD + i
                    for k in range(2):
                        if k:
                            dve.wait_ge(mixed, tile + 1)
                        nc.vector.scalar_tensor_tensor(out=X[:, tile, :], in0=Y[:, n % 2, k, i, :],
                                                       scalar=gates[:, k, tile:tile + 1], in1=X[:, tile, :],
                                                       op0=ALU.mult, op1=ALU.add).then_inc((mixed, added)[k], 1)

        @block.scalar
        def _(act):
            def turned(j, r):
                act.wait_ge(t_full, j + 1)
                if not early(j, 2):
                    act.wait_ge(h_full, (j - 1) * HT)
                nc.scalar.copy(GT_[:, r % 2, :], PT[:, :]).then_inc(t_out, 1)

            def gelus(j, r):
                act.wait_ge(w1_in, (j + 1) * 32)
                if not early(j, 2):
                    act.wait_ge(y_full, j - 1)
                for n in range(HT):
                    act.wait_ge(h_full, j * HT + (n + 1))
                    nc.scalar.activation(HG[:, r % 2, n, :], PH[n][:, :], ACT.Gelu, bias=b1e[:, r % TURN, n:n + 1])\
                        .then_inc(h_out, 1)

            def step(k, r):
                if at(r, 1):
                    turned(k - 1, r - 1)
                if at(r, 2):
                    gelus(k - 2, r - 2)

            run(step, act)

        @block.tensor
        def _(pe):
            def turn(j, r):
                wait(pe, gathered, (j + 1) * 16)
                if not early(j, 1):
                    wait(pe, t_out, j)
                for n in range(SUB):
                    mm = nc.tensor.transpose(PT[:, n * P:(n + 1) * P], GX[:, r % TURN, n, 0:C], ident[:, :])
                mm.then_inc(t_full, 1)

            def first_product(j, r):
                wait(pe, t_out, j + 1)
                wait(pe, w1_in, (j + 1) * 32)
                for n in range(HT):
                    if not early(j, 1):
                        wait(pe, h_out, (j - 1) * HT + (n + 1))
                    nc.tensor.matmul(PH[n][:, :], W1e[:, r % TURN, n * P:(n + 1) * P], GT_[:, r % 2, :], start=True, stop=True)\
                        .then_inc(h_full, 1)

            def second_product(j, r):
                e = pe.value_load(tile_expert[0:1, bass.ds(j, 1)], min_val=0, max_val=E - 1)
                wait(pe, h_out, (j + 1) * HT)
                if not early(j, 2):
                    wait(pe, y_out, j - 1)
                for i in range(SUB):
                    for n in range(HT):
                        mm = nc.tensor.matmul(PY[r % 2][:, i * P:(i + 1) * P], HG[:, r % 2, n, i * P:(i + 1) * P],
                                              W2T[:, bass.ds(e, 1), n * P:(n + 1) * P].rearrange("p e c -> p (e c)"), start=(n == 0), stop=(n == HT - 1))
                mm.then_inc(y_full, 1)

            def step(k, r):
                if at(r, 1):
                    turn(k - 1, r - 1)
                if at(r, 2):
                    first_product(k - 2, r - 2)
                if at(r, 3):
                    second_product(k - 3, r - 3)

            run(step, pe)


def network(nc, t, out):
    chip = Chip(nc)
    nc.disable_value_cache = True
    chosen = chip.dram("chosen", [N_BATCH, 1], U32)
    E, H, _ = t["L1_ffn_w1"].shape
    sorted_rows = chip.dram("sorted_rows", [E * CAP, ROW], F32)
    with ExitStack() as ctx:
        X = chip.sb(ctx, "X", [P, TILES, C], F32)
        ident = chip.sb(ctx, "ident", [P, P], F32)
        second_less_first = chip.sb(ctx, "second_less_first", [P, TILES], F32)
        next_rows = chip.sb(ctx, "next_rows", [P, E], F32)
        id_zero, id_set = (chip.sem(ctx, n) for n in ("id_zero", "id_set"))
        with nc.Block() as block:
            @block.gpsimd
            def _(pool):
                nc.gpsimd.memset(ident[:, :], 0.0).then_inc(id_zero, 1)
                pool.wait_ge(id_zero, 1)
                nc.gpsimd.affine_select(out=ident[:, :], in_=ident[:, :], compare_op=ALU.not_equal, fill=1.0,
                                        base=0, pattern=[[-1, P]], channel_multiplier=1).then_inc(id_set, 1)
                pool.wait_ge(id_set, 1)
        chip.phase = "attn_"
        attention(nc, chip, X, ident, t["L0_attn_x"], t["L0_attn_qkv_w"], t["L0_attn_qkv_b"],
                  t["L0_attn_proj_w"], t["L0_attn_proj_b"])
        W1T, W2T = (chip.sb(ctx, n, [P, E, H], F32) for n in ("W1T", "W2T"))
        B1 = chip.sb(ctx, "B1", [P, E, H // P], F32)
        chip.phase = "prep_"
        prepare(nc, chip, X, ident, chosen, W1T, W2T, B1, t)
        chip.phase = "mix_"
        mixers(nc, chip, X, ident, chosen, sorted_rows, next_rows, second_less_first, t)
        NT = TOP * TOKENS // E_SLOTS + E - 1
        gates = chip.sb(ctx, "gates", [P, TOP, TILES], F32)
        tile_expert, tile_row = (chip.sb(ctx, n, [1, NT], U32) for n in ("tile_expert", "tile_row"))
        chip.phase = "plan_"
        plan(nc, chip, next_rows, second_less_first, gates, tile_expert, tile_row, sorted_rows, NT)
        chip.phase = "moe_"
        routed_experts(nc, chip, X, ident, sorted_rows, gates, tile_expert, tile_row, W1T, W2T, B1, t["L1_ffn_b2"], out, NT)


_OUT = ((32, 256, 128), "float32")


def kernel(**inputs):
    import numpy as _np
    import concourse.bacc as _bacc
    from concourse import mybir as _mybir
    from concourse.bass_utils import run_bass_kernel_spmd as _run

    nc = _bacc.Bacc("TRN2", target_bir_lowering=False, num_devices=1)
    arrays, args = {}, {}
    for name in sorted(inputs):
        a = _np.ascontiguousarray(inputs[name])
        arrays[f"in_{name}"] = a
        args[name] = nc.dram_tensor(f"in_{name}", a.shape, _mybir.dt.from_np(a.dtype), kind="ExternalInput").ap()
    out = nc.dram_tensor("out_0", _OUT[0], _mybir.dt.from_np(_np.dtype(_OUT[1])), kind="ExternalOutput").ap()
    network(nc, args, out)
    r = _run(nc, [arrays], core_ids=[0])
    return r.results[0]["out_0"]
```

```python
from contextlib import ExitStack

import concourse.bass as bass
from concourse import mybir
from concourse.alu_op_type import AluOpType as ALU

ACT = mybir.ActivationFunctionType
AX = mybir.AxisListType
F32 = mybir.dt.float32
BF16 = mybir.dt.bfloat16
I32 = mybir.dt.int32
U32 = mybir.dt.uint32

P = 128
N_BATCH, SEQ, C = 32, 256, 128
TOKENS = N_BATCH * SEQ
TPG = 4
GT = TPG * P
BPG = GT // SEQ
TPB = SEQ // P
GROUPS = TOKENS // GT
TILES = TOKENS // P

HEADS = 16
HD = C // HEADS
PAIRS = HEADS // 2
HALF = 64
UNITS = BPG * HEADS
MAXU = TPG * PAIRS
LEAD = MAXU - 12
QUAD = 4
QUADS = UNITS // QUAD
FILLS = QUADS // 2
PARTS = 3
RUNS = tuple(PARTS - n for n in range(PARTS))
K_ROWS = HD * sum(RUNS)
C_ROWS = 2
BUFS = 3
VW = P // QUAD
PRB = 8
SCB = 3

E_SLOTS = 256
SUB = E_SLOTS // P
CAP = TOKENS + E_SLOTS
ROW = C + 1
TOP = 2
SHARE = TPG * TOP
BIG = 3.0e38

LN_EPS = 1e-5
LN2_EPS = 1e-6
NEWTON = 3
ONE_PAIR = 1.0 + 0x3F80 / 2.0 ** 23
RSQRT_SEED = 1597463007.0


class Chip:

    def __init__(self, nc):
        self.nc = nc
        self.phase = ""

    def sb(self, ctx, name, shape, dt):
        return ctx.enter_context(self.nc.sbuf_tensor(self.phase + name, shape, dt))

    def ps(self, ctx, name, shape, dt=F32):
        return ctx.enter_context(self.nc.psum_tensor(self.phase + name, shape, dt))

    def sem(self, ctx, name):
        return ctx.enter_context(self.nc.semaphore(name))

    def dram(self, name, shape, dt):
        return self.nc.dram_tensor(name, shape, dt, kind="Internal").ap()


class Routed:

    def __init__(self, chip, ctx, E, H):
        self.w1, self.w2 = chip.sb(ctx, "w1_raw", [P, E, H // P, C], F32), chip.sb(ctx, "w2_raw", [P, E, H], F32)
        self.norm_rows, self.bias_rows = chip.sb(ctx, "norm_rows", [E, 2, C], F32), chip.sb(ctx, "bias_rows", [E, H], F32)
        self.rows_in = chip.sem(ctx, "routed_rows_in")
        self.expert_in = [chip.sem(ctx, f"routed_expert_in{e}") for e in range(E)]
        self.W1T, self.W2T = (chip.sb(ctx, n, [P, E, H], F32) for n in ("W1T", "W2T"))
        self.B1 = chip.sb(ctx, "B1", [P, E, H // P], F32)


class Tables:

    def __init__(self, chip, ctx, t):
        E, _, F = t["L0_ffn_W1"].shape
        FT, ER = F // P, t["L1_ffn_router_w"].shape[0]

        def sb(name, shape):
            return chip.sb(ctx, name, shape, F32)

        self.brow, self.Wo, self.bo = sb("brow", [E, FT + 1, P]), sb("Wo", [P, C]), sb("bo", [P, C])
        self.Wraw, self.rw, self.rbr = sb("Wraw", [P, 3, C]), sb("rw", [ER, C]), sb("rbr", [P, ER])
        self.tmv, self.tmr, self.dec, self.rls, self.rlb = (sb(n, [P, 1]) for n in ("tmv", "tmr", "dec", "rls", "rlb"))
        self.loads = [
            (self.brow[:, 0:FT, :], t["L0_ffn_b1"].rearrange("e (n p) -> e n p", n=FT)),
            (self.brow[:, FT, :], t["L0_ffn_b2"]), (self.Wo[:, :], t["L0_ffn_Wo"]),
            (self.bo[:, :], rows(t["L0_ffn_bo"])), (self.Wraw[:, 0, :], t["L1_attn_Wv"]),
            (self.Wraw[:, 1, :], t["L1_attn_Wr"]), (self.Wraw[:, 2, :], t["L1_attn_Wo"]),
            (self.tmv[:, :], column(t["L1_attn_time_mix_v"])), (self.tmr[:, :], column(t["L1_attn_time_mix_r"])),
            (self.dec[:, :], column(t["L1_attn_time_decay"])), (self.rw[:, :], t["L1_ffn_router_w"]),
            (self.rls[:, :], column(t["L1_ffn_router_ln_scale"])), (self.rlb[:, :], column(t["L1_ffn_router_ln_bias"])),
            (self.rbr[:, :], rows(t["L1_ffn_router_b"]))]
        self.w_in = chip.sem(ctx, "tables_in")


def rows(v):
    return bass.AP(tensor=v.tensor, offset=v.offset, ap=[[0, P]] + [list(x) for x in v.ap])


def column(v):
    return v.rearrange("(p a) -> p a", a=1)


def wait(eng, sem, count):
    if isinstance(count, int):
        eng.wait_ge(sem, count)
        return
    held = eng.to_reg(count)
    eng.wait_ge(sem, held)
    eng.free_register(held)


def wait_apart(eng, always, sem, count):
    if isinstance(count, int):
        eng.wait_ge(sem, count)
        return
    held = eng.to_reg(count)
    eng.wait_ge(always, 1)
    eng.wait_ge(sem, held)
    eng.free_register(held)


def newton_rsqrt(eng, always, sem, done, y, var, tmp):
    for n in range(NEWTON):
        eng.tensor_tensor(tmp[:, 2 * n], y[:, n], y[:, n], ALU.mult).then_inc(sem, 1)
        done += 1
        wait_apart(eng, always, sem, done)
        eng.tensor_tensor(tmp[:, 2 * n + 1], tmp[:, 2 * n], var, ALU.mult).then_inc(sem, 1)
        done += 1
        wait_apart(eng, always, sem, done)
        eng.tensor_scalar(tmp[:, 2 * n], tmp[:, 2 * n + 1], -0.5, 1.5, ALU.mult, ALU.add).then_inc(sem, 1)
        done += 1
        wait_apart(eng, always, sem, done)
        eng.tensor_tensor(y[:, n + 1], y[:, n], tmp[:, 2 * n], ALU.mult).then_inc(sem, 1)
        done += 1
        wait_apart(eng, always, sem, done)
    return done


NEWTON_OPS = 4 * NEWTON


def attention(nc, chip, X, ident, x_in, qkv_w, qkv_b, proj_w, proj_b):
    qscale = float(HD) ** -0.5
    with ExitStack() as ctx:
        def sb(name, shape, dt=F32):
            return chip.sb(ctx, name, shape, dt)

        Wqkv, Wproj = sb("Wqkv", [P, 3 * C]), sb("Wproj", [P, C])
        Wqk = sb("Wqk", [P, 2, C])
        qb, qbs, kb = sb("qb", [P, 1]), sb("qbs", [P, 1]), sb("kb", [P, 1])
        vb, pb = sb("vb", [P, C]), sb("pb", [P, C])
        QP, KP = sb("QP", [P, BUFS, 2, PAIRS, GT], BF16), sb("KP", [P, BUFS, PAIRS, GT], BF16)
        V = sb("V", [P, BUFS, TPG, HEADS, VW])
        Xs, XN = sb("Xs", [P, TPG, C]), sb("XN", [P, TPG, C])
        stat, mv = sb("stat", [P, TPG, 6]), sb("mv", [P, TPG, 2])
        var = sb("var", [P, TPG])
        ny, ntmp = sb("ny", [P, NEWTON + 1, TPG]), sb("ntmp", [P, 2 * NEWTON, TPG])
        XNT, OT = sb("XNT", [P, GT]), sb("OT", [P, GT])
        qf, kf, qr, kr = (sb(n, [P, GT]) for n in ("qf", "kf", "qr", "kr"))
        QS, KS = (sb(n, [P, PARTS, GT], BF16) for n in ("QS", "KS"))
        MX = sb("MX", [P, BUFS, TPG, HEADS])
        CM = sb("CM", [P, TPG, C_ROWS, HEADS])
        CB = sb("CB", [P, TPG, HEADS], BF16)
        CT = sb("CT", [C_ROWS * HEADS, GT], BF16)
        PR = sb("PR", [P, PRB, GT])
        PVS, REC = sb("PVS", [P, 2, GT]), sb("REC", [P, TPB, 2, QUAD])
        O = sb("O", [P, TPG, HEADS, HD])

        QD, KD = (chip.dram(n, [GROUPS, PARTS, 2, HD, PAIRS, GT], BF16) for n in ("q_parts", "k_parts"))
        CD = chip.dram("shift_rows", [GROUPS, C_ROWS, HEADS, GT], BF16)

        SC = [chip.ps(ctx, f"score{i}", [P, GT]) for i in range(SCB)]
        PM = [chip.ps(ctx, f"smax{i}", [P, GT]) for i in range(2)]
        PV = [chip.ps(ctx, f"pv{i}", [P, GT]) for i in range(2)]
        MB = chip.ps(ctx, "mb", [P, GT])

        def sem(name):
            return chip.sem(ctx, "a_" + name)

        weights_in, ones_set, kones_set, zeros_set, qbs_set, wqk_set = (
            sem(n) for n in ("weights_in", "ones", "kones", "zeros", "qbs", "wqk"))
        x_chunk = [sem(f"x_chunk{i}") for i in range(3)]
        xs_copied, stats, aggr, newton, xn_done, x_biased = (
            sem(n) for n in ("xs", "stats", "aggr", "newton", "xn", "xbias"))
        xnt_full, xnt_out, q_full, q_out, k_full, k_out, v_full, v_out = (
            sem(n) for n in ("xnt_full", "xnt_out", "q_full", "q_out", "k_full", "k_out", "v_full", "v_out"))
        splits, parts_ready, parts_stored, packed = (sem(n) for n in ("splits", "parts", "stored", "packed"))
        max_full, max_out, shift, ct_full, ct_out, ct_stored, shifted = (
            sem(n) for n in ("max_full", "max_out", "shift", "ct_full", "ct_out", "ct_stored", "shifted"))
        score_full, exp_out, pv_full, pv_out, pvt_full, recs, o_out = (
            sem(n) for n in ("score_full", "exp_out", "pv_full", "pv_out", "pvt_full", "recs", "o_out"))
        ot_full, ot_out, proj_full, x_added = (sem(n) for n in ("ot_full", "ot_out", "proj_full", "x_added"))

        N_PACK = 2 * 2 * PARTS
        X_CHUNKS = ((0, 1), (1, 3), (3, GROUPS))

        def tile_cols(t):
            return slice(t * P, (t + 1) * P)

        def run(steps, eng):
            steps(0, 0)
            n = (GROUPS - 3 - 1) // BUFS
            with eng.Fori(0, n) as i:
                for r in range(BUFS):
                    steps(i * BUFS + (1 + r), 1 + r)
            for g in range(1 + n * BUFS, GROUPS):
                steps(g, g)

        def last(r, ahead):
            return r + ahead >= GROUPS

        block = ctx.enter_context(nc.Block())

        @block.sync
        def _(sp):
            xv = x_in.rearrange("b (t p) c -> p (b t) c", p=P)

            def load_x(n):
                a, b = X_CHUNKS[n]
                sp.dma_start(X[:, a * TPG:b * TPG, :], xv[:, a * TPG:b * TPG, :]).then_inc(x_chunk[n], 16)

            load_x(0)
            for dst, src in ((Wqkv[:, :], qkv_w), (Wproj[:, :], proj_w), (vb[:, :], rows(qkv_b[2 * C:3 * C])),
                             (pb[:, :], rows(proj_b))):
                sp.dma_start(dst, src).then_inc(weights_in, 16)
            for n, dst in enumerate((qb, kb)):
                for half in range(2):
                    src = qkv_b[n * C:(n + 1) * C].rearrange("(j i d a) -> i d j a", i=2, d=HD, a=1)[half]
                    sp.dma_start(dst[half * HALF:(half + 1) * HALF, :], src, allow_slow_non_contiguous=True).then_inc(weights_in, 16)
            load_x(1)
            load_x(2)

            def store(g):
                sp.wait_ge(parts_ready, (g + 1) * 2)
                for part, d in ((QS, QD), (KS, KD)):
                    sp.dma_start(d[bass.ds(g, 1)].rearrange("g s i d j t -> (i d j) (g s) t"), part[:, :, :])\
                        .then_inc(parts_stored, 16)

            def pack(g, buf):
                sp.wait_ge(parts_stored, (g + 1) * 32)
                for half in range(2):
                    at = HALF * half
                    for n, run_ in enumerate(RUNS):
                        q_parts = QD[bass.ds(g, 1), 0:run_, half].rearrange("g s d j t -> (g s) d (j t)")
                        k_part = KD[bass.ds(g, 1), n, half].rearrange("g d j t -> g d (j t)")\
                            .to_broadcast([run_, HD, PAIRS * GT])
                        sp.dma_start(QP[at:at + HD * run_, buf, half].rearrange("p j t -> p (j t)"), q_parts)\
                            .then_inc(packed, 16)
                        sp.dma_start(KP[at:at + HD * run_, buf].rearrange("p j t -> p (j t)"), k_part)\
                            .then_inc(packed, 16)
                        at += HD * run_

            def shift_out(g):
                sp.wait_ge(ct_out, g + 1)
                sp.dma_start(CD[bass.ds(g, 1)].rearrange("g r h t -> (g r h) t"), CT[:, :]).then_inc(ct_stored, 16)

            def shift_in(g, buf):
                sp.wait_ge(ct_stored, (g + 1) * 16)
                for half in range(2):
                    src = CD[bass.ds(g, 1)].rearrange("g r (j i) t -> i (g r) j t", i=2)[half]
                    at = HALF * half + K_ROWS
                    sp.dma_start(QP[at:at + C_ROWS, buf, half], src).then_inc(shifted, 16)

            for g in range(2):
                store(g)
                sp.wait_ge(kones_set, g + 1)
                sp.wait_ge(zeros_set, g + 1)
                pack(g, g)
                if g == 1:
                    shift_out(0)
                sp.wait_ge(packed, (g + 1) * 16 * N_PACK)
            shift_in(0, 0)
            store(2)
            sp.wait_ge(kones_set, BUFS)
            sp.wait_ge(zeros_set, BUFS)

            def step(g, r):
                if not last(r, 2):
                    wait_apart(sp, kones_set, score_full, g * UNITS)
                    pack(g + 2, (r + 2) % BUFS)
                    sp.wait_ge(packed, (g + 3) * (16 * N_PACK))
                if not last(r, 1):
                    shift_out(g + 1)
                    shift_in(g + 1, (r + 1) % BUFS)
                if not last(r, 3):
                    store(g + 3)
                if not last(r, 1):
                    wait_apart(sp, kones_set, shifted, (g + 2) * 32)

            run(step, sp)

        @block.gpsimd
        def _(pool):
            nc.gpsimd.memset(V[:, :, :, :, HD:VW], 1.0).then_inc(ones_set, 1)

            def norm(g, chunk=None):
                if chunk is not None:
                    wait_apart(pool, ones_set, x_chunk[chunk], 16)
                if not (isinstance(g, int) and g == 0):
                    wait_apart(pool, ones_set, xn_done, g * TPG)
                nc.gpsimd.tensor_copy(Xs[:, :, :], X[:, bass.ds(g * TPG, TPG), :]).then_inc(xs_copied, 1)
                wait_apart(pool, ones_set, xs_copied, g + 1)
                nc.gpsimd.tensor_tensor(X[:, bass.ds(g * TPG, TPG), :], Xs[:, :, :],
                                        pb[:, :].unsqueeze(1).to_broadcast([P, TPG, C]), ALU.add).then_inc(x_biased, 1)
                wait_apart(pool, ones_set, aggr, (g + 1) * TPG)
                base = g * (NEWTON_OPS + 2)
                nc.gpsimd.tensor_scalar(var[:, :], mv[:, :, 1], LN_EPS, None, ALU.add).then_inc(newton, 1)
                wait_apart(pool, ones_set, newton, base + 1)
                nc.gpsimd.tensor_scalar(ny[:, 0, :].bitcast(I32), var[:, :].bitcast(I32), -0.5, RSQRT_SEED,
                                        ALU.mult, ALU.add).then_inc(newton, 1)
                wait_apart(pool, ones_set, newton, base + 2)
                newton_rsqrt(nc.gpsimd, ones_set, newton, base + 2, ny, var[:, :], ntmp)

            def split(g):
                for n, (full, f, rem, part) in enumerate(((q_out, qf, qr, QS), (k_out, kf, kr, KS))):
                    base = g * 4 + 2 * n
                    wait_apart(pool, ones_set, full, (g + 1) * 2)
                    nc.gpsimd.tensor_tensor(rem[:, :], f[:, :], part[:, 0, :], ALU.subtract).then_inc(splits, 1)
                    wait_apart(pool, ones_set, splits, base + 1)
                    nc.gpsimd.tensor_copy(part[:, 1, :], rem[:, :]).then_inc(splits, 1)
                    wait_apart(pool, ones_set, splits, base + 2)
                    nc.gpsimd.tensor_tensor(part[:, 2, :], rem[:, :], part[:, 1, :], ALU.subtract)\
                        .then_inc(parts_ready, 1)

            def split_max(g, buf):
                wait_apart(pool, ones_set, max_out, (g + 1) * MAXU)
                wait_apart(pool, ones_set, ct_full, g)
                nc.gpsimd.tensor_scalar(CB[:, :, :], MX[:, buf, :, :], -1.0, None, ALU.mult).then_inc(shift, 1)
                wait_apart(pool, ones_set, shift, g * 4 + 1)
                nc.gpsimd.tensor_scalar(CM[:, :, 0, :], CB[:, :, :], 1.0, None, ALU.mult).then_inc(shift, 1)
                wait_apart(pool, ones_set, shift, g * 4 + 2)
                nc.gpsimd.tensor_tensor(CM[:, :, 1, :], MX[:, buf, :, :], CM[:, :, 0, :], ALU.add).then_inc(shift, 1)
                wait_apart(pool, ones_set, shift, g * 4 + 3)
                nc.gpsimd.tensor_scalar(CM[:, :, 1, :], CM[:, :, 1, :], -1.0, None, ALU.mult).then_inc(shift, 1)

            pool.wait_ge(ones_set, 1)
            pool.wait_ge(weights_in, 128)
            norm(0, 0)
            for buf in range(BUFS):
                nc.gpsimd.memset(KP[:, buf].rearrange("p j t -> p (j t)").bitcast(F32), ONE_PAIR).then_inc(kones_set, 1)
            split(0)
            norm(1, 1)
            split(1)
            norm(2, 1)
            split_max(0, 0)
            split(2)

            def step(g, r):
                if not last(r, 3):
                    norm(g + 3, 2 if r == 0 else None)
                if not last(r, 1):
                    split_max(g + 1, (r + 1) % BUFS)
                if not last(r, 3):
                    split(g + 3)

            run(step, pool)

        @block.scalar
        def _(act):
            act.wait_ge(weights_in, 128)
            nc.scalar.mul(qbs[:, :], qb[:, :], qscale).then_inc(qbs_set, 1)
            act.wait_ge(qbs_set, 1)
            for n in range(2):
                nc.scalar.copy(Wqk[:, n, :].rearrange("p (i d j) -> p i d j", i=2, d=HD),
                               Wqkv[:, n * C:(n + 1) * C].rearrange("p (j i d) -> p i d j", i=2, d=HD))\
                    .then_inc(wqk_set, 1)

            def xnt(g):
                act.wait_ge(xnt_full, g + 1)
                act.wait_ge(v_full, g)
                nc.scalar.copy(XNT[:, :], MB[:, :]).then_inc(xnt_out, 1)

            def q_k(g, full, f, part, out, bias, scale):
                act.wait_ge(full, g + 1)
                act.wait_ge(parts_ready, g * 2)
                nc.scalar.activation(f[:, :], MB[:, :], ACT.Identity, bias=bias[:, 0:1], scale=scale).then_inc(out, 1)
                act.wait_ge(parts_stored, g * 32)
                nc.scalar.activation(part[:, 0, :], MB[:, :], ACT.Identity, bias=bias[:, 0:1], scale=scale)\
                    .then_inc(out, 1)

            def q(g):
                q_k(g, q_full, qf, QS, q_out, qbs, qscale)

            def k(g):
                q_k(g, k_full, kf, KS, k_out, kb, 1.0)

            def ct(g):
                act.wait_ge(ct_full, g + 1)
                act.wait_ge(ct_stored, g * 16)
                nc.scalar.copy(CT[:, :], MB[0:C_ROWS * HEADS, :]).then_inc(ct_out, 1)

            def ot(g):
                act.wait_ge(ot_full, g + 1)
                act.wait_ge(proj_full, g)
                nc.scalar.copy(OT[:, :], MB[:, :]).then_inc(ot_out, 1)

            def exps(g, u, r):
                act.wait_ge(score_full, g * UNITS + (u + 1))
                if u % QUAD == 0 and not (isinstance(g, int) and g * UNITS + u < PRB):
                    act.wait_ge(pv_full, g * QUADS + ((u - PRB) // QUAD + 1))
                nc.scalar.activation(PR[:, u % PRB, :], SC[(r * UNITS + u) % SCB][:, :], ACT.Exp).then_inc(exp_out, 1)

            def sums(g, f):
                act.wait_ge(pv_full, g * QUADS + 2 * (f + 1))
                if not (isinstance(g, int) and g * FILLS + f < 2):
                    act.wait_ge(pvt_full, g * FILLS + (f - 1))
                nc.scalar.copy(PVS[:, f % 2, :], PV[f % 2][:, :]).then_inc(pv_out, 1)

            for g in range(3):
                xnt(g)
                q(g)
                k(g)
                if g == 1:
                    ct(0)

            def step(g, r):
                for u in range(UNITS):
                    exps(g, u, r)
                    if u == 3 and r > 0:
                        sums(g - 1, FILLS - 1)
                    if u in (11, 19, 27):
                        sums(g, (u - 11) // 8)
                    if u == 9 and r > 0:
                        ot(g - 1)
                    if not last(r, 3):
                        if u == 16:
                            xnt(g + 3)
                        if u == 18:
                            q(g + 3)
                        if u == 21:
                            k(g + 3)
                    if u == 23 and not last(r, 1):
                        ct(g + 1)

            run(step, act)
            sums(GROUPS - 1, FILLS - 1)
            ot(GROUPS - 1)

        @block.vector
        def _(dve):
            nc.vector.memset(QP[:, 0].rearrange("p i j t -> p (i j t)").bitcast(F32), 0.0).then_inc(zeros_set, 1)

            def norm_stats(g, t):
                if t == 0:
                    dve.wait_ge(xs_copied, g + 1)
                    dve.wait_ge(xn_done, g * TPG)
                nc.vector.bn_stats(stat[:, t, :], Xs[:, t, :]).then_inc(stats, 1)
                wait_apart(dve, ones_set, stats, g * TPG + (t + 1))
                nc.vector.bn_aggr(mv[:, t, :], stat[:, t, :]).then_inc(aggr, 1)

            def normed(g):
                dve.wait_ge(newton, (g + 1) * (NEWTON_OPS + 2))
                if not (isinstance(g, int) and g == 0):
                    dve.wait_ge(xnt_full, g)
                for t in range(TPG):
                    nc.vector.tensor_scalar(XN[:, t, :], Xs[:, t, :], mv[:, t, 0:1], ny[:, NEWTON, t:t + 1],
                                            ALU.subtract, ALU.mult).then_inc(xn_done, 1)

            def values(g, buf):
                if not (isinstance(g, int) and g < BUFS):
                    dve.wait_ge(pv_full, (g - BUFS + 1) * QUADS)
                dve.wait_ge(v_full, g + 1)
                nc.vector.tensor_tensor(
                    V[:, buf, :, :, 0:HD], MB[:, :].rearrange("p (t h d) -> p t h d", t=TPG, h=HEADS),
                    vb[:, :].rearrange("p (h d) -> p h d", h=HEADS).unsqueeze(1).to_broadcast([P, TPG, HEADS, HD]),
                    ALU.add).then_inc(v_out, 1)

            def row_max(g, w, buf):
                t, j = divmod(w, PAIRS)
                dve.wait_ge(max_full, g * MAXU + (w + 1))
                if w == 0 and not (isinstance(g, int) and g < BUFS):
                    dve.wait_ge(shift, (g - BUFS + 1) * 4)
                nc.vector.tensor_reduce(MX[:, buf, t, 2 * j:2 * j + 2], PM[w % 2][:, :].rearrange("p (h m) -> p h m", h=2),
                                        AX.X, ALU.max).then_inc(max_out, 1)

            def heads(g, f):
                b, half = divmod(f, 2)
                sums = MB[:, :].rearrange("p (n q c w) -> p n q c w", n=TPB, q=2, c=QUAD)
                dve.wait_ge(pvt_full, g * FILLS + (f + 1))
                nc.vector.reciprocal(REC[:, :, :, :], sums[:, :, :, :, HD]).then_inc(recs, 1)
                if f == 0 and not (isinstance(g, int) and g == 0):
                    dve.wait_ge(ot_full, g)
                dve.wait_ge(recs, g * FILLS + (f + 1))
                for n in range(TPB):
                    nc.vector.tensor_tensor(
                        O[:, b * TPB + n, 2 * QUAD * half:2 * QUAD * (half + 1), :].rearrange("p (q c) d -> p q c d", q=2),
                        sums[:, n, :, :, 0:HD], REC[:, n, :, :].unsqueeze(3).to_broadcast([P, 2, QUAD, HD]),
                        ALU.mult).then_inc(o_out, 1)

            def residual(g):
                dve.wait_ge(proj_full, g + 1)
                xg = X[:, bass.ds(g * TPG, TPG), :]
                nc.vector.tensor_tensor(xg, xg, MB[:, :].rearrange("p (t c) -> p t c", t=TPG), ALU.add)\
                    .then_inc(x_added, 1)

            dve.wait_ge(weights_in, 128)
            dve.wait_ge(ones_set, 1)
            for t in range(TPG):
                norm_stats(0, t)
            normed(0)
            for buf in range(1, BUFS):
                nc.vector.memset(QP[:, buf].rearrange("p i j t -> p (i j t)").bitcast(F32), 0.0).then_inc(zeros_set, 1)
            values(0, 0)
            for t in range(TPG):
                norm_stats(1, t)
            normed(1)
            for w in range(MAXU):
                row_max(0, w, 0)
                if w == 14:
                    values(1, 1)
                if w == 24:
                    for t in range(TPG):
                        norm_stats(2, t)
            normed(2)
            for w in range(LEAD):
                row_max(1, w, 1)

            def step(g, r):
                for u in range(UNITS):
                    if u < MAXU - LEAD:
                        if not last(r, 1):
                            row_max(g + 1, u + LEAD, (r + 1) % BUFS)
                    elif not last(r, 2):
                        row_max(g + 2, u + LEAD - MAXU, (r + 2) % BUFS)
                    if u == 3 and not last(r, 2):
                        values(g + 2, (r + 2) % BUFS)
                    if u in (0, 1, 2, 4) and not last(r, 3):
                        norm_stats(g + 3, (0, 1, 2, 4).index(u))
                    if u == 10 and not last(r, 3):
                        normed(g + 3)
                    if u == 5 and r > 0:
                        heads(g - 1, FILLS - 1)
                    if u == 11 and r > 0:
                        residual(g - 1)
                    if u in (14, 25, 29):
                        heads(g, (14, 25, 29).index(u))

            run(step, dve)
            heads(GROUPS - 1, FILLS - 1)
            residual(GROUPS - 1)

        @block.tensor
        def _(pe):
            def xnt(g, free, count):
                wait(pe, xn_done, (g + 1) * TPG)
                if free is not None:
                    wait(pe, free, count)
                for t in range(TPG):
                    mm = nc.tensor.transpose(MB[:, tile_cols(t)], XN[:, t, :], ident[:, :])
                mm.then_inc(xnt_full, 1)

            def q(g):
                wait(pe, xnt_out, g + 1)
                nc.tensor.matmul(MB[:, :], Wqk[:, 0, :], XNT[:, :], start=True, stop=True).then_inc(q_full, 1)

            def k(g, free, count):
                wait(pe, free, count)
                nc.tensor.matmul(MB[:, :], Wqk[:, 1, :], XNT[:, :], start=True, stop=True).then_inc(k_full, 1)

            def v(g, free, count):
                wait(pe, free, count)
                for t in range(TPG):
                    mm = nc.tensor.matmul(MB[:, tile_cols(t)], XNT[:, tile_cols(t)], Wqkv[:, 2 * C:3 * C],
                                          start=True, stop=True)
                mm.then_inc(v_full, 1)

            def max_scores(g, w, buf):
                t, j = divmod(w, PAIRS)
                b = t // TPB
                if w == 0:
                    wait(pe, packed, (g + 1) * (16 * N_PACK))
                if not (isinstance(g, int) and g * MAXU + w < 2):
                    wait(pe, max_out, g * MAXU + (w - 1))
                for i in range(2):
                    mm = nc.tensor.matmul(PM[w % 2][:, i * SEQ:(i + 1) * SEQ], QP[:, buf, i, j, tile_cols(t)],
                                          KP[:, buf, j, b * SEQ:(b + 1) * SEQ], start=True, stop=True)
                mm.then_inc(max_full, 1)

            def scores(g, u, r):
                b, h = divmod(u, HEADS)
                buf = r % BUFS
                if u == 0:
                    wait(pe, shifted, (g + 1) * 32)
                if not (isinstance(g, int) and g * UNITS + u < SCB):
                    wait(pe, exp_out, g * UNITS + (u + 1 - SCB))
                for m in range(TPB):
                    mm = nc.tensor.matmul(SC[(r * UNITS + u) % SCB][:, m * SEQ:(m + 1) * SEQ],
                                          KP[:, buf, h // 2, tile_cols(b * TPB + m)],
                                          QP[:, buf, h % 2, h // 2, b * SEQ:(b + 1) * SEQ], start=True, stop=True)
                mm.then_inc(score_full, 1)

            def pv(g, n, buf):
                b, q = divmod(n, QUADS // BPG)
                wait(pe, exp_out, g * UNITS + (n + 1) * QUAD)
                if n == 0:
                    wait(pe, v_out, g + 1)
                if n % 2 == 0 and not (isinstance(g, int) and g * FILLS + n // 2 < 2):
                    wait(pe, pv_out, g * FILLS + (n // 2 - 1))
                for m in range(TPB):
                    for c in range(QUAD):
                        mm = nc.tensor.matmul(
                            PV[n // 2 % 2][c * VW:(c + 1) * VW, n % 2 * SEQ:(n % 2 + 1) * SEQ],
                            V[:, buf, b * TPB + m, q * QUAD + c, :],
                            PR[:, (n * QUAD + c) % PRB, m * SEQ:(m + 1) * SEQ],
                            start=(m == 0), stop=(m == TPB - 1), tile_position=(0, c * VW), skip_group_check=True)
                mm.then_inc(pv_full, 1)

            def pvt(g, f, free, count):
                wait(pe, pv_out, g * FILLS + (f + 1))
                wait(pe, free, count)
                for n in range(TPB):
                    for q in range(2):
                        mm = nc.tensor.transpose(MB[:, tile_cols(2 * n + q)],
                                                 PVS[:, f % 2, q * SEQ + n * P:q * SEQ + (n + 1) * P], ident[:, :])
                mm.then_inc(pvt_full, 1)

            def ct(g, free, count):
                wait(pe, shift, (g + 1) * 4)
                wait(pe, free, count)
                for t in range(TPG):
                    mm = nc.tensor.transpose(MB[0:C_ROWS * HEADS, tile_cols(t)],
                                             CM[:, t, :, :].rearrange("p r h -> p (r h)"), ident[:, :])
                mm.then_inc(ct_full, 1)

            def ot(g, free, count):
                wait(pe, o_out, (g + 1) * TPB * FILLS)
                wait(pe, free, count)
                for t in range(TPG):
                    mm = nc.tensor.transpose(MB[:, tile_cols(t)], O[:, t, :, :].rearrange("p h d -> p (h d)"),
                                             ident[:, :])
                mm.then_inc(ot_full, 1)

            def proj(g):
                wait(pe, ot_out, g + 1)
                for t in range(TPG):
                    mm = nc.tensor.matmul(MB[:, tile_cols(t)], OT[:, tile_cols(t)], Wproj[:, :], start=True, stop=True)
                mm.then_inc(proj_full, 1)

            wait(pe, weights_in, 128)
            wait(pe, wqk_set, 2)
            xnt(0, None, 0)
            q(0)
            k(0, q_out, 2)
            v(0, k_out, 2)
            xnt(1, v_out, 1)
            for w in range(MAXU):
                max_scores(0, w, 0)
                if w == 3:
                    q(1)
                if w == 7:
                    k(1, q_out, 4)
                if w == 11:
                    v(1, k_out, 4)
            ct(0, v_out, 2)
            for w in range(LEAD):
                max_scores(1, w, 1)
                if w == 0:
                    xnt(2, ct_out, 1)
                if w == 3:
                    q(2)
                if w == 7:
                    k(2, q_out, 6)

            def step(g, r):
                n_o = TPB * FILLS
                for u in range(UNITS):
                    scores(g, u, r)
                    if u == 2 and r > 0:
                        pv(g - 1, QUADS - 1, (r - 1) % BUFS)
                    if u % QUAD == 2 and u > QUAD:
                        pv(g, u // QUAD - 1, r % BUFS)
                    if u < MAXU - LEAD:
                        if not last(r, 1):
                            max_scores(g + 1, u + LEAD, (r + 1) % BUFS)
                    elif not last(r, 2):
                        max_scores(g + 2, u + LEAD - MAXU, (r + 2) % BUFS)
                    if u == 1 and not last(r, 2):
                        if r > 0:
                            v(g + 2, o_out, (g - 1) * n_o + 3 * TPB)
                        else:
                            v(g + 2, k_out, 6)
                    if u == 5 and r > 0:
                        pvt(g - 1, FILLS - 1, *((v_out, g + 3) if not last(r, 2) else (o_out, (g - 1) * n_o + 3 * TPB)))
                    if u == 8 and r > 0:
                        ot(g - 1, o_out, g * n_o)
                    if u == 11 and r > 0:
                        proj(g - 1)
                    if u == 13:
                        pvt(g, 0, *((x_added, g) if r > 0 else (v_out, 3)))
                    if u == 16 and not last(r, 3):
                        xnt(g + 3, o_out, g * n_o + TPB)
                    if u == 18 and not last(r, 3):
                        q(g + 3)
                    if u == 21 and not last(r, 3):
                        k(g + 3, q_out, 2 * (g + 4))
                    if u == 23 and not last(r, 1):
                        ct(g + 1, *((k_out, 2 * (g + 4)) if not last(r, 3) else (o_out, g * n_o + TPB)))
                    if u == 25:
                        pvt(g, 1, *((ct_out, g + 2) if not last(r, 1) else (o_out, g * n_o + TPB)))
                    if u == 29:
                        pvt(g, 2, o_out, g * n_o + 2 * TPB)

            run(step, pe)
            g = GROUPS - 1
            pv(g, QUADS - 1, g % BUFS)
            pvt(g, FILLS - 1, o_out, TPB * (FILLS * g + 3))
            ot(g, o_out, TPB * FILLS * GROUPS)
            proj(g)


def choose_experts(nc, chip, X, ident, chosen, tables, t):
    Wp1d, bp1, Wp2d, bp2 = t["L0_ffn_Wp1"], t["L0_ffn_bp1"], t["L0_ffn_Wp2"], t["L0_ffn_bp2"]
    EB = Wp2d.shape[1]
    with ExitStack() as ctx:
        def sb(name, shape, dt=F32):
            return chip.sb(ctx, name, shape, dt)

        Wp1, Wp2, b1c, b2r = sb("Wp1", [C, C]), sb("Wp2", [C, EB]), sb("bp1c", [C, 1]), sb("bp2r", [P, EB])
        L, LN = sb("L", [N_BATCH, C]), sb("LN", [N_BATCH, C])
        LT, NT = sb("LT", [C, N_BATCH]), sb("NT", [C, N_BATCH])
        stat, mv, var = sb("nstat", [N_BATCH, 6]), sb("nmv", [N_BATCH, 2]), sb("nvar", [N_BATCH, 1])
        ny, ntmp = sb("nny", [N_BATCH, NEWTON + 1, 1]), sb("nntmp", [N_BATCH, 2 * NEWTON, 1])
        logits, best, index = sb("logits", [N_BATCH, EB]), sb("best", [N_BATCH, 8]), sb("index", [N_BATCH, 8], U32)
        last_rows = chip.dram("last_rows", [N_BATCH, C], F32)
        PT, PN = (chip.ps(ctx, n, [P, GT]) for n in ("npt", "npn"))
        (w_in, rows_out, rows_in, chain, newton, t_full, t_out, n_full, n_out, l_full, found, stored) = (
            chip.sem(ctx, "n_" + n) for n in ("w_in rows_out rows_in chain newton t_full t_out n_full n_out l_full "
                                              "found stored").split())
        block = ctx.enter_context(nc.Block())

        @block.sync
        def _(sp):
            for dst, src in ((Wp1[:, :], Wp1d), (Wp2[:, :], Wp2d), (b1c[:, :], column(bp1)), (b2r[:, :], rows(bp2))):
                sp.dma_start(dst, src).then_inc(w_in, 16)
            sp.dma_start(last_rows.rearrange("(a b) c -> a b c", a=1), X[P - 1:P, TPB - 1::TPB, :]).then_inc(rows_out, 16)
            sp.wait_ge(rows_out, 16)
            sp.dma_start(L[:, :], last_rows).then_inc(rows_in, 16)
            for dst, src in tables.loads:
                sp.dma_start(dst, src).then_inc(tables.w_in, 16)
            sp.wait_ge(found, 1)
            sp.dma_start(chosen, index[:, 0:1]).then_inc(stored, 16)
            sp.wait_ge(stored, 16)

        @block.vector
        def _(dve):
            dve.wait_ge(w_in, 64)
            dve.wait_ge(rows_in, 16)
            nc.vector.bn_stats(stat[:, :], L[:, :]).then_inc(chain, 1)
            dve.wait_ge(chain, 1)
            nc.vector.bn_aggr(mv[:, :], stat[:, :]).then_inc(chain, 1)
            dve.wait_ge(chain, 2)
            nc.vector.tensor_scalar(var[:, :], mv[:, 1:2], LN_EPS, None, ALU.add).then_inc(chain, 1)
            dve.wait_ge(chain, 3)
            nc.vector.tensor_scalar(ny[:, 0, :].bitcast(I32), var[:, :].bitcast(I32), -0.5, RSQRT_SEED,
                                    ALU.mult, ALU.add).then_inc(newton, 1)
            dve.wait_ge(newton, 1)
            newton_rsqrt(nc.vector, w_in, newton, 1, ny, var[:, :], ntmp)
            nc.vector.tensor_scalar(LN[:, :], L[:, :], mv[:, 0:1], ny[:, NEWTON, 0:1], ALU.subtract, ALU.mult)\
                .then_inc(chain, 1)
            dve.wait_ge(t_full, 1)
            nc.vector.tensor_copy(LT[:, :], PT[:, 0:N_BATCH]).then_inc(t_out, 1)
            dve.wait_ge(l_full, 1)
            nc.vector.tensor_tensor(logits[:, :], PT[0:N_BATCH, 0:EB], b2r[0:N_BATCH, :], ALU.add).then_inc(chain, 1)
            dve.wait_ge(chain, 5)
            nc.vector.max(best[:, :], logits[:, :]).then_inc(chain, 1)
            dve.wait_ge(chain, 6)
            nc.vector.max_index(index[:, :], best[:, :], logits[:, :]).then_inc(found, 1)

        @block.scalar
        def _(act):
            act.wait_ge(w_in, 64)
            act.wait_ge(n_full, 1)
            nc.scalar.activation(NT[:, :], PN[:, 0:N_BATCH], ACT.Gelu, bias=b1c[:, 0:1]).then_inc(n_out, 1)

        @block.tensor
        def _(pe):
            pe.wait_ge(w_in, 64)
            pe.wait_ge(chain, 4)
            nc.tensor.transpose(PT[:, 0:N_BATCH], LN[:, :], ident[0:N_BATCH, 0:N_BATCH]).then_inc(t_full, 1)
            pe.wait_ge(t_out, 1)
            nc.tensor.matmul(PN[:, 0:N_BATCH], Wp1[:, :], LT[:, :], start=True, stop=True).then_inc(n_full, 1)
            pe.wait_ge(n_out, 1)
            nc.tensor.matmul(PT[0:N_BATCH, 0:EB], NT[:, :], Wp2[:, :], start=True, stop=True).then_inc(l_full, 1)


def mixers(nc, chip, X, ident, chosen, sorted_rows, tile_expert, tile_row, second_less_first, tables, routed, t):
    W1T, W2T, B1 = routed.W1T, routed.W2T, routed.B1
    HBLOCKS = W1T.shape[2] // P
    FOLD = 2
    SCATTER_FIRST = 3
    NT = tile_row.shape[1]
    E, _, F = t["L0_ffn_W1"].shape
    FT = F // P
    NB = FT + 1
    ER = t["L1_ffn_router_w"].shape[0]
    LAST = 6
    with ExitStack() as ctx:
        def sb(name, shape, dt=F32):
            return chip.sb(ctx, name, shape, dt)

        W1e, W2e = sb("W1e", [P, 2, BPG, F]), sb("W2e", [P, 2, BPG, FT, C])
        biases, Be = sb("biases", [P, E, NB]), sb("Be", [P, 2, BPG, NB])
        brow, Wo, bo, Wraw, tmv, tmr, dec = (
            tables.brow, tables.Wo, tables.bo, tables.Wraw, tables.tmv, tables.tmr, tables.dec)
        rw, rls, rlb, rbr, w_in = tables.rw, tables.rls, tables.rlb, tables.rbr, tables.w_in
        sel = sb("sel", [1, N_BATCH], U32)
        bo3 = sb("bo3", [P, C])
        WT = sb("WT", [P, 3, C])
        dec1, dec2, decb = sb("dec1", [P, 1]), sb("dec2", [P, 1]), sb("decb", [P, SEQ])
        zero = sb("zero", [P, SEQ])
        rwT, rwS = sb("rwT", [P, ER]), sb("rwS", [P, ER])
        rbias = sb("rbias", [P, ER])
        rlbb = sb("rlbb", [P, P])
        HN, YN, ZN = (sb(n, [P, TPG, C]) for n in ("HN", "YN", "ZN"))
        XA = sb("XA", [P, 2, TPG, C])
        XF, XR = sb("XF", [P, TPG, C]), sb("XR", [P, TPG, C])
        ZX = sb("ZX", [P, 2, TOP, TPG, ROW])
        goal = sb("goal", [P, TOP, TILES], I32)
        L1, L2 = sb("L1", [P, TPG, ER]), sb("L2", [P, TPG, ER])
        EQ, EQ2, M = sb("EQ", [P, TPG, ER]), sb("EQ2", [P, TOP, TPG, ER]), sb("M", [P, TOP, TPG, ER])
        M12 = sb("M12", [P, TPG, ER], BF16)
        top, which = sb("top", [P, TOP, TPG]), sb("which", [P, TOP, TPG])
        revi, rev = sb("revi", [P, ER], I32), sb("rev", [P, ER])
        starti = sb("starti", [P, ER], I32)
        tri, ones = sb("tri", [P, P]), sb("ones", [P, P])
        trib, onesb = sb("trib", [P, P], BF16), sb("onesb", [P, P], BF16)
        keep = sb("keep", [P, ER, TPG + 1])
        D1, SX = sb("D1", [P, ER, TPG + 1]), sb("SX", [P, ER, TPG + 1])
        SL, slot = sb("SL", [P, TPG, ER]), sb("slot", [P, TOP, TPG])
        SI = sb("SI", [P, 2, TOP, TPG], U32)
        head, headi, start, count = sb("head", [1, ER]), sb("headi", [1, ER], U32), sb("start", [1, ER]), sb("count", [1, ER])
        padi, pad, ends, gain = sb("padi", [1, ER], I32), sb("pad", [1, ER]), sb("ends", [1, ER]), sb("gain", [1, ER])
        one, ioti, iot = sb("one", [1, ER]), sb("ioti", [1, NT], I32), sb("iot", [1, NT])
        after, moved = sb("after", [1, NT, ER - 1]), sb("moved", [1, NT, ER - 1])
        cnt, shift, at_row = sb("cnt", [1, NT]), sb("shift", [1, NT]), sb("at_row", [1, NT])
        empty = sb("empty", [P, SUB, ROW])
        lcol = sb("lcol", [P, 2, ER])
        HT, RT, YT, VT, ZT = (sb(n, [P, GT]) for n in ("HT", "RT", "YT", "VT", "ZT"))
        G = sb("G", [P, BPG, FT, SEQ])
        ST = sb("ST", [P, BPG, SEQ + 1])
        WM = sb("WM", [P, 2, 2, C])
        rest = sb("rest", [P, 2])
        TH, MM = sb("TH", [P, TPG, C]), sb("MM", [P, TPG, C])
        stat = [sb(f"bst{n}", [P, TPG, 6]) for n in range(3)]
        mv = [sb(f"bmv{n}", [P, TPG, 2]) for n in range(3)]
        var, ny, ntmp = sb("bva", [P, 3 * TPG]), sb("bny", [P, NEWTON + 1, 3 * TPG]), sb("bnt", [P, 2 * NEWTON, 3 * TPG])

        PT, PR_, PO, PVV, PG, PQ = (chip.ps(ctx, n, [P, GT]) for n in ("bpt", "bpr", "bpo", "bpv", "bpg", "bpq"))
        PH = [chip.ps(ctx, f"bph{n}", [P, GT]) for n in range(BPG)]

        def sem(name):
            return chip.sem(ctx, "b_" + name)

        (sel_in, zero_set, act_set, dve_set, pe_set, w_exp) = (
            sem(n) for n in ("sel_in", "zero_set", "act_set", "dve_set", "pe_set", "w_exp"))
        stats = [sem(f"stats{n}") for n in range(3)]
        aggr = [sem(f"aggr{n}") for n in range(3)]
        var_set = [sem(f"var{n}") for n in range(3)]
        newton, plan_made, consts, mix_set, pad_set, pads_in = (
            sem(n) for n in ("newton", "plan_made", "consts", "mix_set", "pad_set", "pads_in"))
        applied = [sem(f"applied{n}") for n in range(3)]
        (hn_added, ht_full, ht_out, h1_full, g_out, r_full, r_out, o_full, x_ffn, yt_full, yt_out, scanned,
         v_full, v_out, gate_full, gate_out, o2_full, gated, x_rwkv, zt_full, zt_out, lg_full, lg_out,
         z_copied, goals_in, chain, masked, ranks_full, placed, run_in, scattered, xa_in, xf_back, xr_back) = (sem(n) for n in (
             "hn_added ht_full ht_out h1_full g_out r_full r_out o_full x_ffn yt_full yt_out scanned "
             "v_full v_out gate_full gate_out o2_full gated x_rwkv zt_full zt_out lg_full lg_out z_copied goals_in "
             "chain masked ranks_full placed run_in scattered xa_in xf_back xr_back").split())
        c_full, c_out, a_full, a_out, a_scaled, b_full, b_out, bias_full, bias_out = (
            sem(n) for n in "c_full c_out a_full a_out a_scaled b_full b_out bias_full bias_out".split())
        N_IN = len(tables.loads) + 1

        COLS = ER * HBLOCKS

        def tile_cols(n):
            return slice(n * P, (n + 1) * P)

        def tiles(m, g):
            return m[:, bass.ds(g * TPG, TPG), :]

        def tiles1(m, g):
            return m[:, bass.ds(g * TPG, TPG)]

        def run(step, eng):
            first, turns = LAST + 2, (GROUPS - 1 - (LAST + 2)) // 2
            for k in range(first):
                step(k, k)
            with eng.Fori(0, turns) as i:
                for r in range(2):
                    step(i * 2 + (first + r), first + r)
            for k in range(first + 2 * turns, GROUPS + LAST):
                step(k, k)

        def at(r, d):
            return 0 <= r - d < GROUPS

        block = ctx.enter_context(nc.Block())

        @block.sync
        def _(sp):
            sp.dma_start(sel[:, :], chosen.rearrange("b a -> a b")).then_inc(sel_in, 16)
            sp.wait_ge(sel_in, 16)
            sp.wait_ge(dve_set, 1)

            def experts(g, r):
                for b in range(BPG):
                    e = sp.value_load(sel[0:1, bass.ds(g * BPG + b, 1)], min_val=0, max_val=E - 1)
                    sp.dma_start(W1e[:, r % 2, b, :], t["L0_ffn_W1"][bass.ds(e, 1)].rearrange("e k f -> k (e f)"))\
                        .then_inc(w_exp, 16)
                    sp.dma_start(W2e[:, r % 2, b, :, :], t["L0_ffn_W2"][bass.ds(e, 1)].rearrange(
                        "e (n p) h -> p (e n) h", n=FT)).then_inc(w_exp, 16)
                    sp.dma_start(Be[:, r % 2, b, :], biases[:, bass.ds(e, 1), :].rearrange("p e n -> p (e n)"))\
                        .then_inc(w_exp, 16)

            experts(0, 0)
            for dst, src in ((routed.norm_rows[:, 0, :], t["L1_ffn_expert_ln_scale"]),
                             (routed.norm_rows[:, 1, :], t["L1_ffn_expert_ln_bias"]),
                             (routed.bias_rows[:, :], t["L1_ffn_b1"])):
                sp.dma_start(dst, src).then_inc(routed.rows_in, 16)

            def load_routed(e):
                sp.dma_start(routed.w1[:, e, :, :], t["L1_ffn_w1"][e].rearrange("(n p) d -> p n d", p=P))\
                    .then_inc(routed.expert_in[e], 16)
                sp.dma_start(routed.w2[:, e, :], t["L1_ffn_w2"][e]).then_inc(routed.expert_in[e], 16)

            for e in range(FOLD):
                load_routed(e)

            def step(k, r):
                if at(r, 0) and at(r + 1, 0):
                    wait_apart(sp, sel_in, w_exp, (k + 1) * (3 * 16 * BPG))
                    if r > 0:
                        wait_apart(sp, sel_in, r_out, k * BPG)
                    experts(k + 1, r + 1)
                if (r + 1) * FOLD < ER:
                    for e in range((r + 1) * FOLD, (r + 2) * FOLD):
                        load_routed(e)

            run(step, sp)
            sp.wait_ge(plan_made, 2)
            firsts = [sp.value_load(headi[0:1, e:e + 1], min_val=0, max_val=ER * CAP - E_SLOTS) for e in range(ER)]
            sp.wait_ge(pad_set, 2)
            sp.wait_ge(scattered, 16 * SHARE * GROUPS)
            for row in firsts:
                sp.dma_start(sorted_rows[bass.ds(row, E_SLOTS), :].rearrange("(n p) c -> p n c", p=P), empty[:, :, :])\
                    .then_inc(pads_in, 16)
            sp.wait_ge(pads_in, 16 * ER)

        @block.gpsimd
        def _(pool):
            pool.wait_ge(w_in, 16 * (N_IN - 1))
            nc.gpsimd.memset(zero[:, :], 0.0).then_inc(zero_set, 1)

            nc.gpsimd.iota(revi[:, :], pattern=[[-1, ER]], base=ER, channel_multiplier=0).then_inc(consts, 1)
            nc.gpsimd.iota(starti[:, :], pattern=[[CAP, ER]], base=0, channel_multiplier=0).then_inc(consts, 1)
            nc.gpsimd.iota(goal[:, :, :].rearrange("p k t -> p (k t)"), pattern=[[P, TOP * TILES]], base=0,
                           channel_multiplier=1).then_inc(consts, 1)
            nc.gpsimd.memset(tri[:, :], 1.0).then_inc(consts, 1)
            nc.gpsimd.memset(ones[:, :], 1.0).then_inc(consts, 1)
            nc.gpsimd.memset(keep[:, :, :], 1.0).then_inc(consts, 1)
            nc.gpsimd.iota(ioti[:, :], pattern=[[E_SLOTS, NT]], base=0, channel_multiplier=0).then_inc(consts, 1)
            nc.gpsimd.memset(one[:, :], 1.0).then_inc(consts, 1)
            pool.wait_ge(consts, 8)
            nc.gpsimd.memset(empty[:, :, :], 0.0).then_inc(pad_set, 1)
            pool.wait_ge(pad_set, 1)
            nc.gpsimd.memset(empty[:, :, C:ROW].bitcast(I32), 4 * TOKENS).then_inc(pad_set, 1)
            nc.gpsimd.affine_select(out=tri[:, :], in_=tri[:, :], compare_op=ALU.is_gt, fill=0.0, base=0,
                                    pattern=[[1, P]], channel_multiplier=-1).then_inc(consts, 1)

            def rsqrts(k, r):
                norms = [n for n in range(3) if at(r, 2 * n)]
                for n in norms:
                    g = k - 2 * n
                    wait_apart(pool, w_in, aggr[n], (g + 1) * TPG)
                    if not (isinstance(g, int) and g == 0):
                        wait_apart(pool, w_in, applied[n], g * TPG)
                    slope, least = (1.0, LN_EPS) if n < 2 else (1.0 + LN2_EPS, LN_EPS * LN2_EPS)
                    nc.gpsimd.tensor_scalar(var[:, n * TPG:(n + 1) * TPG], mv[n][:, :, 1], slope, least,
                                            ALU.mult, ALU.add).then_inc(var_set[n], 1)
                for n in norms:
                    wait_apart(pool, w_in, var_set[n], k - 2 * n + 1)
                part = slice(norms[0] * TPG, (norms[-1] + 1) * TPG)
                nc.gpsimd.tensor_scalar(ny[:, 0, part].bitcast(I32), var[:, part].bitcast(I32), -0.5, RSQRT_SEED,
                                        ALU.mult, ALU.add).then_inc(newton, 1)
                wait_apart(pool, w_in, newton, k * (NEWTON_OPS + 1) + 1)
                newton_rsqrt(nc.gpsimd, w_in, newton, k * (NEWTON_OPS + 1) + 1, ny[:, :, part], var[:, part],
                             ntmp[:, :, part])

            def add_norm(g):
                wait_apart(pool, w_in, applied[0], (g + 1) * TPG)
                wait_apart(pool, w_in, xa_in, g + 1)
                nc.gpsimd.tensor_tensor(tiles(X, g), tiles(X, g), HN[:, :, :], ALU.add).then_inc(hn_added, 1)
                wait_apart(pool, w_in, hn_added, g * 2 + 1)
                nc.gpsimd.tensor_tensor(tiles(X, g), tiles(X, g), bo3[:, :].unsqueeze(1).to_broadcast([P, TPG, C]),
                                        ALU.add).then_inc(hn_added, 1)

            def scatter(g, r, tiles_):
                if tiles_[0] == 0:
                    wait_apart(pool, w_in, placed, (g + 1) * 6)
                    wait_apart(pool, w_in, goals_in, g + 1)
                    wait_apart(pool, w_in, z_copied, (g + 1) * TOP)
                    if not (isinstance(g, int) and g == 0):
                        wait_apart(pool, w_in, scattered, g * (16 * SHARE))
                for i in tiles_:
                    for n in range(TOP):
                        nc.gpsimd.indirect_dma_start(out=sorted_rows, out_offset=bass.IndirectOffsetOnAxis(
                            ap=SI[:, r % 2, n, i:i + 1], axis=0), in_=ZX[:, r % 2, n, i, :], in_offset=None)\
                            .then_inc(scattered, 16)

            pool.wait_ge(dve_set, 14)

            def step(k, r):
                if at(r, 6):
                    scatter(k - 6, r - 6, range(SCATTER_FIRST))
                if at(r, 0) or at(r, 2) or at(r, 4):
                    rsqrts(k, r)
                if at(r, 6):
                    scatter(k - 6, r - 6, range(SCATTER_FIRST, TPG))
                if at(r, 0):
                    add_norm(k)

            run(step, pool)

        @block.scalar
        def _(act):
            act.wait_ge(w_in, 16 * (N_IN - 1))
            nc.scalar.activation(dec1[:, :], dec[:, :], ACT.Exp).then_inc(act_set, 1)
            act.wait_ge(act_set, 1)
            nc.scalar.activation(dec2[:, :], dec1[:, :], ACT.Exp, scale=-1.0).then_inc(act_set, 1)
            act.wait_ge(act_set, 2)
            act.wait_ge(zero_set, 1)
            nc.scalar.activation(decb[:, :], zero[:, :], ACT.Identity, bias=dec2[:, 0:1]).then_inc(act_set, 1)

            def turned(g, full, out, dst, used, per):
                act.wait_ge(full, g + 1)
                if not (isinstance(g, int) and g == 0):
                    act.wait_ge(used, g * per)
                nc.scalar.copy(dst[:, :], PT[:, :]).then_inc(out, 1)

            def ahead(g, r):
                if not (isinstance(g, int) and g < 2):
                    act.wait_ge(applied[0], (g - 1) * TPG)
                nc.scalar.copy(XA[:, r % 2], tiles(X, g)).then_inc(xa_in, 1)

            def back(g, full, src, out):
                act.wait_ge(full, g + 1)
                nc.scalar.copy(tiles(X, g), src[:, :, :]).then_inc(out, 1)

            def gelus(g, b, r):
                act.wait_ge(h1_full, g * BPG + (b + 1))
                act.wait_ge(w_exp, (g + 1) * (3 * 16 * BPG))
                if b == 0 and not (isinstance(g, int) and g == 0):
                    act.wait_ge(r_full, g)
                for n in range(FT):
                    nc.scalar.activation(G[:, b, n, :], PH[b][:, n * SEQ:(n + 1) * SEQ], ACT.Gelu,
                                         bias=Be[:, r % 2, b, n:n + 1]).then_inc(g_out, 1)

            def reasoned(g, r):
                act.wait_ge(r_full, g + 1)
                if not (isinstance(g, int) and g == 0):
                    act.wait_ge(o_full, g)
                for b in range(BPG):
                    nc.scalar.activation(RT[:, b * SEQ:(b + 1) * SEQ], PR_[:, b * SEQ:(b + 1) * SEQ], ACT.Identity,
                                         bias=Be[:, r % 2, b, FT:NB]).then_inc(r_out, 1)

            def values(g):
                act.wait_ge(v_full, g + 1)
                if not (isinstance(g, int) and g == 0):
                    act.wait_ge(o2_full, g)
                nc.scalar.copy(VT[:, :], PVV[:, :]).then_inc(v_out, 1)

            def gate(g):
                act.wait_ge(gate_full, g + 1)
                if not (isinstance(g, int) and g == 0):
                    act.wait_ge(gated, g)
                nc.scalar.activation(TH[:, :, :], PG[:, :].rearrange("p (t c) -> p t c", t=TPG), ACT.Tanh, scale=0.5)\
                    .then_inc(gate_out, 1)

            def copies(g, r):
                act.wait_ge(applied[2], (g + 1) * TPG)
                if not (isinstance(g, int) and g < 2):
                    act.wait_ge(scattered, (g - 1) * (16 * SHARE))
                for n in range(TOP):
                    nc.scalar.copy(ZX[:, r % 2, n, :, 0:C], ZN[:, :, :]).then_inc(z_copied, 1)

            def step(k, r):
                if at(r, 4):
                    values(k - 4)
                    gate(k - 4)
                if at(r, 1):
                    turned(k - 1, ht_full, ht_out, HT, h1_full, BPG)
                if at(r, 3):
                    turned(k - 3, yt_full, yt_out, YT, gate_full, 1)
                if at(r, 1):
                    gelus(k - 1, 0, r - 1)
                    gelus(k - 1, 1, r - 1)
                if at(r, 5):
                    turned(k - 5, zt_full, zt_out, ZT, lg_full, 1)
                if at(r, 2):
                    back(k - 2, x_ffn, XF, xf_back)
                if at(r, 5):
                    copies(k - 5, r - 5)
                if at(r, 1):
                    reasoned(k - 1, r - 1)
                if at(r, 4):
                    back(k - 4, x_rwkv, XR, xr_back)
                if at(r + 1, 0):
                    ahead(k + 1, r + 1)
                if r * FOLD < ER:
                    for e in range(r * FOLD, (r + 1) * FOLD):
                        act.wait_ge(b_full, e + 1)
                        nc.scalar.copy(W2T[:, e, :], PQ[:, :]).then_inc(b_out, 1)

            ahead(0, 0)
            run(step, act)

        @block.vector
        def _(dve):
            dve.wait_ge(w_in, 16 * (N_IN - 1))
            dve.wait_ge(pe_set, 1)
            nc.vector.tensor_copy(biases[:, :, :].rearrange("p e n -> p n e"),
                                  PT[:, 0:NB * E].rearrange("p (n e) -> p n e", n=NB)).then_inc(dve_set, 1)
            dve.wait_ge(pe_set, 2)
            nc.vector.tensor_copy(WT[:, :, :], PO[:, 0:3 * C].rearrange("p (n c) -> p n c", n=3)).then_inc(dve_set, 1)
            for n, m in enumerate((tmv, tmr)):
                nc.vector.tensor_scalar(rest[:, n:n + 1], m[:, :], -1.0, 1.0, ALU.mult, ALU.add).then_inc(mix_set, 1)
            dve.wait_ge(mix_set, 2)
            dve.wait_ge(dve_set, 2)
            for n, m in enumerate((tmv, tmr)):
                nc.vector.tensor_scalar(WM[:, n, 0, :], WT[:, n, :], m[:, 0:1], None, ALU.mult).then_inc(mix_set, 1)
                nc.vector.tensor_scalar(WM[:, n, 1, :], WT[:, n, :], rest[:, n:n + 1], None, ALU.mult).then_inc(mix_set, 1)
            nc.vector.tensor_scalar(bo3[:, :], bo[:, :], 0.3, None, ALU.mult).then_inc(dve_set, 1)
            nc.vector.memset(ST[:, :, 0:1], 0.0).then_inc(dve_set, 1)
            dve.wait_ge(pe_set, 3)
            nc.vector.tensor_copy(rwT[:, :], PG[:, 0:ER]).then_inc(dve_set, 1)
            nc.vector.tensor_scalar(rwS[:, :], PG[:, 0:ER], rls[:, 0:1], None, ALU.mult).then_inc(dve_set, 1)
            nc.vector.tensor_scalar(rlbb[:, :], ident[:, :], 0.0, rlb[:, 0:1], ALU.mult, ALU.add).then_inc(dve_set, 1)
            dve.wait_ge(pe_set, 4)
            nc.vector.tensor_tensor(rbias[:, :], PQ[:, 0:ER], rbr[:, :], ALU.add).then_inc(dve_set, 1)
            dve.wait_ge(consts, 9)
            nc.vector.tensor_copy(rev[:, :], revi[:, :]).then_inc(dve_set, 1)
            nc.vector.tensor_copy(SX[:, :, TPG], starti[:, :]).then_inc(dve_set, 1)
            nc.vector.tensor_copy(trib[:, :], tri[:, :]).then_inc(dve_set, 1)
            nc.vector.tensor_copy(onesb[:, :], ones[:, :]).then_inc(dve_set, 1)
            nc.vector.memset(keep[:, :, 0:1], 0.0).then_inc(dve_set, 1)
            nc.vector.memset(ZX[:, :, :, :, :].rearrange("p b k t c -> p (b k t c)"), 0.0).then_inc(dve_set, 1)
            dve.wait_ge(dve_set, 14)
            dve.wait_ge(act_set, 3)

            def norm_stats(n, g, src):
                if not (isinstance(g, int) and g == 0):
                    wait_apart(dve, w_in, applied[n], g * TPG)
                for i in range(TPG):
                    nc.vector.bn_stats(stat[n][:, i, :], src[:, i, :])\
                        .then_inc(stats[n], 1)
                wait_apart(dve, w_in, stats[n], (g + 1) * TPG)
                for i in range(TPG):
                    nc.vector.bn_aggr(mv[n][:, i, :], stat[n][:, i, :]).then_inc(aggr[n], 1)

            def apply(n, g, src, dst, used, per):
                dve.wait_ge(newton, (g + (2 * n + 1)) * (NEWTON_OPS + 1))
                if not (isinstance(g, int) and g == 0):
                    dve.wait_ge(used, g * per)
                    if n == 2:
                        dve.wait_ge(z_copied, g * TOP)
                    if n == 0:
                        dve.wait_ge(hn_added, g * 2)
                for i in range(TPG):
                    nc.vector.tensor_scalar(dst[:, i, :], src[:, i, :],
                                            mv[n][:, i, 0:1], ny[:, NEWTON, n * TPG + i:n * TPG + i + 1], ALU.subtract, ALU.mult)\
                        .then_inc(applied[n], 1)

            def scan(g):
                dve.wait_ge(yt_out, g + 1)
                if not (isinstance(g, int) and g == 0):
                    dve.wait_ge(gate_full, g)
                for b in range(BPG):
                    nc.vector.tensor_tensor_scan(ST[:, b, 1:SEQ + 1], decb[:, :], YT[:, b * SEQ:(b + 1) * SEQ], 0.0,
                                                 ALU.mult, ALU.add).then_inc(scanned, 1)

            def ffn_residual(g):
                dve.wait_ge(o_full, g + 1)
                dve.wait_ge(hn_added, (g + 1) * 2)
                if not (isinstance(g, int) and g == 0):
                    dve.wait_ge(xf_back, g)
                    dve.wait_ge(applied[1], g * TPG)
                nc.vector.scalar_tensor_tensor(out=XF[:, :, :], in0=PO[:, :].rearrange("p (t c) -> p t c", t=TPG), scalar=0.3,
                                               in1=tiles(X, g), op0=ALU.mult, op1=ALU.add).then_inc(x_ffn, 1)
                dve.wait_ge(x_ffn, g + 1)

            def rwkv_residual(g):
                dve.wait_ge(gate_out, g + 1)
                dve.wait_ge(o2_full, g + 1)
                nc.vector.scalar_tensor_tensor(out=MM[:, :, :], in0=TH[:, :, :], scalar=1.0,
                                               in1=PQ[:, :].rearrange("p (t c) -> p t c", t=TPG), op0=ALU.add,
                                               op1=ALU.mult).then_inc(gated, 1)
                dve.wait_ge(gated, g + 1)
                dve.wait_ge(xf_back, g + 1)
                if not (isinstance(g, int) and g == 0):
                    dve.wait_ge(xr_back, g)
                    dve.wait_ge(applied[2], g * TPG)
                nc.vector.scalar_tensor_tensor(out=XR[:, :, :], in0=MM[:, :, :], scalar=0.5, in1=tiles(X, g),
                                               op0=ALU.mult, op1=ALU.add).then_inc(x_rwkv, 1)
                dve.wait_ge(x_rwkv, g + 1)

            def over_e(x):
                return x.unsqueeze(2).to_broadcast([P, TPG, ER])

            def over_t(x):
                return x.unsqueeze(1).to_broadcast([P, TPG, ER])

            def best_two(g, r):
                done = [0]

                def link(ins):
                    done[0] += 1
                    ins.then_inc(chain, 1)
                    dve.wait_ge(chain, g * 12 + done[0])

                dve.wait_ge(lg_full, g + 1)
                nc.vector.tensor_tensor(L1[:, :, :], PT[:, 0:TPG * ER].rearrange("p (t e) -> p t e", t=TPG),
                                        over_t(rbias[:, :]), ALU.add).then_inc(lg_out, 1)
                dve.wait_ge(lg_out, g + 1)
                for n, l in enumerate((L1, L2)):
                    link(nc.vector.tensor_reduce(top[:, n, :], l[:, :, :], AX.X, ALU.max))
                    link(nc.vector.tensor_tensor(EQ[:, :, :], l[:, :, :], over_e(top[:, n, :]), ALU.is_equal))
                    link(nc.vector.tensor_tensor(EQ[:, :, :], EQ[:, :, :], over_t(rev[:, :]), ALU.mult))
                    link(nc.vector.tensor_reduce(which[:, n, :], EQ[:, :, :], AX.X, ALU.max))
                    link(nc.vector.tensor_tensor(M[:, n, :, :], over_t(rev[:, :]), over_e(which[:, n, :]), ALU.is_equal))
                    if n == 0:
                        link(nc.vector.scalar_tensor_tensor(out=L2[:, :, :], in0=M[:, 0, :, :], scalar=-BIG,
                                                            in1=L1[:, :, :], op0=ALU.mult, op1=ALU.add))
                if not (isinstance(g, int) and g == 0):
                    dve.wait_ge(ranks_full, g)
                nc.vector.tensor_tensor(M12[:, :, :], M[:, 0, :, :], M[:, 1, :, :], ALU.add).then_inc(masked, 1)
                link(nc.vector.tensor_tensor(tiles1(second_less_first, g), top[:, 1, :], top[:, 0, :], ALU.subtract))
                if not (isinstance(g, int) and g < 2):
                    dve.wait_ge(scattered, (g - 1) * (16 * SHARE))
                nc.vector.tensor_copy(ZX[:, r % 2, :, :, C].bitcast(I32), goal[:, :, bass.ds(g * TPG, TPG)])\
                    .then_inc(goals_in, 1)

            def places(g, r):
                done = [0]

                def link(ins):
                    done[0] += 1
                    ins.then_inc(placed, 1)
                    dve.wait_ge(placed, g * 6 + done[0])

                nc.vector.tensor_copy(D1[:, :, 0], SX[:, :, TPG]).then_inc(run_in, 1)
                dve.wait_ge(ranks_full, g + 1)
                link(nc.vector.tensor_copy(D1[:, :, 1:], PVV[:, TPG * ER:2 * TPG * ER].rearrange(
                    "p (t e) -> p e t", t=TPG)))
                dve.wait_ge(run_in, g + 1)
                link(nc.vector.tensor_tensor_scan(SX[:, :, :].rearrange("p e t -> p (e t)"),
                                                  keep[:, :, :].rearrange("p e t -> p (e t)"),
                                                  D1[:, :, :].rearrange("p e t -> p (e t)"), 0.0, ALU.mult, ALU.add))
                link(nc.vector.tensor_tensor(SL[:, :, :], PVV[:, 0:TPG * ER].rearrange("p (t e) -> p t e", t=TPG),
                                             SX[:, :, 0:TPG].rearrange("p e t -> p t e"), ALU.add))
                link(nc.vector.tensor_tensor(EQ2[:, :, :, :], M[:, :, :, :],
                                             SL[:, :, :].unsqueeze(1).to_broadcast([P, TOP, TPG, ER]), ALU.mult))
                link(nc.vector.tensor_reduce(slot[:, :, :], EQ2[:, :, :, :], AX.X, ALU.add))
                if not (isinstance(g, int) and g < 2):
                    dve.wait_ge(scattered, (g - 1) * (16 * SHARE))
                link(nc.vector.tensor_copy(SI[:, r % 2, :, :], slot[:, :, :]))

            def fold(e):
                if e == 0:
                    dve.wait_ge(c_full, 1)
                    nc.vector.tensor_copy(lcol[:, :, :], PVV[:, COLS:COLS + 2 * ER].rearrange("p (n e) -> p n e", n=2))\
                        .then_inc(c_out, 1)
                    nc.vector.tensor_copy(B1[:, :, :].rearrange("p e n -> p n e"), PVV[
                        :, COLS + 2 * ER:COLS + (2 + HBLOCKS) * ER].rearrange("p (n e) -> p n e", n=HBLOCKS)).then_inc(c_out, 1)
                dve.wait_ge(a_full, e + 1)
                nc.vector.tensor_copy(W1T[:, e, :], PG[:, :]).then_inc(a_out, 1)
                for done in ([e - 1] if e > 0 else []) + ([e] if e == ER - 1 else []):
                    dve.wait_ge(bias_full, done + 1)
                    dve.wait_ge(c_out, 2)
                    dve.wait_ge(a_out, done + 1)
                    nc.vector.tensor_scalar(W1T[:, done, :], W1T[:, done, :], lcol[:, 0, done:done + 1], None, ALU.mult)\
                        .then_inc(a_scaled, 1)
                if e == ER - 1:
                    nc.vector.tensor_tensor(B1[:, :, :], B1[:, :, :], PVV[:, 0:ER * HBLOCKS].rearrange("p (e n) -> p e n", e=ER),
                                            ALU.add).then_inc(bias_out, 1)

            def step(k, r):
                if at(r, 0):
                    dve.wait_ge(xa_in, k + 1)
                    norm_stats(0, k, XA[:, r % 2])
                if at(r, 2):
                    ffn_residual(k - 2)
                    norm_stats(1, k - 2, XF)
                if at(r, 4):
                    rwkv_residual(k - 4)
                    norm_stats(2, k - 4, XR)
                if at(r, 3):
                    scan(k - 3)
                if r * FOLD < ER:
                    for e in range(r * FOLD, (r + 1) * FOLD):
                        fold(e)
                if at(r, 5):
                    best_two(k - 5, r - 5)
                if at(r, 5):
                    places(k - 5, r - 5)
                if at(r, 0):
                    apply(0, k, XA[:, r % 2], HN, ht_full, 1)
                if at(r, 2):
                    apply(1, k - 2, XF, YN, yt_full, 1)
                if at(r, 4):
                    apply(2, k - 4, XR, ZN, zt_full, 1)

            run(step, dve)

            done = [0]

            def link(ins):
                done[0] += 1
                ins.then_inc(plan_made, 1)
                dve.wait_ge(plan_made, done[0])

            link(nc.vector.tensor_copy(head[:, :], SX[0:1, :, TPG]))
            link(nc.vector.tensor_copy(headi[:, :], head[:, :]))
            link(nc.vector.tensor_copy(start[:, :], starti[0:1, :]))
            link(nc.vector.tensor_copy(iot[:, :], ioti[:, :]))
            link(nc.vector.tensor_tensor(count[:, :], head[:, :], start[:, :], ALU.subtract))
            link(nc.vector.tensor_scalar(padi[:, :], count[:, :], float(E_SLOTS - 1), None, ALU.add))
            bits = E_SLOTS.bit_length() - 1
            link(nc.vector.tensor_scalar(padi[:, :], padi[:, :], bits, bits, ALU.logical_shift_right,
                                         ALU.logical_shift_left))
            link(nc.vector.tensor_copy(pad[:, :], padi[:, :]))
            link(nc.vector.tensor_tensor_scan(ends[:, :], one[:, :], pad[:, :], 0.0, ALU.mult, ALU.add))
            link(nc.vector.tensor_tensor(after[:, :, :], iot[:, :].unsqueeze(2).to_broadcast([1, NT, ER - 1]),
                                         ends[:, 0:ER - 1].unsqueeze(1).to_broadcast([1, NT, ER - 1]), ALU.is_ge))
            link(nc.vector.tensor_reduce(cnt[:, :], after[:, :, :], AX.X, ALU.add))
            link(nc.vector.tensor_copy(tile_expert[:, :], cnt[:, :]))
            link(nc.vector.tensor_scalar(gain[:, :], pad[:, :], -1.0, float(CAP), ALU.mult, ALU.add))
            link(nc.vector.tensor_tensor(moved[:, :, :], after[:, :, :],
                                         gain[:, 0:ER - 1].unsqueeze(1).to_broadcast([1, NT, ER - 1]), ALU.mult))
            link(nc.vector.tensor_reduce(shift[:, :], moved[:, :, :], AX.X, ALU.add))
            link(nc.vector.tensor_tensor(at_row[:, :], iot[:, :], shift[:, :], ALU.add))
            link(nc.vector.tensor_tensor(at_row[:, :], at_row[:, :], head[:, ER - 1:ER].to_broadcast([1, NT]), ALU.min))
            link(nc.vector.tensor_copy(tile_row[:, :], at_row[:, :]))

        @block.tensor
        def _(pe):
            wait(pe, w_in, 16 * (N_IN - 1))
            for n in range(NB):
                mm = nc.tensor.transpose(PT[:, n * E:(n + 1) * E], brow[:, n, :], ident[0:E, 0:E])
            mm.then_inc(pe_set, 1)
            for n in range(3):
                mm = nc.tensor.transpose(PO[:, tile_cols(n)], Wraw[:, n, :], ident[:, :])
            mm.then_inc(pe_set, 1)
            nc.tensor.transpose(PG[:, 0:ER], rw[:, :], ident[0:ER, 0:ER]).then_inc(pe_set, 1)
            wait(pe, dve_set, 7)
            nc.tensor.matmul(PQ[:, 0:ER], rlbb[:, :], rwT[:, :], start=True, stop=True).then_inc(pe_set, 1)
            wait(pe, dve_set, 14)
            wait(pe, mix_set, 6)

            def turn(src, ready, full, g, free, count):
                wait(pe, ready, (g + 1) * TPG)
                wait(pe, free, count)
                for n in range(TPG):
                    mm = nc.tensor.transpose(PT[:, tile_cols(n)], src[:, n, :], ident[:, :])
                mm.then_inc(full, 1)

            def first_product(g, r):
                wait(pe, ht_out, g + 1)
                wait(pe, w_exp, (g + 1) * (3 * 16 * BPG))
                if not (isinstance(g, int) and g == 0):
                    wait(pe, g_out, g * BPG * FT)
                for b in range(BPG):
                    for n in range(FT):
                        mm = nc.tensor.matmul(PH[b][:, n * SEQ:(n + 1) * SEQ], W1e[:, r % 2, b, n * P:(n + 1) * P],
                                              HT[:, b * SEQ:(b + 1) * SEQ], start=True, stop=True)
                    mm.then_inc(h1_full, 1)

            def second_product(g, r):
                wait(pe, g_out, (g + 1) * BPG * FT)
                if not (isinstance(g, int) and g == 0):
                    wait(pe, r_out, g * BPG)
                for b in range(BPG):
                    for n in range(FT):
                        mm = nc.tensor.matmul(PR_[:, b * SEQ:(b + 1) * SEQ], W2e[:, r % 2, b, n, :], G[:, b, n, :],
                                              start=(n == 0), stop=(n == FT - 1))
                mm.then_inc(r_full, 1)

            def by_rows(bank, src, w, full):
                for n in range(TPG):
                    mm = nc.tensor.matmul(bank[:, tile_cols(n)], src[:, tile_cols(n)], w, start=True, stop=True)
                mm.then_inc(full, 1)

            def ffn_out(g):
                wait(pe, r_out, (g + 1) * BPG)
                if not (isinstance(g, int) and g == 0):
                    wait(pe, x_ffn, g)
                by_rows(PO, RT, Wo[:, :], o_full)

            def ranks(g, free):
                wait(pe, masked, g + 1)
                wait(pe, v_out, free)
                m12 = M12[:, :, :].rearrange("p t e -> p (t e)")
                nc.tensor.matmul(PVV[:, 0:TPG * ER], trib[:, :], m12, start=True, stop=True)
                nc.tensor.matmul(PVV[:, TPG * ER:2 * TPG * ER], onesb[:, :], m12, start=True, stop=True)\
                    .then_inc(ranks_full, 1)

            def values_gates(g, r):
                if r == 0:
                    wait(pe, bias_out, 1)
                    wait(pe, a_out, ER)
                    wait(pe, b_out, ER)
                wait(pe, scanned, (g + 1) * BPG)
                wait(pe, yt_out, g + 1)
                if not (isinstance(g, int) and g == 0):
                    wait(pe, v_out, g)
                if at(r, 2):
                    wait(pe, placed, (g - 1) * 6)
                nc.tensor.matmul(PVV[:, :], WM[:, 0, 0, :], YT[:, :], start=True, stop=False)
                nc.tensor.matmul(PVV[:, :].rearrange("p (b s) -> p b s", b=BPG), WM[:, 0, 1, :], ST[:, :, 0:SEQ],
                                 start=False, stop=True).then_inc(v_full, 1)
                if not (isinstance(g, int) and g == 0):
                    wait(pe, gate_out, g)
                for n in range(TPG):
                    b, i = divmod(n, TPB)
                    nc.tensor.matmul(PG[:, tile_cols(n)], YT[:, tile_cols(n)], WM[:, 1, 0, :], start=True, stop=False)
                    mm = nc.tensor.matmul(PG[:, tile_cols(n)], ST[:, b, i * P:(i + 1) * P], WM[:, 1, 1, :],
                                          start=False, stop=True)
                mm.then_inc(gate_full, 1)

            def rwkv_out(g):
                wait(pe, v_out, g + 1)
                if not (isinstance(g, int) and g == 0):
                    wait(pe, gated, g)
                by_rows(PQ, VT, WT[:, 2, :], o2_full)

            def router(g):
                wait(pe, zt_out, g + 1)
                for n in range(TPG):
                    mm = nc.tensor.matmul(PT[:, n * ER:(n + 1) * ER], ZT[:, tile_cols(n)], rwS[:, :], start=True, stop=True)
                mm.then_inc(lg_full, 1)

            def fold(e):
                if e == 0:
                    wait(pe, routed.rows_in, 48)
                    for n in range(2):
                        nc.tensor.transpose(PVV[:, COLS + n * ER:COLS + (n + 1) * ER], routed.norm_rows[:, n, :],
                                            ident[0:ER, 0:ER])
                    for n in range(HBLOCKS):
                        mm = nc.tensor.transpose(PVV[:, COLS + (2 + n) * ER:COLS + (3 + n) * ER],
                                                 routed.bias_rows[:, n * P:(n + 1) * P], ident[0:ER, 0:ER])
                    mm.then_inc(c_full, 1)
                else:
                    wait(pe, a_out, e)
                    wait(pe, b_out, e)
                wait(pe, routed.expert_in[e], 32)
                for n in range(HBLOCKS):
                    mm = nc.tensor.transpose(PG[:, tile_cols(n)], routed.w1[:, e, n, :], ident[:, :])
                mm.then_inc(a_full, 1)
                for n in range(HBLOCKS):
                    mm = nc.tensor.transpose(PQ[:, tile_cols(n)], routed.w2[:, e, tile_cols(n)], ident[:, :])
                mm.then_inc(b_full, 1)
                wait(pe, a_out, e + 1)
                wait(pe, c_out, 2)
                for n in range(HBLOCKS):
                    mm = nc.tensor.matmul(PVV[:, e * HBLOCKS + n:e * HBLOCKS + n + 1], W1T[:, e, tile_cols(n)], lcol[:, 1, e:e + 1],
                                          start=True, stop=True)
                mm.then_inc(bias_full, 1)

            def step(k, r):
                before = (dve_set, 14)
                if at(r - 1, 5):
                    before = (lg_out, k - 5)
                elif at(r - 1, 3):
                    before = (yt_out, k - 3)
                elif at(r - 1, 1):
                    before = (ht_out, k - 1)
                if at(r, 2):
                    ffn_out(k - 2)
                if at(r, 4):
                    values_gates(k - 4, r - 4)
                    rwkv_out(k - 4)
                if at(r, 1):
                    turn(HN, applied[0], ht_full, k - 1, *before)
                    before = (ht_out, k)
                if at(r, 3):
                    turn(YN, applied[1], yt_full, k - 3, *before)
                    before = (yt_out, k - 2)
                if at(r, 1):
                    first_product(k - 1, r - 1)
                if at(r, 5):
                    turn(ZN, applied[2], zt_full, k - 5, *before)
                    router(k - 5)
                if at(r, 1):
                    second_product(k - 1, r - 1)
                if at(r, 5):
                    ranks(k - 5, k - 3 if at(r, 4) else GROUPS)
                if r * FOLD < ER:
                    for e in range(r * FOLD, (r + 1) * FOLD):
                        fold(e)

            run(step, pe)


def routed_experts(nc, chip, idx_ok, X, ident, sorted_rows, second_less_first, tile_expert, tile_row, routed, b2, out, NT):
    W1T, W2T, B1 = routed.W1T, routed.W2T, routed.B1
    E, H = W1T.shape[1], W1T.shape[2]
    HT = H // P
    LAST = 4
    TURN = 4
    LOAD = 8
    YBUFS = 3
    with ExitStack() as ctx:
        def sb(name, shape, dt=F32):
            return chip.sb(ctx, name, shape, dt)

        W1e, b1e, b2e = sb("W1x", [P, TURN, H]), sb("b1x", [P, TURN, HT]), sb("b2x", [P, E, C])
        IT = sb("IT", [P, TURN, SUB], U32)
        GX, GT_ = sb("GX", [P, TURN, SUB, ROW]), sb("GXT", [P, 2, E_SLOTS])
        HG = sb("HG", [P, 2, HT, E_SLOTS])
        YS = sb("YS", [P, 2, SUB, C])
        Y = sb("Y", [P, YBUFS, TOP, LOAD, C])
        ed, den, gates = sb("ed", [P, TILES]), sb("den", [P, TILES]), sb("gates", [P, TOP, TILES])
        results = chip.dram("results", [2 * TOKENS, C], F32)
        PT = chip.ps(ctx, "xpt", [P, E_SLOTS])
        PH = [chip.ps(ctx, f"xph{n}", [P, E_SLOTS]) for n in range(HT)]
        PY = [chip.ps(ctx, f"xpy{n}", [P, E_SLOTS]) for n in range(2)]
        y_in = [chip.sem(ctx, f"x_y_in{n}") for n in range(YBUFS)]
        b2_in, exped, gate_set = (chip.sem(ctx, "x_" + n) for n in ("b2_in", "exped", "gate_set"))
        (w1_in, gathered, t_full, t_out, h_full, h_out, y_full, y_out, scattered, tgt, mixed, added,
         x_out) = (chip.sem(ctx, "x_" + n) for n in (
             "w1_in gathered t_full t_out h_full h_out y_full y_out scattered tgt mixed added x_out").split())

        def run(step, eng):
            first = LAST + 2
            turns = (NT - 1 - first) // TURN
            for k in range(first):
                step(k, k)
            with eng.Fori(0, turns) as i:
                for r in range(TURN):
                    step(i * TURN + (first + r), first + r)
            for k in range(first + TURN * turns, NT + LAST):
                step(k, k)

        def at(r, d):
            return 0 <= r - d < NT

        def early(g, n):
            return isinstance(g, int) and g < n

        def load_results(sp, n):
            for k in range(TOP):
                sp.dma_start(Y[:, n % YBUFS, k, :, :], results.rearrange("(k t p) c -> p k t c", k=TOP, p=P)[
                    :, k, n * LOAD:(n + 1) * LOAD, :]).then_inc(y_in[n % YBUFS], 16)

        def store(sp, n):
            sp.wait_ge(added, (n + 1) * LOAD)
            sp.dma_start(out.rearrange("b (t p) c -> p (b t) c", p=P)[:, n * LOAD:(n + 1) * LOAD, :],
                         X[:, n * LOAD:(n + 1) * LOAD, :]).then_inc(x_out, 16)

        block = ctx.enter_context(nc.Block())

        @block.sync
        def _(sp):
            def load_rows(j, r):
                row = sp.value_load(tile_row[0:1, bass.ds(j, 1)], min_val=0, max_val=E * CAP - E_SLOTS)
                if not early(j, 1):
                    wait_apart(sp, idx_ok, gathered, j * 16)
                if not early(j, TURN):
                    wait_apart(sp, idx_ok, t_full, j - (TURN - 1))
                    wait_apart(sp, idx_ok, tgt, j - (TURN - 1))
                sp.dma_start(GX[:, r % TURN, :, :], sorted_rows[bass.ds(row, E_SLOTS), :].rearrange("(n p) c -> p n c", p=P))\
                    .then_inc(gathered, 16)

            def load(j, r):
                e = sp.value_load(tile_expert[0:1, bass.ds(j, 1)], min_val=0, max_val=E - 1)
                if not early(j, 1):
                    wait_apart(sp, idx_ok, w1_in, j * 32)
                if not early(j, TURN):
                    wait_apart(sp, idx_ok, h_full, (j - (TURN - 1)) * HT)
                    wait_apart(sp, idx_ok, h_out, (j - (TURN - 1)) * HT)
                sp.dma_start(W1e[:, r % TURN, :], W1T[:, bass.ds(e, 1), :].rearrange("p e h -> p (e h)")).then_inc(w1_in, 16)
                sp.dma_start(b1e[:, r % TURN, :], B1[:, bass.ds(e, 1), :].rearrange("p e h -> p (e h)")).then_inc(w1_in, 16)

            def step(k, r):
                if at(r, 0):
                    load(k, r)
                    load_rows(k, r)
                if r == 0:
                    sp.dma_start(b2e[:, :, :], rows(b2)).then_inc(b2_in, 16)

            run(step, sp)
            sp.wait_ge(scattered, NT * SUB * 16)
            for n in range(YBUFS):
                load_results(sp, n)
            for n in range(TILES // LOAD):
                store(sp, n)
                if n + YBUFS < TILES // LOAD:
                    load_results(sp, n + YBUFS)
            sp.wait_ge(x_out, 16 * (TILES // LOAD))

        @block.gpsimd
        def _(pool):
            def scatter(j, r):
                wait_apart(pool, idx_ok, tgt, j + 1)
                wait_apart(pool, idx_ok, y_out, j + 1)
                if not early(j, 1):
                    wait_apart(pool, idx_ok, scattered, j * SUB * 16)
                for n in range(SUB):
                    nc.gpsimd.indirect_dma_start(out=results, out_offset=bass.IndirectOffsetOnAxis(
                        ap=IT[:, r % TURN, n:n + 1], axis=0), in_=YS[:, r % 2, n, :], in_offset=None,
                        bounds_check=2 * TOKENS - 1, oob_is_err=False).then_inc(scattered, 16)

            def step(k, r):
                if at(r, 4):
                    scatter(k - 4, r - 4)

            run(step, pool)

        @block.vector
        def _(dve):
            dve.wait_ge(exped, 1)
            nc.vector.tensor_scalar(den[:, :], ed[:, :], 1.0, None, ALU.add).then_inc(gate_set, 1)
            dve.wait_ge(gate_set, 1)
            nc.vector.reciprocal(gates[:, 0, :], den[:, :]).then_inc(gate_set, 1)
            dve.wait_ge(gate_set, 2)
            nc.vector.tensor_tensor(gates[:, 1, :], ed[:, :], gates[:, 0, :], ALU.mult).then_inc(gate_set, 1)
            dve.wait_ge(gate_set, 3)
            dve.wait_ge(b2_in, 16)

            def targets(j, r):
                dve.wait_ge(gathered, (j + 1) * 16)
                if not early(j, TURN):
                    dve.wait_ge(scattered, (j - (TURN - 1)) * SUB * 16)
                nc.vector.tensor_copy(IT[:, r % TURN, :], GX[:, r % TURN, :, C].bitcast(U32)).then_inc(tgt, 1)

            def results_out(j, r):
                dve.wait_ge(y_full, j + 1)
                if not early(j, 2):
                    dve.wait_ge(scattered, (j - 1) * SUB * 16)
                e = dve.value_load(tile_expert[0:1, bass.ds(j, 1)], min_val=0, max_val=E - 1)
                bias = b2e[:, bass.ds(e, 1), :].to_broadcast([P, SUB, C])
                nc.vector.tensor_tensor(YS[:, r % 2, :, :], PY[r % 2][:, :].rearrange("p (n c) -> p n c", n=SUB),
                                        bias, ALU.add).then_inc(y_out, 1)

            def step(k, r):
                if at(r, 1):
                    targets(k - 1, r - 1)
                if at(r, 3):
                    results_out(k - 3, r - 3)

            run(step, dve)
            for n in range(TILES // LOAD):
                dve.wait_ge(y_in[n % YBUFS], 16 * TOP * (n // YBUFS + 1))
                for k in range(TOP):
                    if k:
                        dve.wait_ge(mixed, (n + 1) * LOAD)
                    for i in range(LOAD):
                        tile = n * LOAD + i
                        nc.vector.scalar_tensor_tensor(out=X[:, tile, :], in0=Y[:, n % YBUFS, k, i, :],
                                                       scalar=gates[:, k, tile:tile + 1], in1=X[:, tile, :],
                                                       op0=ALU.mult, op1=ALU.add).then_inc((mixed, added)[k], 1)

        @block.scalar
        def _(act):
            nc.scalar.activation(ed[:, :], second_less_first[:, :], ACT.Exp).then_inc(exped, 1)

            def turned(j, r):
                act.wait_ge(t_full, j + 1)
                if not early(j, 2):
                    act.wait_ge(h_full, (j - 1) * HT)
                nc.scalar.copy(GT_[:, r % 2, :], PT[:, :]).then_inc(t_out, 1)

            def gelus(j, r):
                act.wait_ge(w1_in, (j + 1) * 32)
                if not early(j, 2):
                    act.wait_ge(y_full, j - 1)
                for n in range(HT):
                    act.wait_ge(h_full, j * HT + (n + 1))
                    nc.scalar.activation(HG[:, r % 2, n, :], PH[n][:, :], ACT.Gelu, bias=b1e[:, r % TURN, n:n + 1])\
                        .then_inc(h_out, 1)

            def step(k, r):
                if at(r, 1):
                    turned(k - 1, r - 1)
                if at(r, 2):
                    gelus(k - 2, r - 2)

            run(step, act)

        @block.tensor
        def _(pe):
            def turn(j, r):
                wait(pe, gathered, (j + 1) * 16)
                if not early(j, 1):
                    wait(pe, t_out, j)
                for n in range(SUB):
                    mm = nc.tensor.transpose(PT[:, n * P:(n + 1) * P], GX[:, r % TURN, n, 0:C], ident[:, :])
                mm.then_inc(t_full, 1)

            def first_product(j, r):
                wait(pe, t_out, j + 1)
                wait(pe, w1_in, (j + 1) * 32)
                for n in range(HT):
                    if not early(j, 1):
                        wait(pe, h_out, (j - 1) * HT + (n + 1))
                    nc.tensor.matmul(PH[n][:, :], W1e[:, r % TURN, n * P:(n + 1) * P], GT_[:, r % 2, :], start=True, stop=True)\
                        .then_inc(h_full, 1)

            def second_product(j, r):
                e = pe.value_load(tile_expert[0:1, bass.ds(j, 1)], min_val=0, max_val=E - 1)
                wait(pe, h_out, (j + 1) * HT)
                if not early(j, 2):
                    wait(pe, y_out, j - 1)
                for i in range(SUB):
                    for n in range(HT):
                        mm = nc.tensor.matmul(PY[r % 2][:, i * P:(i + 1) * P], HG[:, r % 2, n, i * P:(i + 1) * P],
                                              W2T[:, bass.ds(e, 1), n * P:(n + 1) * P].rearrange("p e c -> p (e c)"), start=(n == 0), stop=(n == HT - 1))
                mm.then_inc(y_full, 1)

            def step(k, r):
                if at(r, 1):
                    turn(k - 1, r - 1)
                if at(r, 2):
                    first_product(k - 2, r - 2)
                if at(r, 3):
                    second_product(k - 3, r - 3)

            run(step, pe)


def network(nc, t, out):
    chip = Chip(nc)
    nc.disable_value_cache = True
    chosen = chip.dram("chosen", [N_BATCH, 1], U32)
    E, H, _ = t["L1_ffn_w1"].shape
    sorted_rows = chip.dram("sorted_rows", [E * CAP, ROW], F32)
    with ExitStack() as ctx:
        X = chip.sb(ctx, "X", [P, TILES, C], F32)
        ident = chip.sb(ctx, "ident", [P, P], F32)
        second_less_first = chip.sb(ctx, "second_less_first", [P, TILES], F32)
        NT = TOP * TOKENS // E_SLOTS + E - 1
        tile_expert, tile_row = (chip.sb(ctx, n, [1, NT], U32) for n in ("tile_expert", "tile_row"))
        id_zero, id_set = (chip.sem(ctx, n) for n in ("id_zero", "id_set"))
        with nc.Block() as block:
            @block.gpsimd
            def _(pool):
                nc.gpsimd.memset(ident[:, :], 0.0).then_inc(id_zero, 1)
                pool.wait_ge(id_zero, 1)
                nc.gpsimd.affine_select(out=ident[:, :], in_=ident[:, :], compare_op=ALU.not_equal, fill=1.0,
                                        base=0, pattern=[[-1, P]], channel_multiplier=1).then_inc(id_set, 1)
                pool.wait_ge(id_set, 1)
        chip.phase = "attn_"
        attention(nc, chip, X, ident, t["L0_attn_x"], t["L0_attn_qkv_w"], t["L0_attn_qkv_b"],
                  t["L0_attn_proj_w"], t["L0_attn_proj_b"])
        routed = Routed(chip, ctx, E, H)
        tables = Tables(chip, ctx, t)
        chip.phase = "prep_"
        choose_experts(nc, chip, X, ident, chosen, tables, t)
        chip.phase = "mix_"
        mixers(nc, chip, X, ident, chosen, sorted_rows, tile_expert, tile_row, second_less_first, tables, routed, t)
        chip.phase = "moe_"
        routed_experts(nc, chip, id_set, X, ident, sorted_rows, second_less_first, tile_expert, tile_row, routed, t["L1_ffn_b2"], out, NT)


_OUT = ((32, 256, 128), "float32")


def kernel(**inputs):
    import numpy as _np
    import concourse.bacc as _bacc
    from concourse import mybir as _mybir
    from concourse.bass_utils import run_bass_kernel_spmd as _run

    nc = _bacc.Bacc("TRN2", target_bir_lowering=False, num_devices=1)
    arrays, args = {}, {}
    for name in sorted(inputs):
        a = _np.ascontiguousarray(inputs[name])
        arrays[f"in_{name}"] = a
        args[name] = nc.dram_tensor(f"in_{name}", a.shape, _mybir.dt.from_np(a.dtype), kind="ExternalInput").ap()
    out = nc.dram_tensor("out_0", _OUT[0], _mybir.dt.from_np(_np.dtype(_OUT[1])), kind="ExternalOutput").ap()
    network(nc, args, out)
    r = _run(nc, [arrays], core_ids=[0])
    return r.results[0]["out_0"]
```
